# Optimizing a Trainium2 kernel written in Bass

```python
import numpy as np
import jax
import jax.numpy as jnp

def _softmax(x, axis=-1):
    return jax.nn.softmax(x, axis=axis)

def _gelu(x):
    return jax.nn.gelu(x, approximate=True)

def _silu(x):
    return jax.nn.silu(x)

def _sigmoid(x):
    return jax.nn.sigmoid(x)

def _layernorm(x, axis=-1, eps=1e-05):
    m = jnp.mean(x, axis=axis, keepdims=True)
    v = jnp.var(x, axis=axis, keepdims=True)
    return (x - m) / jnp.sqrt(v + eps)

def _scatter_add(tgt, idx, src, axis=0):
    return tgt.at[idx].add(src)

def _segment_sum(src, seg, n):
    return jax.ops.segment_sum(src, seg, n)
kernel_name = 'mk_gnn_resnorm_d4_gnn_r32_810305'

def setup_inputs(seed: int=0):
    np.random.seed(seed)
    _w = jnp.asarray

    def _rec_inputs():
        import jax
        import jax.numpy as jnp
        _gk = jax.random.key(seed)
        x = -0.000202 + 1 * jax.random.normal(jax.random.fold_in(_gk, 1), (3125, 64), jnp.float32)
        src = jax.random.randint(jax.random.fold_in(_gk, 2), (50000,), 0, 3125, jnp.int32)
        dst = jnp.minimum((3125 * jax.random.uniform(jax.random.fold_in(_gk, 3), (50000,)) ** 2.0).astype(jnp.int32), 99999)
        _o = jnp.argsort(dst, stable=True)
        src = src[_o]
        dst = dst[_o]
        edge_attr_64 = -9.77346e-05 + 0.999888 * jax.random.normal(jax.random.fold_in(_gk, 12), (50000, 64), jnp.float32)
        edge_type_8 = jax.random.randint(jax.random.fold_in(_gk, 14), (50000,), 0, 8, jnp.int32)
        edge_weight = jax.random.uniform(jax.random.fold_in(_gk, 15), (50000,), jnp.float32, 0.0, 0.0625)
        return (x, src, dst, edge_attr_64, edge_type_8, edge_weight)
    x, src, dst, edge_attr_64, edge_type_8, edge_weight = _rec_inputs()

    def _L0_gnn_setup():
        import jax, jax.numpy as jnp
        import numpy as np
        N = 3125
        E = 50000
        NEG_SLOPE = 0.01

        def spmm(rows, cols, vals, x):
            msgs = x[cols] * vals[:, None]
            return jax.ops.segment_sum(msgs, rows, num_segments=N)

        def tag_layer(x, rows, cols, vals, W, b, k, activation):
            fstack = [x]
            for _ in range(k):
                fstack.append(spmm(rows, cols, vals, fstack[-1]))
            h = jnp.concatenate(fstack, axis=-1)
            h = h @ W.T + b
            if activation:
                h = jnp.where(h >= 0, h, NEG_SLOPE * h)
            return h
        key = jax.random.key(seed)
        ks = jax.random.split(key, 10)
        feats = [64, 128, 128, 64]
        k_hops = 2
        inp = {'x': jax.random.normal(ks[0], (N, feats[0]), dtype=jnp.float32), 'rows': jax.random.randint(ks[1], (E,), 0, N, dtype=jnp.int32), 'cols': jax.random.randint(ks[2], (E,), 0, N, dtype=jnp.int32), 'vals': jax.random.uniform(ks[3], (E,), dtype=jnp.float32) / 16.0}
        for i, (fin, fout) in enumerate(zip(feats[:-1], feats[1:]), start=1):
            din = fin * (k_hops + 1)
            w = jax.random.normal(ks[3 + i], (fout, din), dtype=jnp.float32) * np.float32(np.sqrt(2.0 / (din + fout)))
            inp[f'W{i}'] = w
            inp[f'b{i}'] = jnp.zeros((fout,), dtype=jnp.float32)
        return inp
    _L0_gnn_all = _L0_gnn_setup()
    _L0_gnn_in = {k: v for k, v in _L0_gnn_all.items() if k in ('W1', 'b1', 'W2', 'b2', 'W3', 'b3')}
    del _L0_gnn_all

    def _L1_gnn_setup():
        import jax, jax.numpy as jnp
        import numpy as np
        N_NODES = 50000
        N_EDGES = 50000
        D = 64
        R = 8

        def _rgcn_layer(x, edge_index, edge_type, W, root, bias):
            src, dst = (edge_index[0], edge_index[1])
            h = jnp.einsum('nd,rdf->rnf', x, W)
            msg = h[edge_type, src]
            agg = jax.ops.segment_sum(msg, dst, num_segments=x.shape[0])
            return agg + x @ root + bias
        key = jax.random.key(seed)
        ks = jax.random.split(key, 9)
        adj = jax.random.randint(ks[0], (2, N_EDGES), 0, N_NODES, dtype=jnp.int32)
        features = jax.random.normal(ks[1], (N_NODES, D), dtype=jnp.float32)
        edge_type = jax.random.randint(ks[2], (N_EDGES,), 0, R, dtype=jnp.int32)
        s = 1.0 / np.sqrt(D)
        W1 = jax.random.normal(ks[3], (R, D, D), dtype=jnp.float32) * s
        root1 = jax.random.normal(ks[4], (D, D), dtype=jnp.float32) * s
        b1 = jnp.zeros((D,), dtype=jnp.float32)
        W2 = jax.random.normal(ks[5], (R, D, D), dtype=jnp.float32) * s
        root2 = jax.random.normal(ks[6], (D, D), dtype=jnp.float32) * s
        b2 = jnp.zeros((D,), dtype=jnp.float32)
        return {'adj': adj, 'features': features, 'edge_type': edge_type, 'W1': W1, 'root1': root1, 'b1': b1, 'W2': W2, 'root2': root2, 'b2': b2}
    _L1_gnn_all = _L1_gnn_setup()
    _L1_gnn_in = {k: v for k, v in _L1_gnn_all.items() if k in ('W1', 'root1', 'b1', 'W2', 'root2', 'b2')}
    del _L1_gnn_all

    def _L2_gnn_setup():
        import jax, jax.numpy as jnp
        import numpy as np
        NUM_NODES = 3125
        NUM_HYPEREDGES = 6250
        NNZ = 37500
        IN_DIM = 64
        HID_DIM = 64
        OUT_DIM = 64

        def _hypergraph_conv(x, node_idx, edge_idx, D_inv, B_inv, W, b):
            xt = x @ W
            e = B_inv[:, None] * jax.ops.segment_sum(xt[node_idx], edge_idx, num_segments=NUM_HYPEREDGES)
            out = D_inv[:, None] * jax.ops.segment_sum(e[edge_idx], node_idx, num_segments=NUM_NODES)
            return out + b
        key = jax.random.key(seed)
        k1, k2, k3, k4, k5, k6, k7, k8 = jax.random.split(key, 8)
        x = jax.random.normal(k1, (NUM_NODES, IN_DIM), dtype=jnp.float32)
        node_idx = jax.random.randint(k2, (NNZ,), 0, NUM_NODES, dtype=jnp.int64)
        edge_idx = jax.random.randint(k3, (NNZ,), 0, NUM_HYPEREDGES, dtype=jnp.int64)
        hyperedge_index = jnp.stack([node_idx, edge_idx], axis=0)
        s1 = 1.0 / np.sqrt(IN_DIM)
        s2 = 1.0 / np.sqrt(HID_DIM)
        W1 = jax.random.uniform(k4, (IN_DIM, HID_DIM), jnp.float32, -s1, s1)
        b1 = jax.random.uniform(k5, (HID_DIM,), jnp.float32, -s1, s1)
        W2 = jax.random.uniform(k6, (HID_DIM, OUT_DIM), jnp.float32, -s2, s2)
        b2 = jax.random.uniform(k7, (OUT_DIM,), jnp.float32, -s2, s2)
        return {'x': x, 'hyperedge_index': hyperedge_index, 'W1': W1, 'b1': b1, 'W2': W2, 'b2': b2}
    _L2_gnn_all = _L2_gnn_setup()
    _L2_gnn_in = {k: v for k, v in _L2_gnn_all.items() if k in ('W1', 'b1', 'W2', 'b2')}
    del _L2_gnn_all

    def _L3_gnn_setup():
        import jax, jax.numpy as jnp
        import numpy as np
        N_NODES = 50000
        N_EDGES = 25000
        HID = 64

        def _mpnn_layer(h, efeat, src, dst, W_msg, b_msg, W_app, b_app, residual=True):
            h_src = h[src]
            m = jax.nn.relu(jnp.concatenate([h_src, efeat], axis=-1) @ W_msg + b_msg)
            agg = jax.ops.segment_sum(m, dst, num_segments=h.shape[0])
            h_new = jax.nn.relu(jnp.concatenate([h, agg], axis=-1) @ W_app + b_app)
            if residual:
                h_new = h_new + h
            return h_new
        key = jax.random.key(seed)
        ks = jax.random.split(key, 14)
        s = 1.0 / np.sqrt(2 * HID)
        inp = {'feat': jax.random.normal(ks[0], (N_NODES, HID), jnp.float32), 'efeat': jax.random.normal(ks[1], (N_EDGES, HID), jnp.float32), 'src': jax.random.randint(ks[2], (N_EDGES,), 0, N_NODES, jnp.int32), 'dst': jax.random.randint(ks[3], (N_EDGES,), 0, N_NODES, jnp.int32), 'W1_msg': jax.random.uniform(ks[4], (2 * HID, HID), jnp.float32, -s, s), 'b1_msg': jnp.zeros((HID,), jnp.float32), 'W1_app': jax.random.uniform(ks[5], (2 * HID, HID), jnp.float32, -s, s), 'b1_app': jnp.zeros((HID,), jnp.float32), 'W2_msg': jax.random.uniform(ks[6], (2 * HID, HID), jnp.float32, -s, s), 'b2_msg': jnp.zeros((HID,), jnp.float32), 'W2_app': jax.random.uniform(ks[7], (2 * HID, HID), jnp.float32, -s, s), 'b2_app': jnp.zeros((HID,), jnp.float32)}
        return inp
    _L3_gnn_all = _L3_gnn_setup()
    _L3_gnn_in = {k: v for k, v in _L3_gnn_all.items() if k in ('W1_msg', 'b1_msg', 'W1_app', 'b1_app', 'W2_msg', 'b2_msg', 'W2_app', 'b2_app')}
    del _L3_gnn_all
    return {'x': x, 'src': src, 'dst': dst, 'edge_attr_64': edge_attr_64, 'edge_type_8': edge_type_8, 'edge_weight': edge_weight, 'L0_gnn_W1': _L0_gnn_in['W1'], 'L0_gnn_b1': _L0_gnn_in['b1'], 'L0_gnn_W2': _L0_gnn_in['W2'], 'L0_gnn_b2': _L0_gnn_in['b2'], 'L0_gnn_W3': _L0_gnn_in['W3'], 'L0_gnn_b3': _L0_gnn_in['b3'], 'L1_gnn_W1': _L1_gnn_in['W1'], 'L1_gnn_root1': _L1_gnn_in['root1'], 'L1_gnn_b1': _L1_gnn_in['b1'], 'L1_gnn_W2': _L1_gnn_in['W2'], 'L1_gnn_root2': _L1_gnn_in['root2'], 'L1_gnn_b2': _L1_gnn_in['b2'], 'L2_gnn_W1': _L2_gnn_in['W1'], 'L2_gnn_b1': _L2_gnn_in['b1'], 'L2_gnn_W2': _L2_gnn_in['W2'], 'L2_gnn_b2': _L2_gnn_in['b2'], 'L3_gnn_W1_msg': _L3_gnn_in['W1_msg'], 'L3_gnn_b1_msg': _L3_gnn_in['b1_msg'], 'L3_gnn_W1_app': _L3_gnn_in['W1_app'], 'L3_gnn_b1_app': _L3_gnn_in['b1_app'], 'L3_gnn_W2_msg': _L3_gnn_in['W2_msg'], 'L3_gnn_b2_msg': _L3_gnn_in['b2_msg'], 'L3_gnn_W2_app': _L3_gnn_in['W2_app'], 'L3_gnn_b2_app': _L3_gnn_in['b2_app']}

def reference(x, src, dst, edge_attr_64, edge_type_8, edge_weight, L0_gnn_W1, L0_gnn_b1, L0_gnn_W2, L0_gnn_b2, L0_gnn_W3, L0_gnn_b3, L1_gnn_W1, L1_gnn_root1, L1_gnn_b1, L1_gnn_W2, L1_gnn_root2, L1_gnn_b2, L2_gnn_W1, L2_gnn_b1, L2_gnn_W2, L2_gnn_b2, L3_gnn_W1_msg, L3_gnn_b1_msg, L3_gnn_W1_app, L3_gnn_b1_app, L3_gnn_W2_msg, L3_gnn_b2_msg, L3_gnn_W2_app, L3_gnn_b2_app):
    import jax
    import jax.numpy as jnp

    def _L0_gnn_ref(x, rows, cols, vals, W1, b1, W2, b2, W3, b3):
        import jax, jax.numpy as jnp
        import numpy as np
        N = 3125
        E = 50000
        NEG_SLOPE = 0.01

        def spmm(rows, cols, vals, x):
            msgs = x[cols] * vals[:, None]
            return jax.ops.segment_sum(msgs, rows, num_segments=N)

        def tag_layer(x, rows, cols, vals, W, b, k, activation):
            fstack = [x]
            for _ in range(k):
                fstack.append(spmm(rows, cols, vals, fstack[-1]))
            h = jnp.concatenate(fstack, axis=-1)
            h = h @ W.T + b
            if activation:
                h = jnp.where(h >= 0, h, NEG_SLOPE * h)
            return h
        k = 2
        h = tag_layer(x, rows, cols, vals, W1, b1, k, activation=True)
        h = tag_layer(h, rows, cols, vals, W2, b2, k, activation=True)
        h = tag_layer(h, rows, cols, vals, W3, b3, k, activation=False)
        return h

    def _L1_gnn_ref(adj, features, edge_type, W1, root1, b1, W2, root2, b2):
        import jax, jax.numpy as jnp
        import numpy as np
        N_NODES = 50000
        N_EDGES = 50000
        D = 64
        R = 8

        def _rgcn_layer(x, edge_index, edge_type, W, root, bias):
            src, dst = (edge_index[0], edge_index[1])
            h = jnp.einsum('nd,rdf->rnf', x, W)
            msg = h[edge_type, src]
            agg = jax.ops.segment_sum(msg, dst, num_segments=x.shape[0])
            return agg + x @ root + bias
        x = _rgcn_layer(features, adj, edge_type, W1, root1, b1)
        x = jax.nn.relu(x)
        x = _rgcn_layer(x, adj, edge_type, W2, root2, b2)
        return x

    def _L2_gnn_ref(x, hyperedge_index, W1, b1, W2, b2):
        import jax, jax.numpy as jnp
        import numpy as np
        NUM_NODES = 3125
        NUM_HYPEREDGES = 6250
        NNZ = 37500
        IN_DIM = 64
        HID_DIM = 64
        OUT_DIM = 64

        def _hypergraph_conv(x, node_idx, edge_idx, D_inv, B_inv, W, b):
            xt = x @ W
            e = B_inv[:, None] * jax.ops.segment_sum(xt[node_idx], edge_idx, num_segments=NUM_HYPEREDGES)
            out = D_inv[:, None] * jax.ops.segment_sum(e[edge_idx], node_idx, num_segments=NUM_NODES)
            return out + b
        node_idx = hyperedge_index[0]
        edge_idx = hyperedge_index[1]
        ones = jnp.ones((node_idx.shape[0],), dtype=x.dtype)
        D = jax.ops.segment_sum(ones, node_idx, num_segments=NUM_NODES)
        B = jax.ops.segment_sum(ones, edge_idx, num_segments=NUM_HYPEREDGES)
        D_inv = jnp.where(D > 0, 1.0 / D, 0.0)
        B_inv = jnp.where(B > 0, 1.0 / B, 0.0)
        h = jax.nn.relu(_hypergraph_conv(x, node_idx, edge_idx, D_inv, B_inv, W1, b1))
        y = _hypergraph_conv(h, node_idx, edge_idx, D_inv, B_inv, W2, b2)
        return y

    def _L3_gnn_ref(feat, efeat, src, dst, W1_msg, b1_msg, W1_app, b1_app, W2_msg, b2_msg, W2_app, b2_app):
        import jax, jax.numpy as jnp
        import numpy as np
        N_NODES = 50000
        N_EDGES = 25000
        HID = 64

        def _mpnn_layer(h, efeat, src, dst, W_msg, b_msg, W_app, b_app, residual=True):
            h_src = h[src]
            m = jax.nn.relu(jnp.concatenate([h_src, efeat], axis=-1) @ W_msg + b_msg)
            agg = jax.ops.segment_sum(m, dst, num_segments=h.shape[0])
            h_new = jax.nn.relu(jnp.concatenate([h, agg], axis=-1) @ W_app + b_app)
            if residual:
                h_new = h_new + h
            return h_new
        h1 = _mpnn_layer(feat, efeat, src, dst, W1_msg, b1_msg, W1_app, b1_app)
        h2 = _mpnn_layer(h1, efeat, src, dst, W2_msg, b2_msg, W2_app, b2_app)
        return h2
    edge_index = jnp.stack([src, dst])
    x = _layernorm(x + _L0_gnn_ref(x, src, dst, edge_weight, L0_gnn_W1, L0_gnn_b1, L0_gnn_W2, L0_gnn_b2, L0_gnn_W3, L0_gnn_b3), axis=-1)
    x = _layernorm(x + _L1_gnn_ref(edge_index, x, edge_type_8, L1_gnn_W1, L1_gnn_root1, L1_gnn_b1, L1_gnn_W2, L1_gnn_root2, L1_gnn_b2), axis=-1)
    x = _layernorm(x + _L2_gnn_ref(x, edge_index, L2_gnn_W1, L2_gnn_b1, L2_gnn_W2, L2_gnn_b2), axis=-1)
    x = _layernorm(x + _L3_gnn_ref(x, edge_attr_64, src, dst, L3_gnn_W1_msg, L3_gnn_b1_msg, L3_gnn_W1_app, L3_gnn_b1_app, L3_gnn_W2_msg, L3_gnn_b2_msg, L3_gnn_W2_app, L3_gnn_b2_app), axis=-1)
    return x

_drawn_inputs = setup_inputs


def setup_inputs(seed=0):
    import zlib

    import numpy as np

    out = dict(_drawn_inputs(seed))
    spreads = {'L0_gnn_b1': (0.0, 0.1),
     'L0_gnn_b2': (0.0, 0.1),
     'L0_gnn_b3': (0.0, 0.1),
     'L1_gnn_b1': (0.0, 0.373),
     'L1_gnn_b2': (0.0, 0.766),
     'L3_gnn_b1_msg': (0.0, 0.1),
     'L3_gnn_b1_app': (0.0, 0.1),
     'L3_gnn_b2_msg': (0.0, 0.1),
     'L3_gnn_b2_app': (0.0, 0.317)}
    factors = {'edge_weight': 3.706}
    for name, (base, spread) in spreads.items():
        noise = np.random.default_rng([zlib.crc32(name.encode()), seed]).standard_normal(out[name].shape)
        drawn = base * np.exp(spread * noise) if base else spread * noise
        out[name] = jnp.asarray(drawn.astype(out[name].dtype))
    for name, factor in factors.items():
        out[name] = (out[name] * factor).astype(out[name].dtype)
    return out
```

```python
from contextlib import ExitStack

import concourse.bass as bass
from concourse import mybir

FP32 = mybir.dt.float32
BF16 = mybir.dt.bfloat16
I32 = mybir.dt.int32
ALU = mybir.AluOpType
ACT = mybir.ActivationFunctionType
AX = mybir.AxisListType

P = 128
NODES = 3125
EDGES = 50000
F = 64
HID = 128
TYPES = 8
LN_EPS = 1e-5
SLOPE = 0.01

NB = -(-NODES // P)
FULLB = NODES // P
LASTN = NODES - FULLB * P
ROWS = NB * P
COLS = EDGES // P
TAIL = EDGES - COLS * P
EC = COLS + 1
SENT = NB * P
GRP = 8
RING = 4
TILES = -(-((EDGES + NB * (P - 1)) // P + 1) // (GRP * RING)) * GRP * RING
ITERS = TILES // (GRP * RING)
GPP = TILES // GRP
SLOTS = TILES * P
META = 3
RMETA = 4
REC = META + F
SCOL = 15
SSTEPS = COLS // (2 * SCOL)
assert SSTEPS * 2 * SCOL == COLS
MCH = 8
MT = TILES // MCH
BANK = 512
NG = 5
GB = NB // NG
assert NG * GB == NB

PASSES = (
    [dict(d=F, w=True, rev=True)] * 2 + [dict(d=HID, w=True, rev=True)] * 2 + [dict(d=F, w=True, rev=True)] * 2
    + [dict(d=F, typed=True)] * 2
    + [dict(d=F, count=True), dict(d=F, count=True, rev=True), dict(d=F), dict(d=F, rev=True)]
    + [dict(d=F, attr=True)] * 2
)
NPASS = len(PASSES)

PROJ = {
    "tag1": dict(k=[HID, F], d=HID, d2=0),
    "tag2": dict(k=[HID, HID, HID], d=HID, d2=0),
    "tag3": dict(k=[HID], d=3 * F, d2=0),
    "rgcn1": dict(k=[F], d=TYPES * F, d2=F),
    "rgcn2": dict(k=[F], d=TYPES * F, d2=F),
    "hyper1": dict(k=[F], d=F, d2=0),
    "hyper2": dict(k=[F], d=F, d2=0),
    "mpnn1": dict(k=[F], d=F, d2=F),
    "app1": dict(k=[F], d=F, d2=0),
    "mpnn2": dict(k=[F], d=F, d2=F),
    "app2": dict(k=[F], d=F, d2=0),
}
_tr = 0
for _i, _p in enumerate(PROJ.values()):
    _p["index"] = _i
    _p["tr0"] = _tr
    _tr += NG * len(_p["k"])


def gnn_kernel(nc, a, out):
    ctx = ExitStack()
    with ctx:
        def sb(name, shape, dt=FP32):
            return ctx.enter_context(nc.sbuf_tensor(name, shape, dt))

        def sem(name):
            return ctx.enter_context(nc.semaphore(name))

        def dram(name, shape, dt=FP32):
            return nc.dram_tensor(name, shape, dt, kind="Internal").ap()

        records = dram("records", (SLOTS, REC))
        records_rev = dram("records_rev", (SLOTS, RMETA))
        tables = [dram(f"table{n}", (ROWS * (TYPES if q.get("typed") else 1), q["d"]))
                  for n, q in enumerate(PASSES)]

        iota_i = sb("iota_i", [P, P], I32)
        iota_f = sb("iota_f", [P, P])
        part_i = sb("part_i", [P, 1], I32)
        part_f = sb("part_f", [P, 1])
        ident = sb("ident", [P, P])
        below = sb("below", [P, P])
        ones = sb("ones", [P, P])
        zeros = sb("zeros", [P, BANK], BF16)
        tile0_i = sb("tile0_i", [1, TILES], I32)
        tile0_f = sb("tile0_f", [1, TILES])

        src_i = sb("src_i", [P, EC], I32)
        dst_i = sb("dst_i", [P, EC], I32)
        typ_i = sb("typ_i", [P, EC], I32)
        ew = sb("ew", [P, EC])
        slot_i = [sb(f"slot_i{k}", [P, EC], I32) for k in range(2)]
        sel_ring = sb("sel_ring", [P, RING, GRP, P])
        msg_ring = sb("msg_ring", [P, RING, GRP * HID])
        work = sel_ring[:, :, :, :].rearrange("p s g c -> p (s g c)")[:, 0:10 * EC].rearrange("p (n c) -> p n c", n=10)
        blk_f = [work[:, k, :] for k in (0, 1)]
        loc_f = [work[:, k, :] for k in (2, 3)]
        row_f = [work[:, k, :] for k in (4, 5)]
        typed_f = work[:, 6, :]
        blk_i, low_i, tmp_a = (work[:, k, :].bitcast(I32) for k in (7, 8, 9))
        rec_ring = msg_ring[:, :, :].rearrange("p s c -> p (s c)")[:, 0:2 * SCOL * REC]\
            .rearrange("p (h c r) -> p h c r", h=2, c=SCOL)
        recr_ring = sb("recr_ring", [P, 2, SCOL, RMETA])
        slot_ring = sb("slot_ring", [P, 2, SCOL], I32)
        tot = sb("tot", [P, NB + 1])
        base = sb("base", [P, NB + 1])
        padded_i = sb("padded_i", [P, NB + 1], I32)
        padded_f = sb("padded_f", [P, NB + 1])
        start = [sb(f"start{k}", [P, NB + 1]) for k in range(2)]
        tblk = sb("tblk", [1, TILES])
        blk64 = [sb(f"blk64_{k}", [1, TILES], I32) for k in range(2)]
        blk128 = sb("blk128", [1, TILES], I32)

        row_src = sb("row_src", [P, TILES], I32)
        row_typed = sb("row_typed", [P, TILES], I32)
        row_dst = sb("row_dst", [P, TILES], I32)
        loc_dst = sb("loc_dst", [P, TILES])
        loc_src = sb("loc_src", [P, TILES])
        weight = sb("weight", [P, TILES])

        idx_ring = sb("idx_ring", [P, RING, GRP], I32)
        area = sb("area", [P, 16900])
        eq = area[:, 0:(NB + 1) * EC // 2 + 1].bitcast(BF16)[:, 0:(NB + 1) * EC]\
            .rearrange("p (b c) -> p b c", b=NB + 1)
        o = 5200
        cum = area[:, o:o + (NB + 1) * EC].rearrange("p (b c) -> p b c", b=NB + 1)
        chunk = [area[:, k * MT * REC:(k + 1) * MT * REC].rearrange("p (t r) -> p t r", r=REC)
                 for k in range(2)]
        rev_meta = area[:, 8000:8000 + TILES * RMETA].rearrange("p (t r) -> p t r", r=RMETA)
        wide = area[:, 0:NB * TYPES * F].rearrange("p (b d) -> p b d", b=NB)
        attr_ring = area[:, 12800:12800 + RING * GRP * F].rearrange("p (s g f) -> p s g f", s=RING, g=GRP)
        relu_ring = area[:, 14848:14848 + RING * GRP * F].rearrange("p (s g) -> p s g", s=RING)
        attrT = area[0:F, 0:GRP * P]

        def nodes(name, d):
            return sb(name, [P, NB, d])

        x = nodes("x", F)
        xf = nodes("xf", HID)
        agg = nodes("agg", HID)
        h1 = area[:, 0:NB * HID].rearrange("p (b d) -> p b d", b=NB)
        hop = area[:, NB * HID:2 * NB * HID].rearrange("p (b d) -> p b d", b=NB)
        part = area[:, 2 * NB * HID:3 * NB * HID].rearrange("p (b d) -> p b d", b=NB)
        t64 = nodes("t64", F)
        r64 = nodes("r64", F)
        h64 = nodes("h64", F)
        xT = sb("xT", [P, 3, GB * P])
        mean = sb("mean", [P, NB])
        var = sb("var", [P, NB])
        std = sb("std", [P, NB])
        rstd = sb("rstd", [P, NB])
        cnt = sb("cnt", [P, NB])
        has = sb("has", [P, NB])
        inv = [sb(f"inv{k}", [P, NB]) for k in range(2)]

        w_tag1a = sb("w_tag1a", [HID, HID])
        w_tag1b = sb("w_tag1b", [F, HID])
        w_tag2 = sb("w_tag2", [HID, 3, HID])
        w_tag3 = sb("w_tag3", [HID, 3, F])
        w_rel = [sb(f"w_rel{k}", [F, TYPES, F]) for k in range(2)]
        w_root = [sb(f"w_root{k}", [F, F]) for k in range(2)]
        w_hyp = [sb(f"w_hyp{k}", [F, F]) for k in range(2)]
        w_msgh = [sb(f"w_msgh{k}", [F, F]) for k in range(2)]
        w_msge = [sb(f"w_msge{k}", [F, F]) for k in range(2)]
        w_apph = [sb(f"w_apph{k}", [F, F]) for k in range(2)]
        w_appa = [sb(f"w_appa{k}", [F, F]) for k in range(2)]
        b_tag1 = sb("b_tag1", [1, HID])
        b_tag2 = sb("b_tag2", [1, HID])
        b_tag3 = sb("b_tag3", [1, 3 * F])
        b_root = [sb(f"b_root{k}", [1, F]) for k in range(2)]
        b_msg = [sb(f"b_msg{k}", [1, F]) for k in range(2)]
        b_app = [sb(f"b_app{k}", [1, F]) for k in range(2)]
        b_hyp = [sb(f"b_hyp{k}", [P, F]) for k in range(2)]

        ps = ctx.enter_context(nc.psum_tensor("ps", [P, 8 * BANK], FP32))
        CNT0 = 4 * BANK
        TR0 = 5 * BANK
        SECOND0 = 7 * BANK
        ATT0 = 4 * BANK
        MSG0 = 6 * BANK

        edges_in = sem("edges_in")
        x_in = sem("x_in")
        weights_in = sem("weights_in")
        pool_steps = sem("pool_steps")
        pe_steps = sem("pe_steps")
        iota_made = sem("iota_made")
        consts_made = sem("consts_made")
        fill_made = sem("fill_made")
        filled = sem("filled")
        dve_step = sem("dve_step")
        totals_made = sem("totals_made")
        totals_summed = sem("totals_summed")
        ranked = sem("ranked")
        rec_made = sem("rec_made")
        attr_in = [sem(f"attr_in{k}") for k in range(2)]
        scattered = [sem(f"scattered{k}") for k in range(2)]
        chunk_in = [sem(f"chunk_in{k}") for k in range(2)]
        chunk_used = sem("chunk_used")
        rev_in = sem("rev_in")
        blocks_made = sem("blocks_made")
        table_stored = sem("table_stored")
        table_made = sem("table_made")
        acc_zeroed = sem("acc_zeroed")
        idx_ready = sem("idx_ready")
        gathered = [sem(f"gathered{k}") for k in range(RING)]
        sel_ready = sem("sel_ready")
        summed = sem("summed")
        acc_done = sem("acc_done")
        acc_saved = sem("acc_saved")
        acc_copied = sem("acc_copied")
        att_loaded = [sem(f"att_loaded{k}") for k in range(RING)]
        att_turned = sem("att_turned")
        att_ready = sem("att_ready")
        att_projected = sem("att_projected")
        att_added = sem("att_added")
        att_relu = sem("att_relu")
        proj_in = sem("proj_in")
        turned = sem("turned")
        turned_sb = sem("turned_sb")
        product = sem("product")
        product_out = sem("product_out")
        var_made = sem("var_made")
        std_made = sem("std_made")
        out_stored = sem("out_stored")

        def index_of(q):
            return row_dst if q.get("rev") else row_typed if q.get("typed") else row_src

        def table_attr(tile):
            return records.rearrange("(p t) r -> p t r", p=P)[:, bass.ds(tile, GRP), META:REC]

        FILLED = 16 * 2 * -(-TILES // (2 * SCOL))
        N_EDGE_LOADS, N_WEIGHTS = 8, 32
        block = ctx.enter_context(nc.Block())

        @block.sync
        def _(sp):
            sp.wait_ge(fill_made, 4)
            for t, main, tail in ((dst_i, a["dst_cols"], a["dst_tail"]), (src_i, a["src_cols"], a["src_tail"]),
                                  (typ_i, a["typ_cols"], a["typ_tail"]), (ew, a["w_cols"], a["w_tail"])):
                sp.dma_start(t[:, 0:COLS], main).then_inc(edges_in, 16)
                sp.dma_start(t[0:TAIL, COLS:EC], tail).then_inc(edges_in, 16)
            sp.wait_ge(fill_made, 7)
            table = records.rearrange("(p t) r -> p t r", p=P)
            for c in range(0, TILES, 2 * SCOL):
                n = min(2 * SCOL, TILES - c)
                sp.dma_start(table[:, c:c + n, :],
                             rec_ring[:, :, :, :].rearrange("p h c r -> p (h c) r")[:, 0:n, :]).then_inc(filled, 16)
            table = records_rev.rearrange("(p t) r -> p t r", p=P)
            for c in range(0, TILES, 2 * SCOL):
                n = min(2 * SCOL, TILES - c)
                sp.dma_start(table[:, c:c + n, :],
                             recr_ring[:, :, :, :].rearrange("p h c r -> p (h c) r")[:, 0:n, :]).then_inc(filled, 16)
            sp.dma_start(x[:, 0:FULLB, :], a["x"][0:FULLB * P, :].rearrange("(b p) f -> p b f", p=P)).then_inc(x_in, 16)
            sp.dma_start(x[0:LASTN, FULLB, :], a["x"][FULLB * P:NODES, :]).then_inc(x_in, 16)
            loads = [
                (w_tag1a[:, :], a["L0_W1T"][0:HID, :]), (w_tag1b[:, :], a["L0_W1T"][HID:HID + F, :]),
                (w_tag2[:, :, :], a["L0_W2T"].rearrange("(k p) n -> p k n", p=HID)),
                (w_tag3[:, :, :], a["L0_W3T"].rearrange("(k p) n -> p k n", p=HID)),
                (b_tag1[:, :], a["L0_b1"]), (b_tag2[:, :], a["L0_b2"]), (b_tag3[:, 0:F], a["L0_b3"]),
            ]
            for k in range(2):
                s = str(k + 1)
                loads += [
                    (w_rel[k][:, :, :], a["L1_W" + s].rearrange("r d f -> d r f")),
                    (w_root[k][:, :], a["L1_root" + s]), (b_root[k][:, :], a["L1_b" + s]),
                    (w_hyp[k][:, :], a["L2_W" + s]), (b_hyp[k][:, :], a["L2_b" + s].to_broadcast([P, F])),
                    (w_msgh[k][:, :], a["L3_W" + s + "_msg"][0:F, :]), (w_msge[k][:, :], a["L3_W" + s + "_msg"][F:2 * F, :]),
                    (b_msg[k][:, :], a["L3_b" + s + "_msg"]),
                    (w_apph[k][:, :], a["L3_W" + s + "_app"][0:F, :]), (w_appa[k][:, :], a["L3_W" + s + "_app"][F:2 * F, :]),
                    (b_app[k][:, :], a["L3_b" + s + "_app"]),
                ]
            assert len(loads) == N_WEIGHTS - 3
            for to, of in loads:
                sp.dma_start(to, of).then_inc(weights_in, 16)

            attr = a["edge_attr"][0:COLS * P, :].rearrange("(c p) f -> p c f", p=P)

            def load_attr(i, h, first=False):
                if first:
                    sp.wait_ge(filled, FILLED)
                else:
                    sp.wait_ge(scattered[h], 16 * SCOL * i)
                sp.dma_start(rec_ring[:, h, :, META:REC],
                             attr[:, bass.ds(i * 2 * SCOL + h * SCOL, SCOL), :]).then_inc(attr_in[h], 16)

            for h in range(2):
                load_attr(0, h, first=True)
            with sp.Fori(1, SSTEPS) as i:
                for h in range(2):
                    load_attr(i, h)
            sp.wait_ge(scattered[0], 16 * SCOL * SSTEPS)
            sp.dma_start(rec_ring[0:TAIL, 0, 0, META:REC], a["edge_attr"][COLS * P:EDGES, :]).then_inc(attr_in[0], 16)

            sp.wait_ge(table_made, 1)
            sp.dma_start(tables[0].rearrange("(p b) d -> p (b d)", p=P),
                         x[:, :, :].rearrange("p b d -> p (b d)")).then_inc(table_stored, 16)

            sp.wait_ge(scattered[0], 16 * (SCOL * SSTEPS + 1))
            sp.wait_ge(scattered[1], 16 * SCOL * SSTEPS)
            sp.wait_ge(ranked, 2)
            table = records.rearrange("(p t) r -> p t r", p=P)
            for c in range(MCH):
                if c >= 2:
                    sp.wait_ge(chunk_used, c - 1)
                sp.dma_start(chunk[c % 2], table[:, c * MT:(c + 1) * MT, :]).then_inc(chunk_in[c % 2], 16)
            sp.wait_ge(scattered[0], 16 * (2 * SCOL * SSTEPS + 2))
            sp.wait_ge(scattered[1], 16 * 2 * SCOL * SSTEPS)
            sp.dma_start(rev_meta[:, :, :].rearrange("p t r -> p (t r)"),
                         records_rev.rearrange("(p t) r -> p (t r)", p=P)).then_inc(rev_in, 16)

            staged = {2: h1, 3: hop, 6: wide, 7: wide}
            for n in range(NPASS):
                if n:
                    sp.wait_ge(table_made, n + 1)
                    view = staged[n] if n in staged else t64[:, :, :]
                    d = tables[n].rearrange("(p b) d -> p (b d)", p=P)
                    sp.dma_start(d, view.rearrange("p b d -> p (b d)")).then_inc(table_stored, 16)
                if PASSES[n].get("attr"):
                    if n == NPASS - 2:
                        sp.wait_ge(product_out, NG * (PROJ["mpnn1"]["index"] + 1))

                    g0 = GPP * n
                    with sp.Fori(0, ITERS) as i:
                        for s in range(RING):
                            sp.wait_ge(summed, i * RING + (g0 + s + 1))
                            sp.dma_start(attr_ring[:, s, :, :],
                                         table_attr(i * (RING * GRP) + s * GRP)).then_inc(att_loaded[s], 16)
            sp.wait_ge(table_made, NPASS + 1)
            sp.dma_start(out[0:FULLB * P, :].rearrange("(b p) f -> p b f", p=P), x[:, 0:FULLB, :]).then_inc(out_stored, 16)
            sp.dma_start(out[FULLB * P:NODES, :], x[0:LASTN, FULLB, :]).then_inc(out_stored, 16)
            sp.wait_ge(out_stored, 32)

        @block.gpsimd
        def _(pool):
            nc.gpsimd.iota(iota_i[:, :], pattern=[[1, P]], base=0, channel_multiplier=0).then_inc(iota_made, 1)
            nc.gpsimd.iota(part_i[:, :], pattern=[[0, 1]], base=0, channel_multiplier=1).then_inc(iota_made, 1)
            nc.gpsimd.iota(tile0_i[:, :], pattern=[[P, TILES]], base=0, channel_multiplier=0).then_inc(iota_made, 1)

            def put(table, rec, h, j, n=P):
                nc.gpsimd.indirect_dma_start(
                    out=table, out_offset=bass.IndirectOffsetOnAxis(ap=slot_ring[:, h, j:j + 1], axis=0),
                    in_=rec[:, h, j, :], in_offset=None).then_inc(scattered[h], 16)

            pool.wait_ge(filled, FILLED)
            with pool.Fori(0, SSTEPS) as i:
                for h in range(2):
                    pool.wait_ge(rec_made, i * 2 + h + 1)
                    pool.wait_ge(attr_in[h], i * 16 + 16)
                    pool.sem_inc(pool_steps, 1)
                    for j in range(SCOL):
                        put(records, rec_ring, h, j)
            pool.wait_ge(rec_made, 2 * SSTEPS + 1)
            pool.wait_ge(attr_in[0], 16 * (SSTEPS + 1))
            put(records, rec_ring, 0, 0)
            with pool.Fori(0, SSTEPS) as i:
                for h in range(2):
                    pool.wait_ge(rec_made, i * 2 + (2 * SSTEPS + 1 + h + 1))
                    pool.sem_inc(pool_steps, 1)
                    for j in range(SCOL):
                        put(records_rev, recr_ring, h, j)
            pool.wait_ge(rec_made, 4 * SSTEPS + 2)
            put(records_rev, recr_ring, 0, 0)

            for n, q in enumerate(PASSES):
                pool.wait_ge(table_stored, 16 * (n + 1))
                g0 = GPP * n
                with pool.Fori(0, ITERS) as i:
                    for s in range(RING):
                        pool.wait_ge(idx_ready, i * RING + (g0 + s + 1))
                        pool.sem_inc(pool_steps, 1)
                        for j in range(GRP):
                            nc.gpsimd.indirect_dma_start(
                                out=msg_ring[:, s, j * q["d"]:(j + 1) * q["d"]], out_offset=None, in_=tables[n],
                                in_offset=bass.IndirectOffsetOnAxis(ap=idx_ring[:, s, j:j + 1], axis=0),
                            ).then_inc(gathered[s], 16)

        @block.tensor
        def _(pe):
            for k in range(2):
                pe.wait_ge(totals_made, k + 1)
                nc.tensor.matmul(ps[:, 0:NB + 1], below[:, :], tot[:, :], start=True, stop=True)
                nc.tensor.matmul(ps[:, BANK:BANK + NB + 1], ones[:, :], tot[:, :], start=True, stop=True)\
                    .then_inc(totals_summed, 1)
            pe.wait_ge(consts_made, 1)
            pe.wait_ge(weights_in, 16 * (N_WEIGHTS - 3))
            pe.wait_ge(blocks_made, 1)

            def zero_acc(n):
                q = PASSES[n]
                banks = 8 if q.get("count") else -(-NB * q["d"] // BANK)
                for k in range(banks):
                    last = nc.tensor.matmul(ps[:, k * BANK:(k + 1) * BANK], zeros[:, 0:P], zeros[:, :],
                                            start=True, stop=False, skip_group_check=True)
                last.then_inc(acc_zeroed, 1)
                if n == 0:
                    nc.tensor.matmul(ps[:, 0:1], zeros[:, 0:P], zeros[:, 0:1],
                                     start=False, stop=False, skip_group_check=True).then_inc(summed, RING)

            def sum_group(n, i, s):
                q = PASSES[n]
                d = q["d"]
                offsets = (blk128 if d == HID else blk64[1 if q.get("rev") else 0])
                _, at = nc.values_load_multi_w_load_instructions(
                    offsets[0:1, bass.ds(i * (RING * GRP) + s * GRP, GRP)], engines=[mybir.EngineType.PE],
                    min_val=0, max_val=(NB - 1) * d, skip_runtime_bounds_check_because="blocks are 0..24")
                if q.get("attr"):
                    l0 = GPP * (n - (NPASS - 2))
                    pe.wait_ge(att_relu, i * RING + (l0 + s + 1))
                else:
                    pe.wait_ge(gathered[s], i * (16 * GRP) + 16 * GRP * (ITERS * n + 1))
                pe.wait_ge(sel_ready, i * RING + (GPP * n + s + 1))
                for j in range(GRP):
                    rhs = (relu_ring if q.get("attr") else msg_ring)[:, s, j * d:(j + 1) * d]
                    last = nc.tensor.matmul(ps[:, bass.ds(at[j], d)], sel_ring[:, s, j, :], rhs,
                                            start=False, stop=False, skip_group_check=True)
                    if q.get("count"):
                        last = nc.tensor.matmul(ps[:, bass.ds(at[j] + CNT0, 1)], sel_ring[:, s, j, :], ones[:, 0:1],
                                                start=False, stop=False, skip_group_check=True)
                last.then_inc(summed, 1)

            def turn_attr(l, i, s, first=False):
                n = NPASS - 2 + l
                pe.wait_ge(att_loaded[s], i * 16 + 16 * (ITERS * l + 1))
                if not first:
                    pe.wait_ge(att_ready, i * RING + (GPP * l + s))
                pe.sem_inc(pe_steps, 1)
                for j in range(GRP):
                    last = nc.tensor.transpose(ps[0:F, ATT0 + j * P:ATT0 + (j + 1) * P], attr_ring[:, s, j, :], ident[:, :])
                last.then_inc(att_turned, 1)

            def project_attr(l, i, s, first=False):
                pe.wait_ge(att_ready, i * RING + (GPP * l + s + 1))
                if not first:
                    pe.wait_ge(att_added, i * RING + (GPP * l + s))
                m0 = MSG0 + BANK * (s % 2)
                for j in range(GRP):
                    last = nc.tensor.matmul(ps[:, m0 + j * F:m0 + (j + 1) * F], attrT[:, j * P:(j + 1) * P],
                                            w_msge[l][:, :], start=True, stop=True, skip_group_check=True)
                last.then_inc(att_projected, 1)

            def run_pass(n):
                q = PASSES[n]
                if n:
                    pe.wait_ge(acc_saved, n)
                if n == 1:
                    pe.wait_ge(acc_copied, 1)
                zero_acc(n)
                if q.get("attr"):
                    l = n - (NPASS - 2)
                    turn_attr(l, 0, 0, first=(l == 0))
                    project_attr(l, 0, 0, first=(l == 0))

                    def steps(i, last=False):
                        for s in range(RING):
                            more = not (last and s == RING - 1)
                            ni, ns = (i, s + 1) if s + 1 < RING else (i + 1, 0)
                            if more:
                                turn_attr(l, ni, ns)
                            sum_group(n, i, s)
                            if more:
                                project_attr(l, ni, ns)

                    with pe.Fori(0, ITERS - 1) as i:
                        steps(i)
                    steps(ITERS - 1, last=True)
                else:
                    with pe.Fori(0, ITERS) as i:
                        for s in range(RING):
                            sum_group(n, i, s)
                nc.tensor.matmul(ps[:, 0:1], zeros[:, 0:P], zeros[:, 0:1],
                                 start=False, stop=False, skip_group_check=True).then_inc(acc_done, 1)

            def project(name, inputs, weights, bias=None, weights2=None, bias2=None):
                q = PROJ[name]
                d = q["d"]
                pitch = 256 if d == 3 * F else d
                for g in range(NG):
                    m = q["index"] * NG + g
                    for k, (of, kd) in enumerate(zip(inputs, q["k"])):
                        t = q["tr0"] + g * len(q["k"]) + k
                        if g == 0 and k == 0:
                            pe.wait_ge(proj_in, q["index"] + 1)
                        if t:
                            pe.wait_ge(turned_sb, t)
                        for b in range(GB):
                            last = nc.tensor.transpose(ps[0:kd, TR0 + b * P:TR0 + (b + 1) * P],
                                                       of[:, g * GB + b, 0:kd], ident[:, :])
                        last.then_inc(turned, 1)
                    pe.wait_ge(turned_sb, q["tr0"] + (g + 1) * len(q["k"]))
                    if m:
                        pe.wait_ge(product_out, m)
                    for b in range(GB):
                        for c0, w, bi, dd in ((b * pitch, weights, bias, d), (SECOND0 + b * F, weights2, bias2, F)):
                            if w is None:
                                continue
                            for k, (wk, kd) in enumerate(zip(w, q["k"])):
                                last = nc.tensor.matmul(ps[:, c0:c0 + dd], xT[0:kd, k, b * P:(b + 1) * P], wk,
                                                        start=k == 0, stop=k + 1 == len(w) and bi is None,
                                                        skip_group_check=True)
                            if bi is not None:
                                last = nc.tensor.matmul(ps[:, c0:c0 + dd], ones[0:1, :], bi, start=False, stop=True,
                                                        skip_group_check=True)
                    last.then_inc(product, 1)

            def flat(t):
                return t[:, :, :].rearrange("p k n -> p (k n)")

            run_pass(0)
            run_pass(1)
            project("tag1", [xf, agg], [w_tag1a[:, :], w_tag1b[:, :]], b_tag1[:, :])
            pe.wait_ge(product_out, NG * 1)
            run_pass(2)
            run_pass(3)
            project("tag2", [h1, hop, agg], [w_tag2[:, k, :] for k in range(3)], b_tag2[:, :])
            project("tag3", [xf], [flat(w_tag3)], b_tag3[:, :])
            pe.wait_ge(product_out, NG * 3)
            run_pass(4)
            run_pass(5)
            project("rgcn1", [x], [flat(w_rel[0])], None, [w_root[0][:, :]], b_root[0][:, :])
            pe.wait_ge(product_out, NG * 4)
            run_pass(6)
            project("rgcn2", [h64], [flat(w_rel[1])], None, [w_root[1][:, :]], b_root[1][:, :])
            pe.wait_ge(product_out, NG * 5)
            run_pass(7)
            project("hyper1", [x], [w_hyp[0][:, :]])
            pe.wait_ge(product_out, NG * 6)
            run_pass(8)
            run_pass(9)
            project("hyper2", [h64], [w_hyp[1][:, :]])
            pe.wait_ge(product_out, NG * 7)
            run_pass(10)
            run_pass(11)
            project("mpnn1", [x], [w_msgh[0][:, :]], b_msg[0][:, :], [w_apph[0][:, :]], b_app[0][:, :])
            pe.wait_ge(product_out, NG * 8)
            run_pass(12)
            project("app1", [agg], [w_appa[0][:, :]])
            project("mpnn2", [h64], [w_msgh[1][:, :]], b_msg[1][:, :], [w_apph[1][:, :]], b_app[1][:, :])
            pe.wait_ge(product_out, NG * 10)
            run_pass(13)
            project("app2", [agg], [w_appa[1][:, :]])

        @block.scalar
        def _(act):
            def make_records(key, i, h, waited, n=SCOL):
                c = bass.ds(i * (2 * SCOL) + h * SCOL, n)
                if waited is not None:
                    act.wait_ge(scattered[h], waited)
                if key == 0:
                    nc.scalar.copy(rec_ring[:, h, 0:n, 0], row_f[1][:, c])
                    nc.scalar.copy(rec_ring[:, h, 0:n, 1], loc_f[0][:, c])
                    nc.scalar.copy(rec_ring[:, h, 0:n, 2], typed_f[:, c])
                else:
                    nc.scalar.copy(recr_ring[:, h, 0:n, 0], row_f[0][:, c])
                    nc.scalar.copy(recr_ring[:, h, 0:n, 1], loc_f[1][:, c])
                    nc.scalar.copy(recr_ring[:, h, 0:n, 2], ew[:, c])
                nc.scalar.copy(slot_ring[:, h, 0:n], slot_i[key][:, c]).then_inc(rec_made, 1)

            act.wait_ge(ranked, 1)
            act.wait_ge(filled, FILLED)
            for h in range(2):
                make_records(0, 0, h, None)
            with act.Fori(1, SSTEPS) as i:
                for h in range(2):
                    make_records(0, i, h, i * (16 * SCOL))
            make_records(0, SSTEPS, 0, 16 * SCOL * SSTEPS, n=1)
            act.wait_ge(ranked, 2)
            used = [16 * (SCOL * SSTEPS + 1), 16 * SCOL * SSTEPS]
            with act.Fori(0, SSTEPS) as i:
                for h in range(2):
                    make_records(1, i, h, i * (16 * SCOL) + used[h])
            make_records(1, SSTEPS, 0, 16 * (2 * SCOL * SSTEPS + 1), n=1)

            def turn_out(name):
                q = PROJ[name]
                for g in range(NG):
                    for k, kd in enumerate(q["k"]):
                        t = q["tr0"] + g * len(q["k"]) + k
                        m = q["index"] * NG + g
                        act.wait_ge(turned, t + 1)
                        if m:
                            act.wait_ge(product, m)
                        nc.scalar.copy(xT[0:kd, k, :], ps[0:kd, TR0:TR0 + GB * P]).then_inc(turned_sb, 1)

            def make_std(n):
                act.wait_ge(var_made, n)
                nc.scalar.activation(std[:, :], var[:, :], ACT.Sqrt).then_inc(std_made, 1)

            def attr_out(l, i, s, first=False):
                act.wait_ge(att_turned, i * RING + (GPP * l + s + 1))
                if not first:
                    act.wait_ge(att_projected, i * RING + (GPP * l + s))
                nc.scalar.copy(attrT, ps[0:F, ATT0:ATT0 + GRP * P]).then_inc(att_ready, 1)

            def attr_pass(l):
                attr_out(l, 0, 0, first=(l == 0))

                def steps(i, last=False):
                    for s in range(RING):
                        act.wait_ge(att_added, i * RING + (GPP * l + s + 2))
                        nc.scalar.activation(relu_ring[:, s, :], relu_ring[:, s, :], ACT.Relu).then_inc(att_relu, 1)
                        if not (last and s == RING - 1):
                            ni, ns = (i, s + 1) if s + 1 < RING else (i + 1, 0)
                            attr_out(l, ni, ns)

                with act.Fori(0, ITERS - 1) as i:
                    steps(i)
                steps(ITERS - 1, last=True)

            act.wait_ge(acc_saved, 1)
            nc.scalar.copy(xf[:, :, F:HID], ps[:, 0:NB * F].rearrange("p (b d) -> p b d", d=F)).then_inc(acc_copied, 1)
            turn_out("tag1")
            turn_out("tag2")
            turn_out("tag3")
            make_std(1)
            turn_out("rgcn1")
            turn_out("rgcn2")
            make_std(2)
            turn_out("hyper1")
            turn_out("hyper2")
            make_std(3)
            turn_out("mpnn1")
            attr_pass(0)
            turn_out("app1")
            turn_out("mpnn2")
            attr_pass(1)
            turn_out("app2")
            make_std(4)

        @block.vector
        def _(dve):
            done = [0]

            def step(ins):
                ins.then_inc(dve_step, 1)
                done[0] += 1
                dve.wait_ge(dve_step, done[0])

            v = nc.vector
            v.memset(src_i[:, COLS:EC], SENT).then_inc(fill_made, 1)
            v.memset(dst_i[:, COLS:EC], SENT).then_inc(fill_made, 1)
            v.memset(typ_i[:, COLS:EC], 0).then_inc(fill_made, 1)
            v.memset(ew[:, COLS:EC], 0.0).then_inc(fill_made, 1)
            v.memset(x[:, FULLB, :], 0.0).then_inc(fill_made, 1)
            step(v.memset(rec_ring[:, :, :, :], 0.0))
            step(v.memset(recr_ring[:, :, :, :], 0.0))
            v.memset(rec_ring[:, :, :, 1], -1.0).then_inc(fill_made, 1)
            v.memset(recr_ring[:, :, :, 1], -1.0).then_inc(fill_made, 1)
            v.memset(b_tag3[:, F:3 * F], 0.0)
            v.memset(ones[:, :], 1.0)
            v.memset(zeros[:, :], 0.0)
            dve.wait_ge(iota_made, 3)
            step(v.tensor_copy(iota_f[:, :], iota_i[:, :]))
            step(v.tensor_copy(part_f[:, :], part_i[:, :]))
            v.tensor_copy(tile0_f[:, :], tile0_i[:, :])
            v.tensor_scalar(ident[:, :], iota_f[:, :], part_f[:, 0:1], None, ALU.is_equal)
            v.tensor_scalar(below[:, :], iota_f[:, :], part_f[:, 0:1], None, ALU.is_gt).then_inc(consts_made, 1)

            dve.wait_ge(edges_in, 16 * N_EDGE_LOADS)
            for k, key in ((0, dst_i), (1, src_i)):
                v.tensor_scalar(blk_i[:, :], key[:, :], 7, None, ALU.logical_shift_right)
                step(v.tensor_scalar(low_i[:, :], key[:, :], P - 1, None, ALU.bitwise_and))
                v.tensor_copy(blk_f[k][:, :], blk_i[:, :])
                v.scalar_tensor_tensor(row_f[k][:, :], low_i[:, :], float(NB), blk_i[:, :], ALU.mult, ALU.add)
                step(v.tensor_scalar(tmp_a[:, :], blk_i[:, :], float(NB - 1), float(-P), ALU.min, ALU.mult))
                step(v.tensor_tensor(loc_f[k][:, :], key[:, :], tmp_a[:, :], ALU.add))
            step(v.scalar_tensor_tensor(typed_f[:, :], row_f[1][:, :], float(TYPES), typ_i[:, :], ALU.mult, ALU.add))

            for k in range(2):
                with dve.Fori(0, NB + 1) as b:
                    v.tensor_scalar(eq[:, bass.ds(b, 1), :].rearrange("p a c -> p (a c)"), blk_f[k][:, :],
                                    iota_f[:, bass.ds(b, 1)], None, ALU.is_equal).then_inc(dve_step, 1)
                    dve.wait_ge(dve_step, b + (done[0] + 1))
                    row = eq[:, bass.ds(b, 1), :].rearrange("p a c -> p (a c)")
                    v.tensor_tensor_scan(cum[:, bass.ds(b, 1), :].rearrange("p a c -> p (a c)"), row, row, 0.0,
                                         ALU.add, ALU.bypass)
                done[0] += NB + 1
                dve.drain()
                v.tensor_copy(tot[:, :], cum[:, :, EC - 1]).then_inc(totals_made, 1)
                dve.wait_ge(totals_summed, k + 1)
                step(v.tensor_scalar(padded_i[:, :], ps[:, BANK:BANK + NB + 1], float(P - 1), None, ALU.add))
                step(v.tensor_scalar(padded_i[:, :], padded_i[:, :], 7, 7, ALU.logical_shift_right,
                                     ALU.logical_shift_left))
                step(v.tensor_copy(padded_f[:, :], padded_i[:, :]))
                step(v.tensor_tensor_scan(start[k][:, :], padded_f[:, :], padded_f[:, :], 0.0, ALU.add, ALU.bypass))
                step(v.tensor_tensor(start[k][:, :], start[k][:, :], padded_f[:, :], ALU.subtract))
                step(v.scalar_tensor_tensor(base[:, :], ps[:, 0:NB + 1], -1.0, start[k][:, :], ALU.add, ALU.add))
                with dve.Fori(0, NB + 1) as b:
                    c = cum[:, bass.ds(b, 1), :].rearrange("p a c -> p (a c)")
                    v.scalar_tensor_tensor(c, c, base[:, bass.ds(b, 1)],
                                           eq[:, bass.ds(b, 1), :].rearrange("p a c -> p (a c)"),
                                           ALU.add, ALU.mult)
                dve.drain()
                step(v.tensor_reduce(blk_f[k][:, :], cum.rearrange("p b c -> p c b"), AX.X, ALU.add))
                step(v.tensor_copy(slot_i[k][:, :], blk_f[k][:, :]))
                v.tensor_scalar(low_i[:, :], slot_i[k][:, :], P - 1, None, ALU.bitwise_and)
                step(v.tensor_scalar(blk_i[:, :], slot_i[k][:, :], 7, None, ALU.logical_shift_right))
                v.scalar_tensor_tensor(slot_i[k][:, :], low_i[:, :], float(TILES), blk_i[:, :], ALU.mult, ALU.add)\
                    .then_inc(ranked, 1)
                step(v.memset(tblk[:, :], 0.0))
                for b in range(1, NB):
                    step(v.scalar_tensor_tensor(tblk[:, :], tile0_f[:, :], start[k][0:1, b:b + 1], tblk[:, :],
                                                ALU.is_ge, ALU.add))
                step(v.tensor_scalar(blk64[k][:, :], tblk[:, :], float(F), None, ALU.mult))
            v.tensor_scalar(blk128[:, :], tblk[:, :], float(HID), None, ALU.mult).then_inc(blocks_made, 1)

            dve.wait_ge(x_in, 32)
            step(v.tensor_copy(xf[:, :, 0:F], x[:, :, :]))
            v.engine_nop().then_inc(table_made, 1)

            for c in range(MCH):
                dve.wait_ge(chunk_in[c % 2], 16 * (c // 2 + 1))
                t = slice(c * MT, (c + 1) * MT)
                v.tensor_copy(row_src[:, t], chunk[c % 2][:, :, 0])
                v.tensor_copy(loc_dst[:, t], chunk[c % 2][:, :, 1])
                v.tensor_copy(row_typed[:, t], chunk[c % 2][:, :, 2]).then_inc(chunk_used, 1)
            dve.wait_ge(rev_in, 16)
            v.tensor_copy(row_dst[:, :], rev_meta[:, :, 0])
            v.tensor_copy(weight[:, :], rev_meta[:, :, 2])
            step(v.tensor_copy(loc_src[:, :], rev_meta[:, :, 1]))

            def prepare(n, i, s):
                q = PASSES[n]
                g = GPP * n + s
                c0 = i * (RING * GRP) + s * GRP
                dve.wait_ge(summed, i * RING + (g + 1))
                v.tensor_copy(idx_ring[:, s, :], index_of(q)[:, bass.ds(c0, GRP)]).then_inc(idx_ready, 1)
                place = loc_src if q.get("rev") else loc_dst
                for j in range(GRP):
                    c = bass.ds(c0 + j, 1)
                    if q.get("w"):
                        last = v.tensor_scalar(sel_ring[:, s, j, :], iota_f[:, :], place[:, c], weight[:, c],
                                               ALU.is_equal, ALU.mult)
                    else:
                        last = v.tensor_scalar(sel_ring[:, s, j, :], iota_f[:, :], place[:, c], None, ALU.is_equal)
                last.then_inc(sel_ready, 1)

            def run_pass(n):
                if PASSES[n].get("attr"):
                    l = n - (NPASS - 2)
                    prepare(n, 0, 0)
                    prepare(n, 0, 1)

                    def steps(i, last=False):
                        for s in range(RING):
                            if not (last and s >= RING - 2):
                                ni, ns = (i, s + 2) if s + 2 < RING else (i + 1, s + 2 - RING)
                                prepare(n, ni, ns)
                            dve.wait_ge(gathered[s], i * (16 * GRP) + 16 * GRP * (ITERS * n + 1))
                            dve.wait_ge(att_projected, i * RING + (GPP * l + s + 1))
                            m0 = MSG0 + BANK * (s % 2)
                            v.tensor_tensor(relu_ring[:, s, :], ps[:, m0:m0 + GRP * F], msg_ring[:, s, 0:GRP * F],
                                            ALU.add).then_inc(att_added, 1)

                    with dve.Fori(0, ITERS - 1) as i:
                        steps(i)
                    steps(ITERS - 1, last=True)
                else:
                    with dve.Fori(0, ITERS) as i:
                        for s in range(RING):
                            prepare(n, i, s)
                dve.wait_ge(acc_done, n + 1)

            def sums(n):
                d = PASSES[n]["d"]
                return ps[:, 0:NB * d].rearrange("p (b d) -> p b d", d=d)

            def drain_products(name, post):
                q = PROJ[name]
                d = q["d"]
                pitch = 256 if d == 3 * F else d
                for g in range(NG):
                    dve.wait_ge(product, q["index"] * NG + g + 1)
                    b = slice(g * GB, (g + 1) * GB)
                    first = ps[:, 0:GB * pitch].rearrange("p (b d) -> p b d", d=pitch)[:, :, 0:d]
                    second = ps[:, SECOND0:SECOND0 + GB * F].rearrange("p (b d) -> p b d", d=F)
                    post(b, first, second).then_inc(product_out, 1)

            def wide_of(t, n=F):
                return t.unsqueeze(2).to_broadcast([P, NB, n])

            def layernorm(z, n):
                step(v.tensor_reduce(mean[:, :], z, AX.X, ALU.add))
                step(v.tensor_scalar(mean[:, :], mean[:, :], 1.0 / F, None, ALU.mult))
                step(v.tensor_tensor(z, z, wide_of(mean[:, :]), ALU.subtract))
                step(v.tensor_tensor(x[:, :, :], z, z, ALU.mult))
                step(v.tensor_reduce(var[:, :], x[:, :, :], AX.X, ALU.add))
                v.tensor_scalar(var[:, :], var[:, :], 1.0 / F, LN_EPS, ALU.mult, ALU.add).then_inc(var_made, 1)
                dve.wait_ge(std_made, n)
                step(v.reciprocal(rstd[:, :], std[:, :]))
                step(v.tensor_tensor(x[:, :, :], z, wide_of(rstd[:, :]), ALU.mult))

            def signal(s):
                v.engine_nop().then_inc(s, 1)

            def leaky(to):
                def post(b, first, second):
                    step(v.tensor_copy(to[:, b, :], first))
                    return v.scalar_tensor_tensor(to[:, b, :], to[:, b, :], SLOPE, to[:, b, :], ALU.mult, ALU.max)
                return post

            def copy_to(to, to2=None):
                def post(b, first, second):
                    if to2 is not None:
                        v.tensor_copy(to2[:, b, :], second)
                    return v.tensor_copy(to[:, b, :], first)
                return post

            def inverse_degree(k):
                step(v.tensor_copy(cnt[:, :], ps[:, CNT0:CNT0 + NB * F].rearrange("p (b d) -> p b d", d=F)[:, :, 0]))
                v.tensor_scalar(has[:, :], cnt[:, :], 1.0, None, ALU.min)
                step(v.tensor_scalar(inv[k][:, :], cnt[:, :], 1.0, None, ALU.max))
                step(v.reciprocal(inv[k][:, :], inv[k][:, :]))
                step(v.tensor_tensor(inv[k][:, :], inv[k][:, :], has[:, :], ALU.mult))

            v.engine_nop().then_inc(att_added, 1)
            run_pass(0)
            v.tensor_copy(t64[:, :, :], sums(0)).then_inc(acc_saved, 1)
            signal(table_made)
            run_pass(1)
            dve.wait_ge(acc_copied, 1)
            v.tensor_copy(agg[:, :, 0:F], sums(1)).then_inc(acc_saved, 1)
            signal(proj_in)
            drain_products("tag1", leaky(h1))
            signal(table_made)
            run_pass(2)
            v.tensor_copy(hop, sums(2)).then_inc(acc_saved, 1)
            signal(table_made)
            run_pass(3)
            v.tensor_copy(agg[:, :, :], sums(3)).then_inc(acc_saved, 1)
            signal(proj_in)
            drain_products("tag2", leaky(xf))
            signal(proj_in)

            def split(b, first, second):
                v.tensor_copy(part[:, b, :], first[:, :, 0:2 * F])
                return v.tensor_copy(t64[:, b, :], first[:, :, 2 * F:3 * F])

            drain_products("tag3", split)
            signal(table_made)
            run_pass(4)
            v.tensor_tensor(t64[:, :, :], sums(4), part[:, :, F:2 * F], ALU.add).then_inc(acc_saved, 1)
            signal(table_made)
            run_pass(5)
            v.tensor_tensor(h64[:, :, :], sums(5), part[:, :, 0:F], ALU.add).then_inc(acc_saved, 1)
            dve.wait_ge(acc_saved, 6)
            step(v.tensor_tensor(h64[:, :, :], h64[:, :, :], x[:, :, :], ALU.add))
            layernorm(h64[:, :, :], 1)
            signal(proj_in)

            drain_products("rgcn1", copy_to(wide, r64))
            signal(table_made)
            run_pass(6)
            v.tensor_tensor(h64[:, :, :], sums(6), r64[:, :, :], ALU.add).then_inc(acc_saved, 1)
            dve.wait_ge(acc_saved, 7)
            step(v.tensor_scalar(h64[:, :, :], h64[:, :, :], 0.0, None, ALU.max))
            signal(proj_in)
            drain_products("rgcn2", copy_to(wide, r64))
            signal(table_made)
            run_pass(7)
            v.tensor_tensor(h64[:, :, :], sums(7), r64[:, :, :], ALU.add).then_inc(acc_saved, 1)
            dve.wait_ge(acc_saved, 8)
            step(v.tensor_tensor(h64[:, :, :], h64[:, :, :], x[:, :, :], ALU.add))
            layernorm(h64[:, :, :], 2)
            signal(proj_in)

            drain_products("hyper1", copy_to(t64))
            signal(table_made)
            for k in range(2):
                n = 8 + 2 * k
                run_pass(n)
                if k == 0:
                    inverse_degree(0)
                v.tensor_tensor(t64[:, :, :], sums(n), wide_of(inv[0][:, :]), ALU.mult).then_inc(acc_saved, 1)
                signal(table_made)
                run_pass(n + 1)
                if k == 0:
                    inverse_degree(1)
                v.tensor_tensor(h64[:, :, :], sums(n + 1), wide_of(inv[1][:, :]), ALU.mult).then_inc(acc_saved, 1)
                dve.wait_ge(acc_saved, n + 2)
                bias = b_hyp[k][:, :].unsqueeze(1).to_broadcast([P, NB, F])
                step(v.tensor_tensor(h64[:, :, :], h64[:, :, :], bias, ALU.add))
                if k == 0:
                    step(v.tensor_scalar(h64[:, :, :], h64[:, :, :], 0.0, None, ALU.max))
                    signal(proj_in)
                    drain_products("hyper2", copy_to(t64))
                    signal(table_made)
            step(v.tensor_tensor(h64[:, :, :], h64[:, :, :], x[:, :, :], ALU.add))
            layernorm(h64[:, :, :], 3)
            signal(proj_in)

            drain_products("mpnn1", copy_to(t64, r64))
            signal(table_made)

            def applied(kept, to):
                def post(b, first, second):
                    step(v.tensor_tensor(r64[:, b, :], first, r64[:, b, :], ALU.add))
                    return v.scalar_tensor_tensor(to[:, b, :], r64[:, b, :], 0.0, kept[:, b, :], ALU.max, ALU.add)
                return post

            run_pass(12)
            v.tensor_copy(agg[:, :, 0:F], sums(12)).then_inc(acc_saved, 1)
            signal(proj_in)
            drain_products("app1", applied(x, h64))
            signal(proj_in)
            drain_products("mpnn2", copy_to(t64, r64))
            signal(table_made)
            run_pass(13)
            v.tensor_copy(agg[:, :, 0:F], sums(13)).then_inc(acc_saved, 1)
            signal(proj_in)
            drain_products("app2", applied(h64, h64))
            dve.wait_ge(product_out, NG * len(PROJ))
            step(v.tensor_tensor(h64[:, :, :], h64[:, :, :], x[:, :, :], ALU.add))
            layernorm(h64[:, :, :], 4)
            signal(table_made)


def kernel(**inputs):
    import numpy as np
    import concourse.bacc as bacc
    from concourse.bass_utils import run_bass_kernel_spmd

    def arr(name):
        return np.ascontiguousarray(inputs[name])

    arrays = {"x": arr("x"), "edge_attr": arr("edge_attr_64")}
    n = COLS * P
    for short, name in (("src", "src"), ("dst", "dst"), ("typ", "edge_type_8"), ("w", "edge_weight")):
        v = arr(name)
        arrays[short + "_cols"] = np.ascontiguousarray(v[:n].reshape(COLS, P).T)
        arrays[short + "_tail"] = np.ascontiguousarray(v[n:].reshape(TAIL, 1))
    for k in (1, 2, 3):
        arrays[f"L0_W{k}T"] = np.ascontiguousarray(arr(f"L0_gnn_W{k}").T)
        arrays[f"L0_b{k}"] = arr(f"L0_gnn_b{k}").reshape(1, -1)
    for k in ("1", "2"):
        arrays["L1_W" + k] = arr("L1_gnn_W" + k)
        arrays["L1_root" + k] = arr("L1_gnn_root" + k)
        arrays["L1_b" + k] = arr("L1_gnn_b" + k).reshape(1, -1)
        arrays["L2_W" + k] = arr("L2_gnn_W" + k)
        arrays["L2_b" + k] = arr("L2_gnn_b" + k).reshape(1, -1)
        for part in ("_msg", "_app"):
            arrays["L3_W" + k + part] = arr("L3_gnn_W" + k + part)
            arrays["L3_b" + k + part] = arr("L3_gnn_b" + k + part).reshape(1, -1)

    nc = bacc.Bacc("TRN2", target_bir_lowering=False, num_devices=1)
    feeds, aps = {}, {}
    for name, v in arrays.items():
        feeds["in_" + name] = v
        aps[name] = nc.dram_tensor("in_" + name, v.shape, mybir.dt.from_np(v.dtype), kind="ExternalInput").ap()
    out = nc.dram_tensor("out_0", (NODES, F), FP32, kind="ExternalOutput").ap()
    gnn_kernel(nc, aps, out)
    r = run_bass_kernel_spmd(nc, [feeds], core_ids=[0])
    return r.results[0]["out_0"]
```

```python
from contextlib import ExitStack

import concourse.bass as bass
from concourse import mybir

FP32 = mybir.dt.float32
BF16 = mybir.dt.bfloat16
I32 = mybir.dt.int32
ALU = mybir.AluOpType
ACT = mybir.ActivationFunctionType
AX = mybir.AxisListType

P = 128
NODES = 3125
EDGES = 50000
F = 64
HID = 128
TYPES = 8
LN_EPS = 1e-5
SLOPE = 0.01

NB = -(-NODES // P)
FULLB = NODES // P
LASTN = NODES - FULLB * P
ROWS = NB * P
COLS = EDGES // P
TAIL = EDGES - COLS * P
EC = COLS + 1
SENT = NB * P
GRP = 8
RING = 4
TILES = -(-((EDGES + NB * (P - 1)) // P + 1) // (GRP * RING)) * GRP * RING
ITERS = TILES // (GRP * RING)
GPP = TILES // GRP
SLOTS = TILES * P
TILES_D = TILES + -(-(SLOTS - EDGES) // P)
META = 4
REC = META + F
SCOL = 15
SSTEPS = COLS // (2 * SCOL)
assert SSTEPS * 2 * SCOL == COLS
DCOL = 16
DSTEPS = TILES // (2 * DCOL)
assert DSTEPS * 2 * DCOL == TILES
MCH = 8
MT = TILES // MCH
PST = 10
PATCHES = -(-(TILES + NB * (NB - 1)) // PST) * PST
PSTEPS = PATCHES // PST
PBANKS = 5
CBANKS = 2
assert PSTEPS <= 2 * GPP and PSTEPS - GPP == GPP - 2
PH = PATCHES // 2
TK = 4
TQ = TILES // TK
BANK = 512
NG = 5
GB = NB // NG
assert NG * GB == NB

PASSES = (
    [dict(dense=True)] * 6 + [dict(typed=True)] * 2
    + [dict(dense=True, turned=True), dict(dense=True)] * 2 + [dict(attr=True)] * 2
)
NPASS = len(PASSES)
GATHERS = [n for n, q in enumerate(PASSES) if not q.get("dense")]
DENSE = [n for n, q in enumerate(PASSES) if q.get("dense")]
ND = 6
CHB = 5
NCH = NB // CHB

PROJ = {
    "tag1": dict(k=[HID, F], d=HID, d2=0),
    "tag2": dict(k=[HID, HID, HID], d=HID, d2=0),
    "tag3": dict(k=[HID], d=3 * F, d2=0),
    "rgcn1": dict(k=[F], d=TYPES * F, d2=F),
    "rgcn2": dict(k=[F], d=TYPES * F, d2=F),
    "hyper1": dict(k=[F], d=HID, d2=0),
    "hyper2": dict(k=[F], d=HID, d2=0),
    "mpnn1": dict(k=[F], d=HID, d2=0),
    "app1": dict(k=[F], d=HID, d2=0),
    "mpnn2": dict(k=[F], d=HID, d2=0),
    "app2": dict(k=[F], d=HID, d2=0),
}
_tr = 0
for _i, _p in enumerate(PROJ.values()):
    _p["index"] = _i
    _p["tr0"] = _tr
    _tr += NG * len(_p["k"])


def gnn_kernel(nc, a, out):
    ctx = ExitStack()
    with ctx:
        def sb(name, shape, dt=FP32):
            return ctx.enter_context(nc.sbuf_tensor(name, shape, dt))

        def sem(name):
            return ctx.enter_context(nc.semaphore(name))

        def dram(name, shape, dt=FP32):
            return nc.dram_tensor(name, shape, dt, kind="Internal").ap()

        records_s = dram("records_s", (SLOTS, REC))
        records_d = dram("records_d", (P * TILES_D, REC))
        adj = dram("adj", ((NB + 1) * P, ROWS))
        adj_n = dram("adj_n", ((NB + 1) * P, ROWS))
        tables = {n: dram(f"table{n}", (ROWS * (TYPES if q.get("typed") else 1), F))
                  for n, q in enumerate(PASSES) if not q.get("dense")}

        iota_i = sb("iota_i", [P, P], I32)
        iota_f = sb("iota_f", [P, P])
        part_i = sb("part_i", [P, 1], I32)
        part_f = sb("part_f", [P, 1])
        ident = sb("ident", [P, P])
        below = sb("below", [P, P])
        ones = sb("ones", [P, P])
        zeros = sb("zeros", [P, BANK], BF16)
        tile0_i = sb("tile0_i", [1, TILES], I32)
        tile0_f = sb("tile0_f", [1, TILES])

        src_i = sb("src_i", [P, EC], I32)
        dst_i = sb("dst_i", [P, EC], I32)
        typ_i = sb("typ_i", [P, EC], I32)
        ew = sb("ew", [P, EC])
        slot_i = [sb("slot_s", [P, EC], I32), sb("slot_d", [P, TILES], I32)]
        sel_ring = sb("sel_ring", [P, RING, GRP, P])
        flat_sel = sel_ring[:, :, :, :].rearrange("p s g c -> p (s g c)")
        work = flat_sel[:, 0:9 * TILES].rearrange("p (n c) -> p n c", n=9)
        blk_f, key_f = work[:, 0, :], work[:, 1, :]
        blk_i, low_i = work[:, 2, :].bitcast(I32), work[:, 3, :].bitcast(I32)
        src_s, dst_s, w_s, typ_s, bsrc_real = (work[:, k, :] for k in range(4, 9))
        blk2_f = work[:, 1, :]
        to_ring = flat_sel[:, 0:PST * P].rearrange("p (j c) -> p j c", j=PST)
        from_ring = flat_sel[:, PST * P:2 * PST * P].rearrange("p (j c) -> p j c", j=PST)
        patch_ring = flat_sel[:, 2 * PST * P:3 * PST * P].rearrange("p (j c) -> p j c", j=PST)
        big = sb("big", [P, NCH * CHB * P])
        msg_ring = big[:, 0:RING * GRP * F].rearrange("p (s c) -> p s c", s=RING)
        rec_ring = big[:, 0:2 * DCOL * REC].rearrange("p (h c r) -> p h c r", h=2, c=DCOL)
        adj_ring = big[:, :].rearrange("p (j c) -> p j c", j=NCH)
        slot_ring = sb("slot_ring", [P, 2, DCOL], I32)
        tot = sb("tot", [P, NB + 1])
        base = sb("base", [P, NB + 1])
        padded_i = sb("padded_i", [P, NB + 1], I32)
        padded_f = sb("padded_f", [P, NB + 1])
        start = sb("start", [P, NB + 1])
        tblk = sb("tblk", [1, TILES])
        blk64 = sb("blk64", [1, TILES], I32)
        first_b = sb("first_b", [TQ, TK])
        last_b = sb("last_b", [TQ, TK])
        tile_b = sb("tile_b", [TQ, TK])
        n_pat = sb("n_pat", [TQ, TK])
        tot_pat = sb("tot_pat", [TQ, TK])
        cum_pat = sb("cum_pat", [TQ, TK])
        pat0 = sb("pat0", [TQ, TK])
        pat1 = sb("pat1", [TQ, TK])
        shift = sb("shift", [TQ, TK])
        place_i = sb("place_i", [1, PATCHES], I32)

        row_src = sb("row_src", [P, TILES], I32)
        row_typed = sb("row_typed", [P, TILES], I32)
        loc_dst = sb("loc_dst", [P, TILES])

        idx_ring = sb("idx_ring", [P, RING, GRP], I32)
        area = sb("area", [P, 16500])
        AEQ = (NB + 1) * TILES // 2
        eq_all = area[:, 0:AEQ].bitcast(BF16)
        cum_all = area[:, AEQ:AEQ + (NB + 1) * TILES]
        chunk = [area[:, k * MT * REC:(k + 1) * MT * REC].rearrange("p (t r) -> p t r", r=REC)
                 for k in range(2)]
        member = area[0:TQ, 0:TK * PATCHES].rearrange("p (k c) -> p k c", k=TK)
        o = TK * PATCHES
        src_t, loc_t, w_t, shift_t, tile_t = (
            area[0:TQ, o + n * TK * P:o + (n + 1) * TK * P].rearrange("p (k c) -> p k c", k=TK) for n in range(5))
        o += 5 * TK * P
        p_w, p_blk, p_id, p_iota, p_trash, p_tmp = (
            area[:, o + n * PATCHES:o + (n + 1) * PATCHES] for n in range(6))
        o = NB * TYPES * F
        p_src, p_loc, p_keep = (area[:, o + n * PATCHES:o + (n + 1) * PATCHES] for n in range(3))
        p_iota_i = p_tmp.bitcast(I32)
        wide = area[:, 0:NB * TYPES * F].rearrange("p (b d) -> p b d", b=NB)
        attr_ring = area[:, 12800:12800 + RING * GRP * F].rearrange("p (s g f) -> p s g f", s=RING, g=GRP)
        relu_ring = area[:, 1024:1024 + RING * GRP * F].rearrange("p (s g) -> p s g", s=RING)
        attrT = area[0:F, 0:GRP * P]

        def nodes(name, d):
            return sb(name, [P, NB, d])

        x = nodes("x", F)
        xf = nodes("xf", HID)
        agg = nodes("agg", HID)
        h1 = area[:, 0:NB * HID].rearrange("p (b d) -> p b d", b=NB)
        hop = area[:, NB * HID:2 * NB * HID].rearrange("p (b d) -> p b d", b=NB)
        part = area[:, 2 * NB * HID:3 * NB * HID].rearrange("p (b d) -> p b d", b=NB)
        t64 = nodes("t64", F)
        r64 = nodes("r64", F)
        h64 = nodes("h64", F)
        flat_agg = agg[:, :, :].rearrange("p b d -> p (b d)")
        cto_ring = flat_agg[:, 0:PST * P].rearrange("p (j c) -> p j c", j=PST)
        cfrom_ring = flat_agg[:, PST * P:2 * PST * P].rearrange("p (j c) -> p j c", j=PST)
        cpatch_ring = xf[:, :, :].rearrange("p b d -> p (b d)")[:, 0:PST * P].rearrange("p (j c) -> p j c", j=PST)
        SUB = [range(0, 3), range(3, CHB)]
        turned_ring = area[:, 0:2 * 3 * P].rearrange("p (u c) -> p u c", u=2)
        xT = sb("xT", [P, 3, GB * P])
        mean = sb("mean", [P, NB])
        var = sb("var", [P, NB])
        std = sb("std", [P, NB])
        rstd = sb("rstd", [P, NB])
        cnt = sb("cnt", [P, NB])
        has = sb("has", [P, NB])
        inv = [sb(f"inv{k}", [P, NB]) for k in range(2)]

        w_tag1a = sb("w_tag1a", [HID, HID])
        w_tag1b = sb("w_tag1b", [F, HID])
        w_tag2 = sb("w_tag2", [HID, 3, HID])
        w_tag3 = sb("w_tag3", [HID, 3, F])
        w_rel = [sb(f"w_rel{k}", [F, TYPES, F]) for k in range(2)]
        w_root = [sb(f"w_root{k}", [F, F]) for k in range(2)]
        w_hyp = [sb(f"w_hyp{k}", [F, HID]) for k in range(2)]
        w_node = [sb(f"w_node{k}", [F, 2, F]) for k in range(2)]
        w_msge = [sb(f"w_msge{k}", [F, F]) for k in range(2)]
        w_appa = [sb(f"w_appa{k}", [F, HID]) for k in range(2)]
        b_tag1 = sb("b_tag1", [1, HID])
        b_tag2 = sb("b_tag2", [1, HID])
        b_tag3 = sb("b_tag3", [1, 3 * F])
        b_root = [sb(f"b_root{k}", [P, F]) for k in range(2)]
        b_msg = [sb(f"b_msg{k}", [P, F]) for k in range(2)]
        b_app = [sb(f"b_app{k}", [P, F]) for k in range(2)]
        b_hyp = [sb(f"b_hyp{k}", [P, F]) for k in range(2)]

        ps = ctx.enter_context(nc.psum_tensor("ps", [P, 8 * BANK], FP32))
        CNT0 = 4 * BANK
        TR0 = 5 * BANK
        SECOND0 = 7 * BANK
        ATT0 = 4 * BANK
        MSG0 = 6 * BANK

        pool_steps = sem("pool_steps")
        sp_steps = sem("sp_steps")
        pe_steps = sem("pe_steps")
        edges_in = sem("edges_in")
        x_in = sem("x_in")
        weights_in = sem("weights_in")
        iota_made = sem("iota_made")
        consts_made = sem("consts_made")
        fill_made = sem("fill_made")
        filled_s = sem("filled_s")
        filled_d = sem("filled_d")
        cleared = sem("cleared")
        cleared_n = sem("cleared_n")
        ct_turned = sem("ct_turned")
        ct_ready = sem("ct_ready")
        ct_used = sem("ct_used")
        dve_step = sem("dve_step")
        totals_made = sem("totals_made")
        totals_summed = sem("totals_summed")
        ranked = sem("ranked")
        blocks_made = sem("blocks_made")
        slots_ready = sem("slots_ready")
        attr_in = [sem(f"attr_in{k}") for k in range(2)]
        scattered = [sem(f"scattered{k}") for k in range(2)]
        chunk_in = [sem(f"chunk_in{k}") for k in range(2)]
        chunk_used = sem("chunk_used")
        tiles_turned = sem("tiles_turned")
        turned_read = sem("turned_read")
        patches_counted = sem("patches_counted")
        patches_summed = sem("patches_summed")
        member_made = sem("member_made")
        chosen = sem("chosen")
        chosen_read = sem("chosen_read")
        patches_ready = sem("patches_ready")
        to_near = sem("to_near")
        to_ready = sem("to_ready")
        from_ready = sem("from_ready")
        patch_made = sem("patch_made")
        patch_summed = sem("patch_summed")
        ring_cleared = sem("ring_cleared")
        patch_stored = [sem(f"patch_stored{j}") for j in range(PST)]
        adj_in = [sem(f"adj_in{j}") for j in range(NCH)]
        adj_used = sem("adj_used")
        hop_in = sem("hop_in")
        table_stored = sem("table_stored")
        table_made = sem("table_made")
        acc_zeroed = sem("acc_zeroed")
        idx_ready = sem("idx_ready")
        gathered = [sem(f"gathered{k}") for k in range(RING)]
        sel_ready = sem("sel_ready")
        summed = sem("summed")
        acc_done = sem("acc_done")
        acc_saved = sem("acc_saved")
        att_loaded = [sem(f"att_loaded{k}") for k in range(RING)]
        att_turned = sem("att_turned")
        att_ready = sem("att_ready")
        att_projected = sem("att_projected")
        att_added = sem("att_added")
        att_relu = sem("att_relu")
        proj_in = sem("proj_in")
        turned = sem("turned")
        turned_sb = sem("turned_sb")
        product = sem("product")
        product_out = sem("product_out")
        var_made = sem("var_made")
        std_made = sem("std_made")
        out_stored = sem("out_stored")

        def index_of(q):
            return row_typed if q.get("typed") else row_src

        edge_table = records_d.rearrange("(p t) r -> p t r", p=P)
        slot_table = records_s.rearrange("(p t) r -> p t r", p=P)

        FCOL = NB * F // REC
        filler = h64[:, :, :].rearrange("p b d -> p (b d)")[:, 0:FCOL * REC].rearrange("p (c r) -> p c r", r=REC)

        def fill_parts(n):
            return [(c, min(FCOL, n - c)) for c in range(0, n, FCOL)]

        S_USED = [16 * (SCOL * SSTEPS + 1), 16 * SCOL * SSTEPS]
        D_USED = [u + 16 * DCOL * DSTEPS for u in S_USED]
        N_EDGE_LOADS, N_WEIGHTS = 8, 29
        block = ctx.enter_context(nc.Block())

        @block.sync
        def _(sp):
            sp.wait_ge(fill_made, 4)
            for t, main, tail in ((dst_i, a["dst_cols"], a["dst_tail"]), (src_i, a["src_cols"], a["src_tail"]),
                                  (typ_i, a["typ_cols"], a["typ_tail"]), (ew, a["w_cols"], a["w_tail"])):
                sp.dma_start(t[:, 0:COLS], main).then_inc(edges_in, 16)
                sp.dma_start(t[0:TAIL, COLS:EC], tail).then_inc(edges_in, 16)
            sp.wait_ge(fill_made, 6)

            def fill(table, n, done):
                for c, m in fill_parts(n):
                    sp.dma_start(table[:, c:c + m, :], filler[:, 0:m, :]).then_inc(done, 16)

            fill(slot_table, TILES, filled_s)
            sp.dma_start(x[:, 0:FULLB, :], a["x"][0:FULLB * P, :].rearrange("(b p) f -> p b f", p=P)).then_inc(x_in, 16)
            sp.dma_start(x[0:LASTN, FULLB, :], a["x"][FULLB * P:NODES, :]).then_inc(x_in, 16)
            loads = [
                (w_tag1a[:, :], a["L0_W1T"][0:HID, :]), (w_tag1b[:, :], a["L0_W1T"][HID:HID + F, :]),
                (w_tag2[:, :, :], a["L0_W2T"].rearrange("(k p) n -> p k n", p=HID)),
                (w_tag3[:, :, :], a["L0_W3T"].rearrange("(k p) n -> p k n", p=HID)),
                (b_tag1[:, :], a["L0_b1"]), (b_tag2[:, :], a["L0_b2"]), (b_tag3[:, 0:F], a["L0_b3"]),
            ]
            for k in range(2):
                s = str(k + 1)
                loads += [
                    (w_rel[k][:, :, :], a["L1_W" + s].rearrange("r d f -> d r f")),
                    (w_root[k][:, :], a["L1_root" + s]), (b_root[k][:, :], a["L1_b" + s].to_broadcast([P, F])),
                    (w_hyp[k][:, 0:F], a["L2_W" + s]), (b_hyp[k][:, :], a["L2_b" + s].to_broadcast([P, F])),
                    (w_node[k][:, 0, :], a["L3_W" + s + "_msg"][0:F, :]), (w_msge[k][:, :], a["L3_W" + s + "_msg"][F:2 * F, :]),
                    (b_msg[k][:, :], a["L3_b" + s + "_msg"].to_broadcast([P, F])),
                    (w_node[k][:, 1, :], a["L3_W" + s + "_app"][0:F, :]), (w_appa[k][:, 0:F], a["L3_W" + s + "_app"][F:2 * F, :]),
                    (b_app[k][:, :], a["L3_b" + s + "_app"].to_broadcast([P, F])),
                ]
            assert len(loads) == N_WEIGHTS
            for to, of in loads:
                sp.dma_start(to, of).then_inc(weights_in, 16)

            attr = a["edge_attr"][0:COLS * P, :].rearrange("(c p) f -> p c f", p=P)
            zero = t64[:, :, :].rearrange("p b d -> p (b d)")

            def clear(matrix, i, h, done):
                for c in range(2):
                    sp.dma_start(matrix[bass.ds(i * (2 * P) + h * P, P), c * ROWS // 2:(c + 1) * ROWS // 2], zero)\
                        .then_inc(done, 16)

            def load_attr(i, h, first=False):
                if not first:
                    sp.wait_ge(scattered[h], 16 * SCOL * i)
                sp.dma_start(rec_ring[:, h, 0:SCOL, META:REC],
                             attr[:, bass.ds(i * 2 * SCOL + h * SCOL, SCOL), :]).then_inc(attr_in[h], 16)
                clear(adj, i, h, cleared)

            for h in range(2):
                load_attr(0, h, first=True)
            fill(edge_table, TILES_D, filled_d)
            with sp.Fori(1, SSTEPS) as i:
                for h in range(2):
                    load_attr(i, h)
            sp.wait_ge(scattered[0], 16 * SCOL * SSTEPS)
            sp.dma_start(rec_ring[0:TAIL, 0, 0, META:REC], a["edge_attr"][COLS * P:EDGES, :]).then_inc(attr_in[0], 16)

            sp.wait_ge(scattered[0], S_USED[0])
            sp.wait_ge(scattered[1], S_USED[1])
            sp.wait_ge(ranked, 1)

            def load_chunks(table, c0):
                for c in range(MCH):
                    if c0 + c >= 2:
                        sp.wait_ge(chunk_used, c0 + c - 1)
                    sp.dma_start(chunk[c % 2], table[:, c * MT:(c + 1) * MT, :]).then_inc(chunk_in[c % 2], 16)

            load_chunks(slot_table, 0)

            def load_records(i, h):
                sp.wait_ge(scattered[h], i * (16 * DCOL) + S_USED[h])
                sp.dma_start(rec_ring[:, h, :, :], slot_table[:, bass.ds(i * 2 * DCOL + h * DCOL, DCOL), :])\
                    .then_inc(attr_in[h], 16)
                clear(adj_n, i, h, cleared_n)

            with sp.Fori(0, DSTEPS) as i:
                for h in range(2):
                    load_records(i, h)
            sp.wait_ge(scattered[0], D_USED[0])
            sp.wait_ge(scattered[1], D_USED[1])
            load_chunks(edge_table, MCH)

            sp.wait_ge(patches_ready, 1)
            sp.wait_ge(cleared, 16 * 4 * SSTEPS)

            def store_patches(matrix, ring, i, g0):
                _, at = nc.values_load_multi_w_load_instructions(
                    place_i[0:1, bass.ds(i * PST + g0 % PSTEPS * PST, PST)], engines=[mybir.EngineType.SP], min_val=0,
                    max_val=NB * P * ROWS + PST * P, skip_runtime_bounds_check_because="made from block numbers")
                for j in range(PST):
                    sp.wait_ge(patch_summed, i * PST + (g0 * PST + j + 1))
                    sp.sem_inc(sp_steps, 1)
                    sp.dma_start(bass.AP(tensor=matrix.tensor, offset=at[j], ap=[[ROWS, P], [1, P]]),
                                 ring[:, j, :]).then_inc(patch_stored[j], 16)

            with sp.Fori(0, PSTEPS) as i:
                store_patches(adj, patch_ring, i, 0)
            for j in range(PST):
                sp.wait_ge(patch_stored[j], 16 * PSTEPS)

            def load_matrix(n, matrix):
                with sp.Fori(0, NB) as b:
                    for j in range(NCH):
                        sp.wait_ge(adj_used, b * NCH + (NB * NCH * n + j + 1))
                        sp.dma_start(adj_ring[:, j, :], matrix[bass.ds(b * P, P), j * CHB * P:(j + 1) * CHB * P])\
                            .then_inc(adj_in[j], 16)

            for n in range(ND):
                load_matrix(n, adj)

            for g, n in enumerate(GATHERS):
                if g == 2:
                    for j in range(PST):
                        sp.wait_ge(patch_stored[j], 2 * 16 * PSTEPS)
                    sp.wait_ge(acc_done, GATHERS[1] + 1)
                    for k in range(ND, len(DENSE)):
                        load_matrix(k, adj_n)
                sp.wait_ge(table_made, g + 1)
                staged = wide if PASSES[n].get("typed") else t64[:, :, :]
                sp.dma_start(tables[n].rearrange("(p b) d -> p (b d)", p=P), staged.rearrange("p b d -> p (b d)"))\
                    .then_inc(table_stored, 16)
                if PASSES[n].get("typed"):
                    if g == 0:
                        sp.wait_ge(cleared_n, 16 * 4 * DSTEPS)
                    with sp.Fori(0, GPP if g == 0 else PSTEPS - GPP) as i:
                        store_patches(adj_n, cpatch_ring, i, PSTEPS + GPP * g)
                if PASSES[n].get("attr"):
                    with sp.Fori(0, ITERS) as i:
                        for s in range(RING):
                            sp.wait_ge(summed, i * RING + (GPP * g + s + 1))
                            sp.dma_start(attr_ring[:, s, :, :],
                                         edge_table[:, bass.ds(i * (RING * GRP) + s * GRP, GRP), META:REC])\
                                .then_inc(att_loaded[s], 16)
            sp.wait_ge(table_made, len(GATHERS) + 1)
            sp.dma_start(out[0:FULLB * P, :].rearrange("(b p) f -> p b f", p=P), x[:, 0:FULLB, :]).then_inc(out_stored, 16)
            sp.dma_start(out[FULLB * P:NODES, :], x[0:LASTN, FULLB, :]).then_inc(out_stored, 16)
            sp.wait_ge(out_stored, 32)

        @block.gpsimd
        def _(pool):
            nc.gpsimd.iota(iota_i[:, :], pattern=[[1, P]], base=0, channel_multiplier=0).then_inc(iota_made, 1)
            nc.gpsimd.iota(part_i[:, :], pattern=[[0, 1]], base=0, channel_multiplier=1).then_inc(iota_made, 1)
            nc.gpsimd.iota(tile0_i[:, :], pattern=[[P, TILES]], base=0, channel_multiplier=0).then_inc(iota_made, 1)

            def put(table, h, j):
                nc.gpsimd.indirect_dma_start(
                    out=table, out_offset=bass.IndirectOffsetOnAxis(ap=slot_ring[:, h, j:j + 1], axis=0),
                    in_=rec_ring[:, h, j, :], in_offset=None).then_inc(scattered[h], 16)

            pool.wait_ge(filled_s, 16 * len(fill_parts(TILES)))
            with pool.Fori(0, SSTEPS) as i:
                for h in range(2):
                    pool.wait_ge(slots_ready, i * 2 + h + 1)
                    pool.wait_ge(attr_in[h], i * 16 + 16)
                    pool.sem_inc(pool_steps, 1)
                    for j in range(SCOL):
                        put(records_s, h, j)
            pool.wait_ge(slots_ready, 2 * SSTEPS + 1)
            pool.wait_ge(attr_in[0], 16 * (SSTEPS + 1))
            put(records_s, 0, 0)
            pool.wait_ge(ranked, 2)
            pool.wait_ge(filled_d, 16 * len(fill_parts(TILES_D)))
            a0 = [16 * (SSTEPS + 1), 16 * SSTEPS]
            with pool.Fori(0, DSTEPS) as i:
                for h in range(2):
                    pool.wait_ge(slots_ready, i * 2 + (2 * SSTEPS + 1 + h + 1))
                    pool.wait_ge(attr_in[h], i * 16 + (a0[h] + 16))
                    pool.sem_inc(pool_steps, 1)
                    for j in range(DCOL):
                        put(records_d, h, j)
            nc.gpsimd.iota(p_iota_i, pattern=[[1, PATCHES]], base=0, channel_multiplier=0).then_inc(iota_made, 1)
            pool.wait_ge(iota_made, 5)
            nc.gpsimd.iota(p_iota_i, pattern=[[0, PSTEPS], [P, PST]], base=NB * P * ROWS, channel_multiplier=0)\
                .then_inc(iota_made, 1)

            for g, n in enumerate(GATHERS):
                pool.wait_ge(table_stored, 16 * (g + 1))
                g0 = GPP * g
                with pool.Fori(0, ITERS) as i:
                    for s in range(RING):
                        pool.wait_ge(idx_ready, i * RING + (g0 + s + 1))
                        pool.sem_inc(pool_steps, 1)
                        for j in range(GRP):
                            nc.gpsimd.indirect_dma_start(
                                out=msg_ring[:, s, j * F:(j + 1) * F], out_offset=None, in_=tables[n],
                                in_offset=bass.IndirectOffsetOnAxis(ap=idx_ring[:, s, j:j + 1], axis=0),
                            ).then_inc(gathered[s], 16)

        @block.tensor
        def _(pe):
            for k in range(2):
                pe.wait_ge(totals_made, k + 1)
                nc.tensor.matmul(ps[:, 0:NB + 1], below[:, :], tot[:, :], start=True, stop=True)
                nc.tensor.matmul(ps[:, BANK:BANK + NB + 1], ones[:, :], tot[:, :], start=True, stop=True)\
                    .then_inc(totals_summed, 1)
            pe.wait_ge(consts_made, 1)
            pe.wait_ge(blocks_made, 1)
            for m, t in enumerate((blk_f, bsrc_real, blk2_f, src_s, loc_dst[:, :], w_s)):
                for k in range(TK):
                    last = nc.tensor.transpose(ps[0:TQ, m * BANK + k * P:m * BANK + (k + 1) * P],
                                               t[:, k * TQ:(k + 1) * TQ], ident[:, :])
            last.then_inc(tiles_turned, 1)
            pe.wait_ge(patches_counted, 1)
            nc.tensor.matmul(ps[0:TQ, 0:TK], below[0:TQ, 0:TQ], n_pat[:, :], start=True, stop=True)
            nc.tensor.matmul(ps[0:TQ, BANK:BANK + TK], ones[0:TQ, 0:TQ], n_pat[:, :], start=True, stop=True)\
                .then_inc(patches_summed, 1)
            pe.wait_ge(member_made, 1)

            def choose(lhs):
                for m, t in enumerate(lhs):
                    for h in range(2):
                        for k in range(TK):
                            last = nc.tensor.matmul(ps[:, (2 * m + h) * BANK:(2 * m + h) * BANK + PH],
                                                    ones[0:TQ, :] if t is None else t[:, k, :],
                                                    member[:, k, h * PH:(h + 1) * PH], start=k == 0, stop=k + 1 == TK)
                last.then_inc(chosen, 1)

            choose([src_t, shift_t, loc_t, w_t])
            pe.wait_ge(chosen_read, 1)
            choose([tile_t, None])
            pe.wait_ge(patches_ready, 1)

            def patches(to, fr, i, g0, bank0, banks, first=False):
                for j in range(PST):
                    n = g0 * PST + j + 1
                    pe.wait_ge(to_ready, i * PST + n)
                    pe.wait_ge(from_ready, i * PST + n)
                    if not (first and j < banks):
                        pe.wait_ge(patch_summed, i * PST + (n - banks))
                    c = (bank0 + j % banks) * BANK
                    nc.tensor.matmul(ps[:, c:c + P], to[:, j, :], fr[:, j, :], start=True, stop=True,
                                     skip_group_check=True).then_inc(patch_made, 1)

            patches(to_ring, from_ring, 0, 0, 0, PBANKS, first=True)
            with pe.Fori(1, PSTEPS) as i:
                patches(to_ring, from_ring, i, 0, 0, PBANKS)
            pe.wait_ge(patch_summed, PATCHES)

            pe.wait_ge(weights_in, 16 * N_WEIGHTS)

            def zero_acc(n):
                q = PASSES[n]
                banks = -(-NB * (HID if q.get("dense") else F) // BANK)
                for k in range(banks):
                    last = nc.tensor.matmul(ps[:, k * BANK:(k + 1) * BANK], zeros[:, 0:P], zeros[:, :],
                                            start=True, stop=False, skip_group_check=True)
                last.then_inc(acc_zeroed, 1)
                if n == 0:
                    for free, m in ((summed, RING), (adj_used, NCH), (ct_used, 2)):
                        nc.tensor.matmul(ps[:, 0:1], zeros[:, 0:P], zeros[:, 0:1],
                                         start=False, stop=False, skip_group_check=True).then_inc(free, m)

            def close_pass():
                nc.tensor.matmul(ps[:, 0:1], zeros[:, 0:P], zeros[:, 0:1],
                                 start=False, stop=False, skip_group_check=True).then_inc(acc_done, 1)

            def turned_pass(n, of):
                m = DENSE.index(n)
                t0 = 2 * NCH * NB * ((m - ND) // 2)
                pe.wait_ge(hop_in, m + 1)
                pe.wait_ge(acc_saved, n)
                zero_acc(n)
                with pe.Fori(0, NB) as b:
                    for u in range(2 * NCH + 1):
                        if u < 2 * NCH:
                            j, sub = u // 2, SUB[u % 2]
                            if u % 2 == 0:
                                pe.wait_ge(adj_in[j], b * 16 + 16 * (NB * m + 1))
                            if not (t0 == 0 and u == 0):
                                pe.wait_ge(ct_ready, b * (2 * NCH) + (t0 + u))
                            else:
                                pe.wait_ge(ct_ready, b * (2 * NCH))
                            pe.sem_inc(pe_steps, 1)
                            for q, k in enumerate(sub):
                                last = nc.tensor.transpose(ps[:, 7 * BANK + q * P:7 * BANK + (q + 1) * P],
                                                           adj_ring[:, j, k * P:(k + 1) * P], ident[:, :])
                            last.then_inc(ct_turned, 1)
                        if u:
                            j, sub = (u - 1) // 2, SUB[(u - 1) % 2]
                            pe.wait_ge(ct_ready, b * (2 * NCH) + (t0 + u))
                            for q, k in enumerate(sub):
                                last = nc.tensor.matmul(ps[:, bass.ds(b * P, P)],
                                                        turned_ring[:, (u - 1) % 2, q * P:(q + 1) * P],
                                                        of[:, j * CHB + k, :],
                                                        start=False, stop=False, skip_group_check=True)
                            last.then_inc(ct_used, 1)
                            if (u - 1) % 2:
                                pe.sem_inc(adj_used, 1)
                close_pass()

            def dense_pass(n, of):
                m = DENSE.index(n)
                pe.wait_ge(hop_in, m + 1)
                if n:
                    pe.wait_ge(acc_saved, n)
                zero_acc(n)
                with pe.Fori(0, NB) as b:
                    for j in range(NCH):
                        pe.wait_ge(adj_in[j], b * 16 + 16 * (NB * m + 1))
                        for k in range(CHB):
                            c = (j * CHB + k) * P
                            last = nc.tensor.matmul(ps[:, c:c + P], adj_ring[:, j, k * P:(k + 1) * P],
                                                    of[:, bass.ds(b, 1), :].rearrange("p a d -> p (a d)"),
                                                    start=False, stop=False, skip_group_check=True)
                        last.then_inc(adj_used, 1)
                close_pass()

            def sum_group(n, i, s):
                q = PASSES[n]
                d = F
                g = GPP * GATHERS.index(n)
                offsets = blk64
                _, at = nc.values_load_multi_w_load_instructions(
                    offsets[0:1, bass.ds(i * (RING * GRP) + s * GRP, GRP)], engines=[mybir.EngineType.PE],
                    min_val=0, max_val=(NB - 1) * d, skip_runtime_bounds_check_because="blocks are 0..24")
                if q.get("attr"):
                    l0 = GPP * (n - (NPASS - 2))
                    pe.wait_ge(att_relu, i * RING + (l0 + s + 1))
                else:
                    pe.wait_ge(gathered[s], i * (16 * GRP) + 16 * GRP * (ITERS * GATHERS.index(n) + 1))
                pe.wait_ge(sel_ready, i * RING + (g + s + 1))
                for j in range(GRP):
                    rhs = (relu_ring if q.get("attr") else msg_ring)[:, s, j * d:(j + 1) * d]
                    last = nc.tensor.matmul(ps[:, bass.ds(at[j], d)], sel_ring[:, s, j, :], rhs,
                                            start=False, stop=False, skip_group_check=True)
                last.then_inc(summed, 1)

            def turn_attr(l, i, s, first=False):
                n = NPASS - 2 + l
                pe.wait_ge(att_loaded[s], i * 16 + 16 * (ITERS * l + 1))
                if not first:
                    pe.wait_ge(att_ready, i * RING + (GPP * l + s))
                pe.sem_inc(pe_steps, 1)
                for j in range(GRP):
                    last = nc.tensor.transpose(ps[0:F, ATT0 + j * P:ATT0 + (j + 1) * P], attr_ring[:, s, j, :], ident[:, :])
                last.then_inc(att_turned, 1)

            def project_attr(l, i, s, first=False):
                pe.wait_ge(att_ready, i * RING + (GPP * l + s + 1))
                if not first:
                    pe.wait_ge(att_added, i * RING + (GPP * l + s))
                m0 = MSG0 + BANK * (s % 2)
                for j in range(GRP):
                    last = nc.tensor.matmul(ps[:, m0 + j * F:m0 + (j + 1) * F], attrT[:, j * P:(j + 1) * P],
                                            w_msge[l][:, :], start=True, stop=True, skip_group_check=True)
                last.then_inc(att_projected, 1)

            def run_pass(n):
                q = PASSES[n]
                pe.wait_ge(acc_saved, n)
                zero_acc(n)
                if q.get("attr"):
                    l = n - (NPASS - 2)
                    turn_attr(l, 0, 0, first=(l == 0))
                    project_attr(l, 0, 0, first=(l == 0))

                    def steps(i, last=False):
                        for s in range(RING):
                            more = not (last and s == RING - 1)
                            ni, ns = (i, s + 1) if s + 1 < RING else (i + 1, 0)
                            if more:
                                turn_attr(l, ni, ns)
                            sum_group(n, i, s)
                            if more:
                                project_attr(l, ni, ns)

                    with pe.Fori(0, ITERS - 1) as i:
                        steps(i)
                    steps(ITERS - 1, last=True)
                else:
                    m = GATHERS.index(n)

                    def steps(i, last=False):
                        for s in range(RING):
                            if not (last and m == 1 and s >= RING - 2):
                                patches(cto_ring, cfrom_ring, i * RING, PSTEPS + GPP * m + s, 4, CBANKS)
                            sum_group(n, i, s)

                    with pe.Fori(0, ITERS - 1) as i:
                        steps(i)
                    steps(ITERS - 1, last=True)
                close_pass()

            def project(name, inputs, weights, bias=None, weights2=None):
                q = PROJ[name]
                d = q["d"]
                pitch = 256 if d == 3 * F else d
                for g in range(NG):
                    m = q["index"] * NG + g
                    for k, (of, kd) in enumerate(zip(inputs, q["k"])):
                        t = q["tr0"] + g * len(q["k"]) + k
                        if g == 0 and k == 0:
                            pe.wait_ge(proj_in, q["index"] + 1)
                        if t:
                            pe.wait_ge(turned_sb, t)
                        for b in range(GB):
                            last = nc.tensor.transpose(ps[0:kd, TR0 + b * P:TR0 + (b + 1) * P],
                                                       of[:, g * GB + b, 0:kd], ident[:, :])
                        last.then_inc(turned, 1)
                    pe.wait_ge(turned_sb, q["tr0"] + (g + 1) * len(q["k"]))
                    if m:
                        pe.wait_ge(product_out, m)
                    for b in range(GB):
                        for c0, w, bi, dd in ((b * pitch, weights, bias, d), (SECOND0 + b * F, weights2, None, F)):
                            if w is None:
                                continue
                            for k, (wk, kd) in enumerate(zip(w, q["k"])):
                                last = nc.tensor.matmul(ps[:, c0:c0 + dd], xT[0:kd, k, b * P:(b + 1) * P], wk,
                                                        start=k == 0, stop=k + 1 == len(w) and bi is None,
                                                        skip_group_check=True)
                            if bi is not None:
                                last = nc.tensor.matmul(ps[:, c0:c0 + dd], ones[0:1, :], bi, start=False, stop=True,
                                                        skip_group_check=True)
                    last.then_inc(product, 1)

            def flat(t):
                return t[:, :, :].rearrange("p k n -> p (k n)")

            dense_pass(0, xf)
            dense_pass(1, xf)
            project("tag1", [xf, agg], [w_tag1a[:, :], w_tag1b[:, :]], b_tag1[:, :])
            pe.wait_ge(product_out, NG * 1)
            dense_pass(2, h1)
            dense_pass(3, hop)
            project("tag2", [h1, hop, agg], [w_tag2[:, k, :] for k in range(3)], b_tag2[:, :])
            project("tag3", [xf], [flat(w_tag3)], b_tag3[:, :])
            pe.wait_ge(product_out, NG * 3)
            dense_pass(4, agg)
            dense_pass(5, agg)
            project("rgcn1", [x], [flat(w_rel[0])], None, [w_root[0][:, :]])
            pe.wait_ge(product_out, NG * 4)
            run_pass(6)
            project("rgcn2", [h64], [flat(w_rel[1])], None, [w_root[1][:, :]])
            pe.wait_ge(product_out, NG * 5)
            run_pass(7)
            project("hyper1", [x], [w_hyp[0][:, :]])
            pe.wait_ge(product_out, NG * 6)
            turned_pass(8, agg)
            dense_pass(9, agg)
            project("hyper2", [h64], [w_hyp[1][:, :]])
            pe.wait_ge(product_out, NG * 7)
            turned_pass(10, agg)
            dense_pass(11, agg)
            project("mpnn1", [x], [flat(w_node[0])])
            pe.wait_ge(product_out, NG * 8)
            run_pass(12)
            project("app1", [agg], [w_appa[0][:, :]])
            project("mpnn2", [h64], [flat(w_node[1])])
            pe.wait_ge(product_out, NG * 10)
            run_pass(13)
            project("app2", [agg], [w_appa[1][:, :]])

        @block.scalar
        def _(act):
            def make_records(i, h, waited, n=SCOL):
                c = bass.ds(i * (2 * SCOL) + h * SCOL, n)
                if waited is not None:
                    act.wait_ge(scattered[h], waited)
                for w, t in enumerate((src_i, dst_i, ew, typ_i)):
                    nc.scalar.copy(rec_ring[:, h, 0:n, w], t[:, c])
                nc.scalar.copy(slot_ring[:, h, 0:n], slot_i[0][:, c]).then_inc(slots_ready, 1)

            act.wait_ge(edges_in, 16 * N_EDGE_LOADS)
            act.wait_ge(ranked, 1)
            for h in range(2):
                make_records(0, h, None)
            with act.Fori(1, SSTEPS) as i:
                for h in range(2):
                    make_records(i, h, i * (16 * SCOL))
            make_records(SSTEPS, 0, 16 * SCOL * SSTEPS, n=1)

            act.wait_ge(patches_ready, 1)

            def select_to(to, i, g0, first=False):
                half = PST // 2
                for h in range(2):
                    for j in range(h * half, (h + 1) * half):
                        if not first:
                            act.wait_ge(patch_made, i * PST + (g0 * PST + j + 1 - PST))
                        nc.scalar.activation(to[:, j, :], iota_f[:, :], ACT.Abs,
                                             bias=p_loc[:, bass.ds(i * PST + (g0 % PSTEPS * PST + j), 1)])\
                            .then_inc(to_near, 1)
                    for j in range(h * half, (h + 1) * half):
                        act.wait_ge(to_near, i * PST + (g0 * PST + j + 1))
                        nc.scalar.activation(to[:, j, :], to[:, j, :], ACT.Relu, bias=1.0, scale=-1.0)\
                            .then_inc(to_ready, 1)

            select_to(to_ring, 0, 0, first=True)
            with act.Fori(1, PSTEPS) as i:
                select_to(to_ring, i, 0)

            def count_pass(m):
                with act.Fori(0, GPP if m == 0 else PSTEPS - GPP) as i:
                    select_to(cto_ring, i, PSTEPS + GPP * m)

            def turned_out(m):
                t0 = 2 * NCH * NB * m
                with act.Fori(0, NB) as b:
                    for u in range(2 * NCH):
                        act.wait_ge(ct_turned, b * (2 * NCH) + (t0 + u + 1))
                        act.wait_ge(ct_used, b * (2 * NCH) + (t0 + u + 1))
                        n = len(SUB[u % 2]) * P
                        nc.scalar.copy(turned_ring[:, u % 2, 0:n], ps[:, 7 * BANK:7 * BANK + n]).then_inc(ct_ready, 1)

            def turn_out(name):
                q = PROJ[name]
                for g in range(NG):
                    for k, kd in enumerate(q["k"]):
                        t = q["tr0"] + g * len(q["k"]) + k
                        m = q["index"] * NG + g
                        act.wait_ge(turned, t + 1)
                        if m:
                            act.wait_ge(product, m)
                        nc.scalar.copy(xT[0:kd, k, :], ps[0:kd, TR0:TR0 + GB * P]).then_inc(turned_sb, 1)

            def make_std(n):
                act.wait_ge(var_made, n)
                nc.scalar.activation(std[:, :], var[:, :], ACT.Sqrt).then_inc(std_made, 1)

            def attr_out(l, i, s, first=False):
                act.wait_ge(att_turned, i * RING + (GPP * l + s + 1))
                if not first:
                    act.wait_ge(att_projected, i * RING + (GPP * l + s))
                nc.scalar.copy(attrT, ps[0:F, ATT0:ATT0 + GRP * P]).then_inc(att_ready, 1)

            def attr_pass(l):
                attr_out(l, 0, 0, first=(l == 0))

                def steps(i, last=False):
                    for s in range(RING):
                        act.wait_ge(att_added, i * RING + (GPP * l + s + 2))
                        nc.scalar.activation(relu_ring[:, s, :], relu_ring[:, s, :], ACT.Relu).then_inc(att_relu, 1)
                        if not (last and s == RING - 1):
                            ni, ns = (i, s + 1) if s + 1 < RING else (i + 1, 0)
                            attr_out(l, ni, ns)

                with act.Fori(0, ITERS - 1) as i:
                    steps(i)
                steps(ITERS - 1, last=True)

            turn_out("tag1")
            turn_out("tag2")
            turn_out("tag3")
            make_std(1)
            turn_out("rgcn1")
            act.wait_ge(ring_cleared, 1)
            count_pass(0)
            turn_out("rgcn2")
            count_pass(1)
            make_std(2)
            turn_out("hyper1")
            turned_out(0)
            turn_out("hyper2")
            turned_out(1)
            make_std(3)
            turn_out("mpnn1")
            attr_pass(0)
            turn_out("app1")
            turn_out("mpnn2")
            attr_pass(1)
            turn_out("app2")
            make_std(4)

        @block.vector
        def _(dve):
            done = [0]

            def step(ins):
                ins.then_inc(dve_step, 1)
                done[0] += 1
                dve.wait_ge(dve_step, done[0])

            v = nc.vector
            v.memset(src_i[:, COLS:EC], SENT).then_inc(fill_made, 1)
            v.memset(dst_i[:, COLS:EC], SENT).then_inc(fill_made, 1)
            v.memset(typ_i[:, COLS:EC], 0).then_inc(fill_made, 1)
            v.memset(ew[:, COLS:EC], 0.0).then_inc(fill_made, 1)
            v.memset(x[:, FULLB, :], 0.0).then_inc(fill_made, 1)
            v.memset(t64[:, :, :], 0.0)
            v.memset(rec_ring[:, :, :, :], 0.0)
            step(v.memset(filler, 0.0))
            v.memset(filler[:, :, 0:2], float(SENT)).then_inc(fill_made, 1)
            v.memset(b_tag3[:, F:3 * F], 0.0)
            for k in range(2):
                v.memset(w_hyp[k][:, F:HID], 0.0)
                v.memset(w_appa[k][:, F:HID], 0.0)
            v.memset(ones[:, :], 1.0)
            v.memset(zeros[:, :], 0.0)
            dve.wait_ge(iota_made, 3)
            step(v.tensor_copy(iota_f[:, :], iota_i[:, :]))
            step(v.tensor_copy(part_f[:, :], part_i[:, :]))
            v.tensor_copy(tile0_f[:, :], tile0_i[:, :])
            v.tensor_scalar(ident[:, :], iota_f[:, :], part_f[:, 0:1], None, ALU.is_equal)
            v.tensor_scalar(below[:, :], iota_f[:, :], part_f[:, 0:1], None, ALU.is_gt).then_inc(consts_made, 1)

            dve.wait_ge(edges_in, 16 * N_EDGE_LOADS)

            def rank(k, n, b0):
                eq = eq_all[:, 0:(NB + 1) * n].rearrange("p (b c) -> p b c", c=n)
                cum = cum_all[:, 0:(NB + 1) * n].rearrange("p (b c) -> p b c", c=n)
                with dve.Fori(0, NB + 1) as b:
                    v.tensor_scalar(eq[:, bass.ds(b, 1), :].rearrange("p a c -> p (a c)"), blk_f[:, 0:n],
                                    iota_f[:, bass.ds(b, 1)], None, ALU.is_equal).then_inc(dve_step, 1)
                    dve.wait_ge(dve_step, b + (done[0] + 1))
                    row = eq[:, bass.ds(b, 1), :].rearrange("p a c -> p (a c)")
                    v.tensor_tensor_scan(cum[:, bass.ds(b, 1), :].rearrange("p a c -> p (a c)"), row, row, 0.0,
                                         ALU.add, ALU.bypass)
                done[0] += NB + 1
                dve.drain()
                v.tensor_copy(tot[:, :], cum[:, :, n - 1]).then_inc(totals_made, 1)
                dve.wait_ge(totals_summed, k + 1)
                step(v.tensor_scalar(padded_i[:, :], ps[:, BANK:BANK + NB + 1], float(P - 1), None, ALU.add))
                step(v.tensor_scalar(padded_i[:, :], padded_i[:, :], 7, 7, ALU.logical_shift_right,
                                     ALU.logical_shift_left))
                step(v.tensor_copy(padded_f[:, :], padded_i[:, :]))
                step(v.tensor_tensor_scan(start[:, :], padded_f[:, :], padded_f[:, :], 0.0, ALU.add, ALU.bypass))
                step(v.tensor_tensor(start[:, :], start[:, :], padded_f[:, :], ALU.subtract))
                step(v.scalar_tensor_tensor(base[:, :], ps[:, 0:NB + 1], -1.0, start[:, :], ALU.add, ALU.add))
                with dve.Fori(0, NB + 1) as b:
                    c = cum[:, bass.ds(b, 1), :].rearrange("p a c -> p (a c)")
                    v.scalar_tensor_tensor(c, c, base[:, bass.ds(b, 1)],
                                           eq[:, bass.ds(b, 1), :].rearrange("p a c -> p (a c)"),
                                           ALU.add, ALU.mult)
                dve.drain()
                step(v.tensor_reduce(blk_f[:, 0:n], cum.rearrange("p b c -> p c b"), AX.X, ALU.add))
                step(v.tensor_copy(slot_i[k][:, :], blk_f[:, 0:n]))

            def tile_blocks():
                step(v.memset(tblk[:, :], 0.0))
                for b in range(1, NB):
                    step(v.scalar_tensor_tensor(tblk[:, :], tile0_f[:, :], start[0:1, b:b + 1], tblk[:, :],
                                                ALU.is_ge, ALU.add))
                step(v.tensor_scalar(blk64[:, :], tblk[:, :], float(F), None, ALU.mult))

            def split_ids(ids, n=TILES):
                step(v.tensor_copy(low_i[:, 0:n], ids))
                step(v.tensor_scalar(blk_i[:, 0:n], low_i[:, 0:n], 7, None, ALU.logical_shift_right))
                step(v.tensor_scalar(low_i[:, 0:n], low_i[:, 0:n], P - 1, None, ALU.bitwise_and))

            def rows_of(to):
                v.scalar_tensor_tensor(to, low_i[:, :], float(NB), blk_i[:, :], ALU.mult, ALU.add)

            def place_of(to, ids):
                step(v.tensor_scalar(to, blk_i[:, :], float(NB - 1), float(-P), ALU.min, ALU.mult))
                step(v.tensor_tensor(to, ids, to, ALU.add))

            split_ids(src_i[:, :], EC)
            step(v.tensor_copy(blk_f[:, 0:EC], blk_i[:, 0:EC]))
            rank(0, EC, 0)
            v.engine_nop().then_inc(ranked, 1)

            for c in range(MCH):
                dve.wait_ge(chunk_in[c % 2], 16 * (c // 2 + 1))
                v.tensor_copy(key_f[:, c * MT:(c + 1) * MT], chunk[c % 2][:, :, 1]).then_inc(chunk_used, 1)
            dve.wait_ge(chunk_used, MCH)
            split_ids(key_f)
            step(v.tensor_copy(blk_f, blk_i))
            rank(1, TILES, 0)
            v.tensor_scalar(low_i, slot_i[1][:, :], P - 1, None, ALU.bitwise_and)
            step(v.tensor_scalar(blk_i, slot_i[1][:, :], 7, None, ALU.logical_shift_right))
            step(v.scalar_tensor_tensor(slot_i[1][:, :], low_i, float(TILES_D), blk_i, ALU.mult, ALU.add))
            v.engine_nop().then_inc(ranked, 1)
            with dve.Fori(0, DSTEPS) as i:
                for h in range(2):
                    dve.wait_ge(scattered[h], i * (16 * DCOL) + S_USED[h])
                    v.tensor_copy(slot_ring[:, h, :], slot_i[1][:, bass.ds(i * (2 * DCOL) + h * DCOL, DCOL)])\
                        .then_inc(slots_ready, 1)
            tile_blocks()

            for c in range(MCH):
                dve.wait_ge(chunk_in[c % 2], 16 * ((MCH + c) // 2 + 1))
                for w, t in enumerate((src_s, dst_s, w_s, typ_s)):
                    last = v.tensor_copy(t[:, c * MT:(c + 1) * MT], chunk[c % 2][:, :, w])
                last.then_inc(chunk_used, 1)
            dve.wait_ge(chunk_used, 2 * MCH)
            split_ids(dst_s)
            v.tensor_copy(blk2_f, blk_i)
            place_of(loc_dst[:, :], dst_s)
            split_ids(src_s)
            v.tensor_copy(blk_f, blk_i)
            rows_of(row_src[:, :])
            step(v.engine_nop())
            step(v.scalar_tensor_tensor(bsrc_real, blk_f, float(NB), blk_f, ALU.is_lt, ALU.mult))
            step(v.scalar_tensor_tensor(row_typed[:, :], row_src[:, :], float(TYPES), typ_s, ALU.mult, ALU.add))
            v.engine_nop().then_inc(blocks_made, 1)

            def banks(m):
                return ps[0:TQ, m * BANK:(m + 1) * BANK].rearrange("p (k c) -> p k c", k=TK)

            dve.wait_ge(tiles_turned, 1)
            v.tensor_reduce(first_b[:, :], banks(0), AX.X, ALU.min)
            v.tensor_reduce(last_b[:, :], banks(1), AX.X, ALU.max)
            v.tensor_reduce(tile_b[:, :], banks(2), AX.X, ALU.min)
            v.tensor_copy(src_t, banks(3))
            v.tensor_copy(loc_t, banks(4))
            step(v.tensor_copy(w_t, banks(5)))
            step(v.scalar_tensor_tensor(n_pat[:, :], last_b[:, :], 1.0, first_b[:, :], ALU.add, ALU.subtract))
            step(v.tensor_scalar(n_pat[:, :], n_pat[:, :], 0.0, None, ALU.max))
            v.engine_nop().then_inc(patches_counted, 1)
            dve.wait_ge(patches_summed, 1)
            step(v.tensor_copy(tot_pat[:, :], ps[0:TQ, BANK:BANK + TK]))
            step(v.tensor_tensor_scan(cum_pat[:, :], tot_pat[:, :], tot_pat[:, :], 0.0, ALU.add, ALU.bypass))
            step(v.tensor_tensor(cum_pat[:, :], cum_pat[:, :], tot_pat[:, :], ALU.subtract))
            step(v.tensor_tensor(pat0[:, :], ps[0:TQ, 0:TK], cum_pat[:, :], ALU.add))
            step(v.tensor_tensor(pat1[:, :], pat0[:, :], n_pat[:, :], ALU.add))
            step(v.tensor_tensor(shift[:, :], first_b[:, :], pat0[:, :], ALU.subtract))
            v.tensor_copy(shift_t, shift[:, :].unsqueeze(2).to_broadcast([TQ, TK, P]))
            v.tensor_copy(tile_t, tile_b[:, :].unsqueeze(2).to_broadcast([TQ, TK, P]))
            dve.wait_ge(iota_made, 4)
            step(v.tensor_copy(p_iota, p_iota_i))
            v.engine_nop().then_inc(iota_made, 1)
            for k in range(TK):
                step(v.tensor_scalar(member[:, k, :], p_iota[0:TQ, :], pat1[:, k:k + 1], None, ALU.is_lt))
                step(v.scalar_tensor_tensor(member[:, k, :], p_iota[0:TQ, :], pat0[:, k:k + 1], member[:, k, :],
                                            ALU.is_ge, ALU.mult))
            v.engine_nop().then_inc(member_made, 1)
            dve.wait_ge(iota_made, 6)
            step(v.tensor_copy(p_trash, p_iota_i))

            def two(t):
                return t.rearrange("p (h c) -> p h c", h=2)

            def chosen_at(m):
                return ps[:, 2 * m * BANK:2 * (m + 1) * BANK].rearrange("p (h c) -> p h c", h=2)[:, :, 0:PH]

            dve.wait_ge(chosen, 1)
            step(v.tensor_tensor(two(p_blk), chosen_at(1), two(p_iota), ALU.add))
            step(v.scalar_tensor_tensor(two(p_src), two(p_blk), float(-P), chosen_at(0), ALU.mult, ALU.add))
            v.tensor_scalar(two(p_loc), chosen_at(2), -1.0, None, ALU.mult)
            step(v.tensor_copy(two(p_w), chosen_at(3)))
            v.engine_nop().then_inc(chosen_read, 1)
            dve.wait_ge(chosen, 2)
            step(v.scalar_tensor_tensor(two(p_id), chosen_at(0), float(NB), two(p_blk), ALU.mult, ALU.add))
            step(v.scalar_tensor_tensor(two(p_id), two(p_id), float(-NB * NB), chosen_at(1), ALU.add, ALU.mult))
            step(v.memset(p_keep[:, 0:1], 0.0))
            step(v.tensor_tensor(p_keep[:, 1:PATCHES], p_id[:, 1:PATCHES], p_id[:, 0:PATCHES - 1], ALU.is_equal))
            r = slice(0, 1)
            step(v.scalar_tensor_tensor(two(p_tmp)[r], chosen_at(0)[r], float(P * ROWS), two(p_trash)[r],
                                        ALU.mult, ALU.subtract))
            step(v.scalar_tensor_tensor(p_tmp[r], p_blk[r], float(P), p_tmp[r], ALU.mult, ALU.add))
            step(v.tensor_scalar(p_blk[r, 0:PATCHES - 1], p_keep[r, 1:PATCHES], -1.0, 1.0, ALU.mult, ALU.add))
            step(v.memset(p_blk[r, PATCHES - 1:PATCHES], 1.0))
            step(v.scalar_tensor_tensor(p_blk[r], p_id[r], 0.0, p_blk[r], ALU.is_lt, ALU.mult))
            step(v.tensor_tensor(p_tmp[r], p_tmp[r], p_blk[r], ALU.mult))
            step(v.tensor_tensor(place_i[:, :], p_tmp[r], p_trash[r], ALU.add))
            step(v.memset(patch_ring, 0.0))
            v.engine_nop().then_inc(patches_ready, 1)

            def select_from(to, i, j, g0, weighted=True):
                c = bass.ds(i * PST + (g0 % PSTEPS * PST + j), 1)
                if weighted:
                    last = v.tensor_scalar(to[:, j, :], iota_f[:, :], p_src[:, c], p_w[:, c], ALU.is_equal, ALU.mult)
                else:
                    last = v.tensor_scalar(to[:, j, :], iota_f[:, :], p_src[:, c], None, ALU.is_equal)
                last.then_inc(from_ready, 1)

            def join_patch(ring, i, j, g0, bank, first=False):
                n = g0 * PST + j
                dve.wait_ge(patch_made, i * PST + (n + 1))
                if not first:
                    dve.wait_ge(patch_stored[j], i * 16 + 16 * g0)
                if not (first and j == 0):
                    dve.wait_ge(patch_summed, i * PST + n)
                v.scalar_tensor_tensor(ring[:, j, :], ring[:, (j - 1) % PST, :],
                                       p_keep[:, bass.ds(i * PST + (g0 % PSTEPS * PST + j), 1)],
                                       ps[:, bank * BANK:bank * BANK + P], ALU.mult, ALU.add).then_inc(patch_summed, 1)

            for j in range(PST):
                select_from(from_ring, 0, j, 0)
            for j in range(PST):
                join_patch(patch_ring, 0, j, 0, j % PBANKS, first=True)
                select_from(from_ring, 1, j, 0)
            with dve.Fori(1, PSTEPS - 1) as i:
                for j in range(PST):
                    join_patch(patch_ring, i, j, 0, j % PBANKS)
                    select_from(from_ring, i, j, 1)
            for j in range(PST):
                join_patch(patch_ring, PSTEPS - 1, j, 0, j % PBANKS)
            dve.wait_ge(patch_summed, PATCHES)

            dve.wait_ge(x_in, 32)
            step(v.memset(xf[:, :, F:HID], 0.0))
            step(v.tensor_copy(xf[:, :, 0:F], x[:, :, :]))
            v.engine_nop().then_inc(hop_in, 1)

            def prepare(n, i, s):
                q = PASSES[n]
                g = GPP * GATHERS.index(n) + s
                c0 = i * (RING * GRP) + s * GRP
                dve.wait_ge(summed, i * RING + (g + 1))
                v.tensor_copy(idx_ring[:, s, :], index_of(q)[:, bass.ds(c0, GRP)]).then_inc(idx_ready, 1)
                for j in range(GRP):
                    c = bass.ds(c0 + j, 1)
                    last = v.tensor_scalar(sel_ring[:, s, j, :], iota_f[:, :], loc_dst[:, c], None, ALU.is_equal)
                last.then_inc(sel_ready, 1)

            def run_pass(n):
                if PASSES[n].get("attr"):
                    l = n - (NPASS - 2)
                    prepare(n, 0, 0)
                    prepare(n, 0, 1)

                    def steps(i, last=False):
                        for s in range(RING):
                            if not (last and s >= RING - 2):
                                ni, ns = (i, s + 2) if s + 2 < RING else (i + 1, s + 2 - RING)
                                prepare(n, ni, ns)
                            dve.wait_ge(gathered[s], i * (16 * GRP) + 16 * GRP * (ITERS * GATHERS.index(n) + 1))
                            dve.wait_ge(att_projected, i * RING + (GPP * l + s + 1))
                            m0 = MSG0 + BANK * (s % 2)
                            v.tensor_tensor(relu_ring[:, s, :], ps[:, m0:m0 + GRP * F], msg_ring[:, s, 0:GRP * F],
                                            ALU.add).then_inc(att_added, 1)

                    with dve.Fori(0, ITERS - 1) as i:
                        steps(i)
                    steps(ITERS - 1, last=True)
                else:
                    m = GATHERS.index(n)
                    if m == 0:
                        step(v.memset(cpatch_ring, 0.0))
                        for j in range(PST):
                            select_from(cfrom_ring, 0, j, PSTEPS, weighted=False)
                    prepare(n, 0, 0)
                    prepare(n, 0, 1)

                    def steps(i, last=False):
                        for s in range(RING):
                            if not (last and s >= RING - 2):
                                ni, ns = (i, s + 2) if s + 2 < RING else (i + 1, s + 2 - RING)
                                prepare(n, ni, ns)
                            if last and m == 1 and s >= RING - 2:
                                continue
                            g0 = PSTEPS + GPP * m + s
                            for j in range(PST):
                                join_patch(cpatch_ring, i * RING, j, g0, 4 + j % CBANKS)
                                if not (last and m == 1 and s == RING - 3):
                                    select_from(cfrom_ring, i * RING, j, g0 + 1, weighted=False)

                    with dve.Fori(0, ITERS - 1) as i:
                        steps(i)
                    steps(ITERS - 1, last=True)
                dve.wait_ge(acc_done, n + 1)

            def sums(n):
                return ps[:, 0:NB * F].rearrange("p (b d) -> p b d", d=F)

            def dense_sums(c=0, d=F):
                return ps[:, 0:NB * HID].rearrange("p (b d) -> p b d", d=HID)[:, :, c:c + d]

            def drain_products(name, post):
                q = PROJ[name]
                d = q["d"]
                pitch = 256 if d == 3 * F else d
                for g in range(NG):
                    dve.wait_ge(product, q["index"] * NG + g + 1)
                    b = slice(g * GB, (g + 1) * GB)
                    first = ps[:, 0:GB * pitch].rearrange("p (b d) -> p b d", d=pitch)[:, :, 0:d]
                    second = ps[:, SECOND0:SECOND0 + GB * F].rearrange("p (b d) -> p b d", d=F)
                    post(b, first, second).then_inc(product_out, 1)

            def wide_of(t, n=F):
                return t.unsqueeze(2).to_broadcast([P, NB, n])

            def layernorm(z, n):
                step(v.tensor_reduce(mean[:, :], z, AX.X, ALU.add))
                step(v.tensor_scalar(mean[:, :], mean[:, :], 1.0 / F, None, ALU.mult))
                step(v.tensor_tensor(z, z, wide_of(mean[:, :]), ALU.subtract))
                step(v.tensor_tensor(x[:, :, :], z, z, ALU.mult))
                step(v.tensor_reduce(var[:, :], x[:, :, :], AX.X, ALU.add))
                v.tensor_scalar(var[:, :], var[:, :], 1.0 / F, LN_EPS, ALU.mult, ALU.add).then_inc(var_made, 1)
                dve.wait_ge(std_made, n)
                step(v.reciprocal(rstd[:, :], std[:, :]))
                step(v.tensor_tensor(x[:, :, :], z, wide_of(rstd[:, :]), ALU.mult))

            def signal(s):
                v.engine_nop().then_inc(s, 1)

            def leaky(to):
                def post(b, first, second):
                    step(v.tensor_copy(to[:, b, :], first))
                    return v.scalar_tensor_tensor(to[:, b, :], to[:, b, :], SLOPE, to[:, b, :], ALU.mult, ALU.max)
                return post

            def along(t):
                return t[:, :].unsqueeze(1).to_broadcast([P, GB, F])

            def relational(k):
                def post(b, first, second):
                    v.tensor_tensor(r64[:, b, :], second, along(b_root[k]), ALU.add)
                    return v.tensor_copy(wide[:, b, :], first)
                return post

            def hyper(b, first, second):
                return v.tensor_copy(agg[:, b, 0:F], first[:, :, 0:F])

            def message(k):
                def post(b, first, second):
                    v.tensor_tensor(t64[:, b, :], first[:, :, 0:F], along(b_msg[k]), ALU.add)
                    return v.tensor_tensor(r64[:, b, :], first[:, :, F:HID], along(b_app[k]), ALU.add)
                return post

            def inverse_degree(k):
                step(v.tensor_copy(cnt[:, :], dense_sums(F, 1).rearrange("p b d -> p (b d)")))
                v.tensor_scalar(has[:, :], cnt[:, :], 1.0, None, ALU.min)
                step(v.tensor_scalar(inv[k][:, :], cnt[:, :], 1.0, None, ALU.max))
                step(v.reciprocal(inv[k][:, :], inv[k][:, :]))
                step(v.tensor_tensor(inv[k][:, :], inv[k][:, :], has[:, :], ALU.mult))

            v.engine_nop().then_inc(att_added, 1)

            def saved(n):
                dve.wait_ge(acc_saved, n)

            dve.wait_ge(acc_done, 1)
            v.tensor_copy(xf[:, :, F:HID], dense_sums()).then_inc(acc_saved, 1)
            saved(1)
            signal(hop_in)
            dve.wait_ge(acc_done, 2)
            v.tensor_copy(agg[:, :, 0:F], dense_sums(F)).then_inc(acc_saved, 1)
            saved(2)
            signal(proj_in)
            drain_products("tag1", leaky(h1))
            dve.wait_ge(product_out, NG)
            signal(hop_in)
            dve.wait_ge(acc_done, 3)
            v.tensor_copy(hop, dense_sums(0, HID)).then_inc(acc_saved, 1)
            saved(3)
            signal(hop_in)
            dve.wait_ge(acc_done, 4)
            v.tensor_copy(agg[:, :, :], dense_sums(0, HID)).then_inc(acc_saved, 1)
            saved(4)
            signal(proj_in)
            drain_products("tag2", leaky(xf))
            dve.wait_ge(product_out, 2 * NG)
            signal(proj_in)

            def split(b, first, second):
                v.tensor_copy(part[:, b, :], first[:, :, 0:2 * F])
                return v.tensor_copy(agg[:, b, 0:F], first[:, :, 2 * F:3 * F])

            drain_products("tag3", split)
            dve.wait_ge(product_out, 3 * NG)
            signal(hop_in)
            dve.wait_ge(acc_done, 5)
            v.tensor_tensor(agg[:, :, 0:F], dense_sums(), part[:, :, F:2 * F], ALU.add).then_inc(acc_saved, 1)
            saved(5)
            signal(hop_in)
            dve.wait_ge(acc_done, 6)
            v.tensor_tensor(h64[:, :, :], dense_sums(), part[:, :, 0:F], ALU.add).then_inc(acc_saved, 1)
            dve.wait_ge(acc_saved, 6)
            step(v.tensor_tensor(h64[:, :, :], h64[:, :, :], x[:, :, :], ALU.add))
            layernorm(h64[:, :, :], 1)
            signal(proj_in)

            signal(ring_cleared)
            drain_products("rgcn1", relational(0))
            signal(table_made)
            run_pass(6)
            v.tensor_tensor(h64[:, :, :], sums(6), r64[:, :, :], ALU.add).then_inc(acc_saved, 1)
            dve.wait_ge(acc_saved, 7)
            step(v.tensor_scalar(h64[:, :, :], h64[:, :, :], 0.0, None, ALU.max))
            signal(proj_in)
            drain_products("rgcn2", relational(1))
            signal(table_made)
            run_pass(7)
            v.tensor_tensor(h64[:, :, :], sums(7), r64[:, :, :], ALU.add).then_inc(acc_saved, 1)
            dve.wait_ge(acc_saved, 8)
            step(v.tensor_tensor(h64[:, :, :], h64[:, :, :], x[:, :, :], ALU.add))
            layernorm(h64[:, :, :], 2)
            signal(proj_in)

            v.memset(agg[:, :, F:F + 1], 1.0)
            v.memset(agg[:, :, F + 1:HID], 0.0)
            drain_products("hyper1", hyper)
            dve.wait_ge(product_out, 6 * NG)
            signal(hop_in)
            for k in range(2):
                n = 8 + 2 * k
                dve.wait_ge(acc_done, n + 1)
                if k == 0:
                    inverse_degree(0)
                v.tensor_tensor(agg[:, :, 0:F], dense_sums(), wide_of(inv[0][:, :]), ALU.mult).then_inc(acc_saved, 1)
                saved(n + 1)
                signal(hop_in)
                dve.wait_ge(acc_done, n + 2)
                if k == 0:
                    inverse_degree(1)
                v.tensor_tensor(h64[:, :, :], dense_sums(), wide_of(inv[1][:, :]), ALU.mult).then_inc(acc_saved, 1)
                saved(n + 2)
                bias = b_hyp[k][:, :].unsqueeze(1).to_broadcast([P, NB, F])
                step(v.tensor_tensor(h64[:, :, :], h64[:, :, :], bias, ALU.add))
                if k == 0:
                    step(v.tensor_scalar(h64[:, :, :], h64[:, :, :], 0.0, None, ALU.max))
                    signal(proj_in)
                    drain_products("hyper2", hyper)
                    dve.wait_ge(product_out, 7 * NG)
                    signal(hop_in)
            step(v.tensor_tensor(h64[:, :, :], h64[:, :, :], x[:, :, :], ALU.add))
            layernorm(h64[:, :, :], 3)
            signal(proj_in)

            drain_products("mpnn1", message(0))
            signal(table_made)

            def applied(kept, to):
                def post(b, first, second):
                    step(v.tensor_tensor(r64[:, b, :], first[:, :, 0:F], r64[:, b, :], ALU.add))
                    return v.scalar_tensor_tensor(to[:, b, :], r64[:, b, :], 0.0, kept[:, b, :], ALU.max, ALU.add)
                return post

            run_pass(12)
            v.tensor_copy(agg[:, :, 0:F], sums(12)).then_inc(acc_saved, 1)
            signal(proj_in)
            drain_products("app1", applied(x, h64))
            signal(proj_in)
            drain_products("mpnn2", message(1))
            signal(table_made)
            run_pass(13)
            v.tensor_copy(agg[:, :, 0:F], sums(13)).then_inc(acc_saved, 1)
            signal(proj_in)
            drain_products("app2", applied(h64, h64))
            dve.wait_ge(product_out, NG * len(PROJ))
            step(v.tensor_tensor(h64[:, :, :], h64[:, :, :], x[:, :, :], ALU.add))
            layernorm(h64[:, :, :], 4)
            signal(table_made)


def kernel(**inputs):
    import numpy as np
    import concourse.bacc as bacc
    from concourse.bass_utils import run_bass_kernel_spmd

    def arr(name):
        return np.ascontiguousarray(inputs[name])

    arrays = {"x": arr("x"), "edge_attr": arr("edge_attr_64")}
    n = COLS * P
    for short, name in (("src", "src"), ("dst", "dst"), ("typ", "edge_type_8"), ("w", "edge_weight")):
        v = arr(name)
        arrays[short + "_cols"] = np.ascontiguousarray(v[:n].reshape(COLS, P).T)
        arrays[short + "_tail"] = np.ascontiguousarray(v[n:].reshape(TAIL, 1))
    for k in (1, 2, 3):
        arrays[f"L0_W{k}T"] = np.ascontiguousarray(arr(f"L0_gnn_W{k}").T)
        arrays[f"L0_b{k}"] = arr(f"L0_gnn_b{k}").reshape(1, -1)
    for k in ("1", "2"):
        arrays["L1_W" + k] = arr("L1_gnn_W" + k)
        arrays["L1_root" + k] = arr("L1_gnn_root" + k)
        arrays["L1_b" + k] = arr("L1_gnn_b" + k).reshape(1, -1)
        arrays["L2_W" + k] = arr("L2_gnn_W" + k)
        arrays["L2_b" + k] = arr("L2_gnn_b" + k).reshape(1, -1)
        for part in ("_msg", "_app"):
            arrays["L3_W" + k + part] = arr("L3_gnn_W" + k + part)
            arrays["L3_b" + k + part] = arr("L3_gnn_b" + k + part).reshape(1, -1)

    nc = bacc.Bacc("TRN2", target_bir_lowering=False, num_devices=1)
    feeds, aps = {}, {}
    for name, v in arrays.items():
        feeds["in_" + name] = v
        aps[name] = nc.dram_tensor("in_" + name, v.shape, mybir.dt.from_np(v.dtype), kind="ExternalInput").ap()
    out = nc.dram_tensor("out_0", (NODES, F), FP32, kind="ExternalOutput").ap()
    gnn_kernel(nc, aps, out)
    r = run_bass_kernel_spmd(nc, [feeds], core_ids=[0])
    return r.results[0]["out_0"]
```

```python
from contextlib import ExitStack

import concourse.bass as bass
from concourse import mybir

FP32 = mybir.dt.float32
BF16 = mybir.dt.bfloat16
I32 = mybir.dt.int32
ALU = mybir.AluOpType
ACT = mybir.ActivationFunctionType
AX = mybir.AxisListType

P = 128
NODES = 3125
EDGES = 50000
F = 64
HID = 128
TYPES = 8
LN_EPS = 1e-5
SLOPE = 0.01

NB = -(-NODES // P)
FULLB = NODES // P
LASTN = NODES - FULLB * P
ROWS = NB * P
COLS = EDGES // P
TAIL = EDGES - COLS * P
EC = COLS + 1
SENT = NB * P
GRP = 8
RING = 4
TILES = -(-((EDGES + NB * (P - 1)) // P + 1) // (GRP * RING)) * GRP * RING
ITERS = TILES // (GRP * RING)
GPP = TILES // GRP
SLOTS = TILES * P
TILES_D = TILES + -(-(SLOTS - EDGES) // P)
META = 4
REC = META + F
SCOL = 15
SSTEPS = COLS // (2 * SCOL)
assert SSTEPS * 2 * SCOL == COLS
DCOL = 16
DSTEPS = TILES // (2 * DCOL)
assert DSTEPS * 2 * DCOL == TILES
MCH = 8
MT = TILES // MCH
PST = 10
PATCHES = -(-(TILES + NB * (NB - 1)) // (2 * PST)) * 2 * PST
PSTEPS = PATCHES // PST
PSLOTS = 2 * PST
PBANK0 = [0, 4]
PBANKS = [5, 4]
CREDIT = [0, 16]
CSETS = [GPP, PSTEPS - GPP]
assert CSETS[0] % RING == 0 and CSETS[1] % 2 == 0 and CSETS[1] == GPP - 2
PH = PATCHES // 2
TK = 4
TQ = TILES // TK
BANK = 512
NG = 5
ROOTW = 96
GB = NB // NG
assert NG * GB == NB and GB * ROOTW <= BANK

PASSES = (
    [dict(dense=True)] * 6 + [dict(typed=True)] * 2
    + [dict(dense=True, turned=True), dict(dense=True)] * 2 + [dict(attr=True)] * 2
)
NPASS = len(PASSES)
GATHERS = [n for n, q in enumerate(PASSES) if not q.get("dense")]
DENSE = [n for n, q in enumerate(PASSES) if q.get("dense")]
ND = 6
CHB = 5
NCH = NB // CHB
TB = 5

PROJ = {
    "tag1": dict(k=[HID, F], d=HID, d2=0),
    "tag2": dict(k=[HID, HID, HID], d=HID, d2=0),
    "tag3": dict(k=[HID], d=3 * F, d2=0),
    "rgcn1": dict(k=[F], d=TYPES * F, d2=ROOTW),
    "rgcn2": dict(k=[F], d=TYPES * F, d2=ROOTW),
    "hyper1": dict(k=[F], d=HID, d2=0),
    "hyper2": dict(k=[F], d=HID, d2=0),
    "mpnn1": dict(k=[F], d=HID, d2=0),
    "app1": dict(k=[F], d=HID, d2=0),
    "mpnn2": dict(k=[F], d=HID, d2=0),
    "app2": dict(k=[F], d=HID, d2=0),
}
_tr = 0
for _i, _p in enumerate(PROJ.values()):
    _p["index"] = _i
    _p["tr0"] = _tr
    _tr += NG * len(_p["k"])


def gnn_kernel(nc, a, out):
    ctx = ExitStack()
    with ctx:
        def sb(name, shape, dt=FP32):
            return ctx.enter_context(nc.sbuf_tensor(name, shape, dt))

        def sem(name):
            return ctx.enter_context(nc.semaphore(name))

        def dram(name, shape, dt=FP32):
            return nc.dram_tensor(name, shape, dt, kind="Internal").ap()

        records_s = dram("records_s", (SLOTS, REC))
        records_d = dram("records_d", (P * TILES_D, REC))
        adj = dram("adj", ((NB + 1) * P, ROWS))
        adj_n = dram("adj_n", ((NB + 1) * P, ROWS))
        tables = {n: dram(f"table{n}", (ROWS * (TYPES if q.get("typed") else 1), F))
                  for n, q in enumerate(PASSES) if not q.get("dense")}

        iota_i = sb("iota_i", [P, P], I32)
        iota_f = sb("iota_f", [P, P])
        part_i = sb("part_i", [P, 1], I32)
        part_f = sb("part_f", [P, 1])
        ident = sb("ident", [P, P])
        below = sb("below", [P, P])
        ones = sb("ones", [P, P])
        zeros = sb("zeros", [P, BANK], BF16)
        tile0_i = sb("tile0_i", [1, TILES], I32)
        tile0_f = sb("tile0_f", [1, TILES])

        src_i = sb("src_i", [P, EC], I32)
        dst_i = sb("dst_i", [P, EC], I32)
        typ_i = sb("typ_i", [P, EC], I32)
        ew = sb("ew", [P, EC])
        slot_i = [sb("slot_s", [P, EC], I32), sb("slot_d", [P, TILES], I32)]
        sel_ring = sb("sel_ring", [P, RING, GRP, P])
        flat_sel = sel_ring[:, :, :, :].rearrange("p s g c -> p (s g c)")
        work = flat_sel[:, 0:9 * TILES].rearrange("p (n c) -> p n c", n=9)
        blk_f, key_f = work[:, 0, :], work[:, 1, :]
        blk_i, low_i = work[:, 2, :].bitcast(I32), work[:, 3, :].bitcast(I32)
        src_s, dst_s, w_s, typ_s, bsrc_real = (work[:, k, :] for k in range(4, 9))
        blk2_f = work[:, 1, :]
        big = sb("big", [P, NCH * CHB * P])
        msg_ring = big[:, 0:RING * GRP * F].rearrange("p (s c) -> p s c", s=RING)
        rec_ring = big[:, 0:2 * DCOL * REC].rearrange("p (h c r) -> p h c r", h=2, c=DCOL)
        adj_ring = big[:, :].rearrange("p (j c) -> p j c", j=NCH)
        slot_ring = sb("slot_ring", [P, 2, DCOL], I32)
        tot = sb("tot", [P, NB + 1])
        base = sb("base", [P, NB + 1])
        padded_i = sb("padded_i", [P, NB + 1], I32)
        padded_f = sb("padded_f", [P, NB + 1])
        start = sb("start", [P, NB + 1])
        tblk = sb("tblk", [1, TILES])
        blk64 = sb("blk64", [1, TILES], I32)
        first_b = sb("first_b", [TQ, TK])
        last_b = sb("last_b", [TQ, TK])
        tile_b = sb("tile_b", [TQ, TK])
        n_pat = sb("n_pat", [TQ, TK])
        tot_pat = sb("tot_pat", [TQ, TK])
        cum_pat = sb("cum_pat", [TQ, TK])
        pat0 = sb("pat0", [TQ, TK])
        pat1 = sb("pat1", [TQ, TK])
        shift = sb("shift", [TQ, TK])
        place_i = sb("place_i", [1, PATCHES], I32)

        row_src = sb("row_src", [P, TILES], I32)
        row_typed = sb("row_typed", [P, TILES], I32)
        loc_dst = sb("loc_dst", [P, TILES])

        idx_ring = sb("idx_ring", [P, RING, GRP], I32)
        area = sb("area", [P, 16500])
        AEQ = (NB + 1) * TILES // 2
        eq_all = area[:, 0:AEQ].bitcast(BF16)
        cum_all = area[:, AEQ:AEQ + (NB + 1) * TILES]
        chunk = [area[:, k * MT * REC:(k + 1) * MT * REC].rearrange("p (t r) -> p t r", r=REC)
                 for k in range(2)]
        member = area[0:TQ, 0:TK * PATCHES].rearrange("p (k c) -> p k c", k=TK)
        o = TK * PATCHES
        src_t, loc_t, w_t, shift_t, tile_t = (
            area[0:TQ, o + n * TK * P:o + (n + 1) * TK * P].rearrange("p (k c) -> p k c", k=TK) for n in range(5))
        o += 5 * TK * P
        p_w, p_blk, p_id, p_iota, p_trash, p_tmp = (
            area[:, o + n * PATCHES:o + (n + 1) * PATCHES] for n in range(6))
        o = NB * TYPES * F
        p_src, p_loc, p_keep = (area[:, o + n * PATCHES:o + (n + 1) * PATCHES] for n in range(3))
        p_iota_i = p_tmp.bitcast(I32)
        wide = area[:, 0:NB * TYPES * F].rearrange("p (b d) -> p b d", b=NB)
        attr_ring = area[:, 12800:12800 + RING * GRP * F].rearrange("p (s g f) -> p s g f", s=RING, g=GRP)
        relu_ring = area[:, 1024:1024 + RING * GRP * F].rearrange("p (s g) -> p s g", s=RING)
        attrT = area[0:F, 0:GRP * P]

        def nodes(name, d):
            return sb(name, [P, NB, d])

        x = nodes("x", F)
        xf = nodes("xf", HID)
        agg = nodes("agg", HID)
        h1 = area[:, 0:NB * HID].rearrange("p (b d) -> p b d", b=NB)
        hop = area[:, NB * HID:2 * NB * HID].rearrange("p (b d) -> p b d", b=NB)
        part = area[:, 2 * NB * HID:3 * NB * HID].rearrange("p (b d) -> p b d", b=NB)
        t64 = nodes("t64", F)
        r64 = nodes("r64", F)
        h64 = nodes("h64", F)
        def slots_of(t, n):
            return t[:, 0:n * P].rearrange("p (j c) -> p j c", j=n)

        flat_agg = agg[:, :, :].rearrange("p b d -> p (b d)")
        flat_xf = xf[:, :, :].rearrange("p b d -> p (b d)")
        flat_t64 = t64[:, :, :].rearrange("p b d -> p (b d)")
        to_rings = [slots_of(big[:, :], PSLOTS), slots_of(flat_agg, PSLOTS)]
        from_rings = [slots_of(flat_sel, PSLOTS), slots_of(flat_xf, PSLOTS)]
        patch_rings = [[flat_agg[:, j * P:(j + 1) * P] for j in range(PSLOTS)],
                       [flat_t64[:, j * P:(j + 1) * P] for j in range(PST)]
                       + [t[:, j * P:(j + 1) * P] for t in (flat_agg, flat_xf) for j in range(PSLOTS, NB)]]
        assert len(patch_rings[1]) == PSLOTS
        SUB = [range(0, 3), range(3, CHB)]
        turned_ring = area[:, 0:2 * 3 * P].rearrange("p (u c) -> p u c", u=2)
        xT = sb("xT", [P, 3, GB * P])
        mean = sb("mean", [P, NB])
        var = sb("var", [P, NB])
        std = sb("std", [P, NB])
        rstd = sb("rstd", [P, NB])
        cnt = sb("cnt", [P, NB])
        has = sb("has", [P, NB])
        inv = [sb(f"inv{k}", [P, NB]) for k in range(2)]

        w_tag1a = sb("w_tag1a", [HID, HID])
        w_tag1b = sb("w_tag1b", [F, HID])
        w_tag2 = sb("w_tag2", [HID, 3, HID])
        w_tag3 = sb("w_tag3", [HID, 3, F])
        w_rel = [sb(f"w_rel{k}", [F, TYPES, F]) for k in range(2)]
        w_root = [sb(f"w_root{k}", [F, ROOTW]) for k in range(2)]
        w_hyp = [sb(f"w_hyp{k}", [F, HID]) for k in range(2)]
        w_node = [sb(f"w_node{k}", [F, 2, F]) for k in range(2)]
        w_msge = [sb(f"w_msge{k}", [F, F]) for k in range(2)]
        w_appa = [sb(f"w_appa{k}", [F, HID]) for k in range(2)]
        b_tag1 = sb("b_tag1", [1, HID])
        b_tag2 = sb("b_tag2", [1, HID])
        b_tag3 = sb("b_tag3", [1, 3 * F])
        b_root = [sb(f"b_root{k}", [P, F]) for k in range(2)]
        b_msg = [sb(f"b_msg{k}", [P, F]) for k in range(2)]
        b_app = [sb(f"b_app{k}", [P, F]) for k in range(2)]
        b_hyp = [sb(f"b_hyp{k}", [P, F]) for k in range(2)]

        ps = ctx.enter_context(nc.psum_tensor("ps", [P, 8 * BANK], FP32))
        TR0 = 5 * BANK
        SECOND0 = 7 * BANK
        ATT0 = 4 * BANK
        MSG0 = 6 * BANK

        pool_steps = sem("pool_steps")
        sp_steps = sem("sp_steps")
        pe_steps = sem("pe_steps")
        edges_in = sem("edges_in")
        x_in = sem("x_in")
        weights_in = sem("weights_in")
        iota_made = sem("iota_made")
        consts_made = sem("consts_made")
        fill_made = sem("fill_made")
        filled_s = sem("filled_s")
        filled_d = sem("filled_d")
        cleared = sem("cleared")
        cleared_n = sem("cleared_n")
        ct_turned = sem("ct_turned")
        ct_ready = sem("ct_ready")
        ct_used = sem("ct_used")
        row_saved = sem("row_saved")
        dve_step = sem("dve_step")
        totals_made = sem("totals_made")
        totals_summed = sem("totals_summed")
        ranked = sem("ranked")
        blocks_made = sem("blocks_made")
        slots_ready = sem("slots_ready")
        attr_in = [sem(f"attr_in{k}") for k in range(2)]
        scattered = [sem(f"scattered{k}") for k in range(2)]
        chunk_in = [sem(f"chunk_in{k}") for k in range(2)]
        chunk_used = sem("chunk_used")
        tiles_turned = sem("tiles_turned")
        turned_read = sem("turned_read")
        patches_counted = sem("patches_counted")
        patches_summed = sem("patches_summed")
        member_made = sem("member_made")
        chosen = sem("chosen")
        chosen_read = sem("chosen_read")
        patches_ready = sem("patches_ready")
        to_near = sem("to_near")
        to_ready = sem("to_ready")
        from_made = sem("from_made")
        from_ready = sem("from_ready")
        patch_made = sem("patch_made")
        patch_summed = sem("patch_summed")
        ring_cleared = sem("ring_cleared")
        patch_stored = [[sem(f"patch_stored{k}_{h}") for h in range(2)] for k in range(2)]
        adj_in = [sem(f"adj_in{j}") for j in range(NCH)]
        adj_used = sem("adj_used")
        hop_in = sem("hop_in")
        table_stored = sem("table_stored")
        table_made = sem("table_made")
        acc_zeroed = sem("acc_zeroed")
        idx_ready = sem("idx_ready")
        gathered = [sem(f"gathered{k}") for k in range(RING)]
        sel_ready = sem("sel_ready")
        summed = sem("summed")
        acc_done = sem("acc_done")
        acc_saved = sem("acc_saved")
        att_loaded = [sem(f"att_loaded{k}") for k in range(RING)]
        att_turned = sem("att_turned")
        att_ready = sem("att_ready")
        att_projected = sem("att_projected")
        att_added = sem("att_added")
        att_relu = sem("att_relu")
        proj_in = sem("proj_in")
        turned = sem("turned")
        turned_sb = sem("turned_sb")
        product = sem("product")
        rel_made = sem("rel_made")
        rel_out = sem("rel_out")
        product_out = sem("product_out")
        var_made = sem("var_made")
        std_made = sem("std_made")
        out_stored = sem("out_stored")

        def index_of(q):
            return row_typed if q.get("typed") else row_src

        edge_table = records_d.rearrange("(p t) r -> p t r", p=P)
        slot_table = records_s.rearrange("(p t) r -> p t r", p=P)

        FCOL = NB * F // REC
        filler = h64[:, :, :].rearrange("p b d -> p (b d)")[:, 0:FCOL * REC].rearrange("p (c r) -> p c r", r=REC)

        def fill_parts(n):
            return [(c, min(FCOL, n - c)) for c in range(0, n, FCOL)]

        S_USED = [16 * (SCOL * SSTEPS + 1), 16 * SCOL * SSTEPS]
        D_USED = [u + 16 * DCOL * DSTEPS for u in S_USED]
        N_EDGE_LOADS, N_WEIGHTS = 8, 29
        block = ctx.enter_context(nc.Block())

        @block.sync
        def _(sp):
            sp.wait_ge(fill_made, 4)
            for t, main, tail in ((dst_i, a["dst_cols"], a["dst_tail"]), (src_i, a["src_cols"], a["src_tail"]),
                                  (typ_i, a["typ_cols"], a["typ_tail"]), (ew, a["w_cols"], a["w_tail"])):
                sp.dma_start(t[:, 0:COLS], main).then_inc(edges_in, 16)
                sp.dma_start(t[0:TAIL, COLS:EC], tail).then_inc(edges_in, 16)
            sp.wait_ge(fill_made, 6)

            def fill(table, n, done):
                for c, m in fill_parts(n):
                    sp.dma_start(table[:, c:c + m, :], filler[:, 0:m, :]).then_inc(done, 16)

            fill(slot_table, TILES, filled_s)
            sp.dma_start(x[:, 0:FULLB, :], a["x"][0:FULLB * P, :].rearrange("(b p) f -> p b f", p=P)).then_inc(x_in, 16)
            sp.dma_start(x[0:LASTN, FULLB, :], a["x"][FULLB * P:NODES, :]).then_inc(x_in, 16)
            loads = [
                (w_tag1a[:, :], a["L0_W1T"][0:HID, :]), (w_tag1b[:, :], a["L0_W1T"][HID:HID + F, :]),
                (w_tag2[:, :, :], a["L0_W2T"].rearrange("(k p) n -> p k n", p=HID)),
                (w_tag3[:, :, :], a["L0_W3T"].rearrange("(k p) n -> p k n", p=HID)),
                (b_tag1[:, :], a["L0_b1"]), (b_tag2[:, :], a["L0_b2"]), (b_tag3[:, 0:F], a["L0_b3"]),
            ]
            for k in range(2):
                s = str(k + 1)
                loads += [
                    (w_rel[k][:, :, :], a["L1_W" + s].rearrange("r d f -> d r f")),
                    (w_root[k][:, 0:F], a["L1_root" + s]), (b_root[k][:, :], a["L1_b" + s].to_broadcast([P, F])),
                    (w_hyp[k][:, 0:F], a["L2_W" + s]), (b_hyp[k][:, :], a["L2_b" + s].to_broadcast([P, F])),
                    (w_node[k][:, 0, :], a["L3_W" + s + "_msg"][0:F, :]), (w_msge[k][:, :], a["L3_W" + s + "_msg"][F:2 * F, :]),
                    (b_msg[k][:, :], a["L3_b" + s + "_msg"].to_broadcast([P, F])),
                    (w_node[k][:, 1, :], a["L3_W" + s + "_app"][0:F, :]), (w_appa[k][:, 0:F], a["L3_W" + s + "_app"][F:2 * F, :]),
                    (b_app[k][:, :], a["L3_b" + s + "_app"].to_broadcast([P, F])),
                ]
            assert len(loads) == N_WEIGHTS
            for to, of in loads:
                sp.dma_start(to, of).then_inc(weights_in, 16)

            attr = a["edge_attr"][0:COLS * P, :].rearrange("(c p) f -> p c f", p=P)
            zero = t64[:, :, :].rearrange("p b d -> p (b d)")

            def clear(matrix, i, h, done):
                for c in range(2):
                    sp.dma_start(matrix[bass.ds(i * (2 * P) + h * P, P), c * ROWS // 2:(c + 1) * ROWS // 2], zero)\
                        .then_inc(done, 16)

            def load_attr(i, h, first=False):
                if not first:
                    sp.wait_ge(scattered[h], 16 * SCOL * i)
                sp.dma_start(rec_ring[:, h, 0:SCOL, META:REC],
                             attr[:, bass.ds(i * 2 * SCOL + h * SCOL, SCOL), :]).then_inc(attr_in[h], 16)
                clear(adj, i, h, cleared)

            for h in range(2):
                load_attr(0, h, first=True)
            fill(edge_table, TILES_D, filled_d)
            with sp.Fori(1, SSTEPS) as i:
                for h in range(2):
                    load_attr(i, h)
            sp.wait_ge(scattered[0], 16 * SCOL * SSTEPS)
            sp.dma_start(rec_ring[0:TAIL, 0, 0, META:REC], a["edge_attr"][COLS * P:EDGES, :]).then_inc(attr_in[0], 16)

            sp.wait_ge(scattered[0], S_USED[0])
            sp.wait_ge(scattered[1], S_USED[1])
            sp.wait_ge(ranked, 1)

            def load_chunks(table, c0):
                for c in range(MCH):
                    if c0 + c >= 2:
                        sp.wait_ge(chunk_used, c0 + c - 1)
                    sp.dma_start(chunk[c % 2], table[:, c * MT:(c + 1) * MT, :]).then_inc(chunk_in[c % 2], 16)

            load_chunks(slot_table, 0)

            def load_records(i, h):
                sp.wait_ge(scattered[h], i * (16 * DCOL) + S_USED[h])
                sp.dma_start(rec_ring[:, h, :, :], slot_table[:, bass.ds(i * 2 * DCOL + h * DCOL, DCOL), :])\
                    .then_inc(attr_in[h], 16)
                clear(adj_n, i, h, cleared_n)

            with sp.Fori(0, DSTEPS) as i:
                for h in range(2):
                    load_records(i, h)
            sp.wait_ge(scattered[0], D_USED[0])
            sp.wait_ge(scattered[1], D_USED[1])
            load_chunks(edge_table, MCH)

            sp.wait_ge(patches_ready, 1)
            sp.wait_ge(cleared, 16 * 4 * SSTEPS)

            def store_patches(k, matrix, i, c0):
                _, at = nc.values_load_multi_w_load_instructions(
                    place_i[0:1, bass.ds(i * (2 * PST) + c0, PST)], engines=[mybir.EngineType.SP], min_val=0,
                    max_val=NB * P * ROWS + 2 * PST * P, skip_runtime_bounds_check_because="made from block numbers")
                for j in range(PST):
                    slot = (c0 + j) % PSLOTS
                    if j % (PST // 2) == 0:
                        sp.wait_ge(patch_summed, i * (2 * PST) + (k * PATCHES + c0 + j + PST // 2))
                        sp.sem_inc(sp_steps, 1)
                    sp.dma_start(bass.AP(tensor=matrix.tensor, offset=at[j], ap=[[ROWS, P], [1, P]]),
                                 patch_rings[k][slot]).then_inc(patch_stored[k][c0 // PST % 2], 16)

            def all_stored(k):
                for stored in patch_stored[k]:
                    sp.wait_ge(stored, 16 * (PATCHES // 2) + CREDIT[k])

            with sp.Fori(0, PSTEPS // 2) as i:
                for h in range(2):
                    store_patches(0, adj, i, h * PST)
            all_stored(0)

            def load_matrix(n, matrix):
                with sp.Fori(0, NB) as b:
                    for j in range(NCH):
                        sp.wait_ge(adj_used, b * NCH + (NB * NCH * n + j + 1))
                        sp.dma_start(adj_ring[:, j, :], matrix[bass.ds(b * P, P), j * CHB * P:(j + 1) * CHB * P])\
                            .then_inc(adj_in[j], 16)

            for n in range(ND):
                load_matrix(n, adj)

            for g, n in enumerate(GATHERS):
                if g == 2:
                    all_stored(1)
                    sp.wait_ge(acc_done, GATHERS[1] + 1)
                    for k in range(ND, len(DENSE)):
                        load_matrix(k, adj_n)
                sp.wait_ge(table_made, g + 1)
                staged = wide if PASSES[n].get("typed") else t64[:, :, :]
                sp.dma_start(tables[n].rearrange("(p b) d -> p (b d)", p=P), staged.rearrange("p b d -> p (b d)"))\
                    .then_inc(table_stored, 16)
                if PASSES[n].get("typed"):
                    if g == 0:
                        sp.wait_ge(cleared_n, 16 * 4 * DSTEPS)
                    with sp.Fori(0, CSETS[g] // 2) as i:
                        for h in range(2):
                            store_patches(1, adj_n, i, (g * CSETS[0] + h) * PST)
                if PASSES[n].get("attr"):
                    with sp.Fori(0, ITERS) as i:
                        for s in range(RING):
                            sp.wait_ge(summed, i * RING + (GPP * g + s + 1))
                            sp.dma_start(attr_ring[:, s, :, :],
                                         edge_table[:, bass.ds(i * (RING * GRP) + s * GRP, GRP), META:REC])\
                                .then_inc(att_loaded[s], 16)
            sp.wait_ge(table_made, len(GATHERS) + 1)
            sp.dma_start(out[0:FULLB * P, :].rearrange("(b p) f -> p b f", p=P), x[:, 0:FULLB, :]).then_inc(out_stored, 16)
            sp.dma_start(out[FULLB * P:NODES, :], x[0:LASTN, FULLB, :]).then_inc(out_stored, 16)
            sp.wait_ge(out_stored, 32)

        @block.gpsimd
        def _(pool):
            nc.gpsimd.iota(iota_i[:, :], pattern=[[1, P]], base=0, channel_multiplier=0).then_inc(iota_made, 1)
            nc.gpsimd.iota(part_i[:, :], pattern=[[0, 1]], base=0, channel_multiplier=1).then_inc(iota_made, 1)
            nc.gpsimd.iota(tile0_i[:, :], pattern=[[P, TILES]], base=0, channel_multiplier=0).then_inc(iota_made, 1)

            def put(table, h, j):
                nc.gpsimd.indirect_dma_start(
                    out=table, out_offset=bass.IndirectOffsetOnAxis(ap=slot_ring[:, h, j:j + 1], axis=0),
                    in_=rec_ring[:, h, j, :], in_offset=None).then_inc(scattered[h], 16)

            pool.wait_ge(filled_s, 16 * len(fill_parts(TILES)))
            with pool.Fori(0, SSTEPS) as i:
                for h in range(2):
                    pool.wait_ge(slots_ready, i * 2 + h + 1)
                    pool.wait_ge(attr_in[h], i * 16 + 16)
                    pool.sem_inc(pool_steps, 1)
                    for j in range(SCOL):
                        put(records_s, h, j)
            pool.wait_ge(slots_ready, 2 * SSTEPS + 1)
            pool.wait_ge(attr_in[0], 16 * (SSTEPS + 1))
            put(records_s, 0, 0)
            pool.wait_ge(ranked, 2)
            pool.wait_ge(filled_d, 16 * len(fill_parts(TILES_D)))
            a0 = [16 * (SSTEPS + 1), 16 * SSTEPS]
            with pool.Fori(0, DSTEPS) as i:
                for h in range(2):
                    pool.wait_ge(slots_ready, i * 2 + (2 * SSTEPS + 1 + h + 1))
                    pool.wait_ge(attr_in[h], i * 16 + (a0[h] + 16))
                    pool.sem_inc(pool_steps, 1)
                    for j in range(DCOL):
                        put(records_d, h, j)
            nc.gpsimd.iota(p_iota_i, pattern=[[1, PATCHES]], base=0, channel_multiplier=0).then_inc(iota_made, 1)
            pool.wait_ge(iota_made, 5)
            nc.gpsimd.iota(p_iota_i, pattern=[[0, PSTEPS // 2], [P, 2 * PST]], base=NB * P * ROWS, channel_multiplier=0)\
                .then_inc(iota_made, 1)

            pool.wait_ge(patches_ready, 1)
            with pool.Fori(0, PSTEPS // 2) as i:
                for h in range(2):
                    t = from_rings[0][:, h * PST:(h + 1) * PST, :]
                    pool.wait_ge(from_made, i * (2 * PST) + (h + 1) * PST)
                    nc.gpsimd.tensor_tensor(t, t, p_w[:, bass.ds(i * (2 * PST) + h * PST, PST)].unsqueeze(2)
                                            .to_broadcast([P, PST, P]), ALU.mult).then_inc(from_ready, 1)

            for g, n in enumerate(GATHERS):
                pool.wait_ge(table_stored, 16 * (g + 1))
                g0 = GPP * g
                with pool.Fori(0, ITERS) as i:
                    for s in range(RING):
                        pool.wait_ge(idx_ready, i * RING + (g0 + s + 1))
                        pool.sem_inc(pool_steps, 1)
                        for j in range(GRP):
                            nc.gpsimd.indirect_dma_start(
                                out=msg_ring[:, s, j * F:(j + 1) * F], out_offset=None, in_=tables[n],
                                in_offset=bass.IndirectOffsetOnAxis(ap=idx_ring[:, s, j:j + 1], axis=0),
                            ).then_inc(gathered[s], 16)

        @block.tensor
        def _(pe):
            for k in range(2):
                pe.wait_ge(totals_made, k + 1)
                nc.tensor.matmul(ps[:, 0:NB + 1], below[:, :], tot[:, :], start=True, stop=True)
                nc.tensor.matmul(ps[:, BANK:BANK + NB + 1], ones[:, :], tot[:, :], start=True, stop=True)\
                    .then_inc(totals_summed, 1)
            pe.wait_ge(consts_made, 1)
            pe.wait_ge(blocks_made, 1)
            for m, t in enumerate((blk_f, bsrc_real, blk2_f, src_s, loc_dst[:, :], w_s)):
                for k in range(TK):
                    last = nc.tensor.transpose(ps[0:TQ, m * BANK + k * P:m * BANK + (k + 1) * P],
                                               t[:, k * TQ:(k + 1) * TQ], ident[:, :])
            last.then_inc(tiles_turned, 1)
            pe.wait_ge(patches_counted, 1)
            nc.tensor.matmul(ps[0:TQ, 0:TK], below[0:TQ, 0:TQ], n_pat[:, :], start=True, stop=True)
            nc.tensor.matmul(ps[0:TQ, BANK:BANK + TK], ones[0:TQ, 0:TQ], n_pat[:, :], start=True, stop=True)\
                .then_inc(patches_summed, 1)
            pe.wait_ge(member_made, 1)

            def choose(lhs):
                for m, t in enumerate(lhs):
                    for h in range(2):
                        for k in range(TK):
                            last = nc.tensor.matmul(ps[:, (2 * m + h) * BANK:(2 * m + h) * BANK + PH],
                                                    ones[0:TQ, :] if t is None else t[:, k, :],
                                                    member[:, k, h * PH:(h + 1) * PH], start=k == 0, stop=k + 1 == TK)
                last.then_inc(chosen, 1)

            choose([src_t, shift_t, loc_t, w_t])
            pe.wait_ge(chosen_read, 1)
            choose([tile_t, None])
            pe.wait_ge(patches_ready, 1)

            def patches(k, i, w, c0, first=False):
                pe.wait_ge(to_ready, i * (w // PST) + (k * PSTEPS + c0 // PST + 1))
                pe.wait_ge(from_ready, i * (w // PST) + (k * PSTEPS + c0 // PST + 1))
                for j in range(PST):
                    if j % 2 == 0 and not (first and j < 2 * PBANKS[k]):
                        pe.wait_ge(patch_summed, i * w + (k * PATCHES + c0 + j + 2 - 2 * PBANKS[k]))
                    at = (PBANK0[k] + (c0 + j) // 2 % PBANKS[k]) * BANK + j % 2 * P
                    slot = (c0 + j) % PSLOTS
                    nc.tensor.matmul(ps[:, at:at + P], to_rings[k][:, slot, :], from_rings[k][:, slot, :],
                                     start=True, stop=True, skip_group_check=True).then_inc(patch_made, 1)

            patches(0, 0, 2 * PST, 0, first=True)
            patches(0, 0, 2 * PST, PST)
            with pe.Fori(1, PSTEPS // 2) as i:
                for h in range(2):
                    patches(0, i, 2 * PST, h * PST)
            pe.wait_ge(patch_summed, PATCHES)

            pe.wait_ge(weights_in, 16 * N_WEIGHTS)

            def zero_acc(n):
                q = PASSES[n]
                banks = -(-NB * (HID if q.get("dense") else F) // BANK)
                for k in range(banks):
                    last = nc.tensor.matmul(ps[:, k * BANK:(k + 1) * BANK], zeros[:, 0:P], zeros[:, :],
                                            start=True, stop=False, skip_group_check=True)
                last.then_inc(acc_zeroed, 1)
                if n == 0:
                    for free, m in ((summed, RING), (adj_used, NCH), (ct_used, 2), (ct_ready, 2)):
                        nc.tensor.matmul(ps[:, 0:1], zeros[:, 0:P], zeros[:, 0:1],
                                         start=False, stop=False, skip_group_check=True).then_inc(free, m)

            def close_pass():
                nc.tensor.matmul(ps[:, 0:1], zeros[:, 0:P], zeros[:, 0:1],
                                 start=False, stop=False, skip_group_check=True).then_inc(acc_done, 1)

            def turned_pass(n, of):
                m = DENSE.index(n)
                r0 = NB * ((m - ND) // 2)
                pe.wait_ge(hop_in, m + 1)
                pe.wait_ge(acc_saved, n)

                def turn(i, k, u):
                    j, sub = u // 2, SUB[u % 2]
                    before = (r0 + k) * 2 * NCH + u
                    if u % 2 == 0:
                        pe.wait_ge(adj_in[j], i * (16 * TB) + 16 * (NB * m + k + 1))
                    pe.wait_ge(ct_ready, i * (TB * 2 * NCH) + (before + 1))
                    pe.sem_inc(pe_steps, 1)
                    for q, c in enumerate(sub):
                        last = nc.tensor.transpose(ps[:, (TB + u % 2) * BANK + q * P:(TB + u % 2) * BANK + (q + 1) * P],
                                                   adj_ring[:, j, c * P:(c + 1) * P], ident[:, :])
                    last.then_inc(ct_turned, 1)

                def multiply(i, k, u):
                    j, sub = u // 2, SUB[u % 2]
                    if u == 0:
                        pe.wait_ge(row_saved, i * TB + (r0 + k + 1))
                    pe.wait_ge(ct_ready, i * (TB * 2 * NCH) + ((r0 + k) * 2 * NCH + u + 3))
                    for q, c in enumerate(sub):
                        last = nc.tensor.matmul(ps[:, k * BANK:k * BANK + P], turned_ring[:, u % 2, q * P:(q + 1) * P],
                                                of[:, j * CHB + c, :], start=u == 0 and q == 0,
                                                stop=u + 1 == 2 * NCH and q + 1 == len(sub), skip_group_check=True)
                    last.then_inc(ct_used, 1)
                    if u % 2:
                        pe.sem_inc(adj_used, 1)

                with pe.Fori(0, NB // TB) as i:
                    turn(i, 0, 0)
                    for k in range(TB):
                        for u in range(2 * NCH):
                            nk, nu = (k, u + 1) if u + 1 < 2 * NCH else (k + 1, 0)
                            if nk < TB:
                                turn(i, nk, nu)
                            multiply(i, k, u)
                pe.sem_inc(acc_done, 1)

            def dense_pass(n, of):
                m = DENSE.index(n)
                pe.wait_ge(hop_in, m + 1)
                if n:
                    pe.wait_ge(acc_saved, n)
                zero_acc(n)
                with pe.Fori(0, NB) as b:
                    for j in range(NCH):
                        pe.wait_ge(adj_in[j], b * 16 + 16 * (NB * m + 1))
                        for k in range(CHB):
                            c = (j * CHB + k) * P
                            last = nc.tensor.matmul(ps[:, c:c + P], adj_ring[:, j, k * P:(k + 1) * P],
                                                    of[:, bass.ds(b, 1), :].rearrange("p a d -> p (a d)"),
                                                    start=False, stop=False, skip_group_check=True)
                        last.then_inc(adj_used, 1)
                close_pass()

            def sum_group(n, i, s):
                q = PASSES[n]
                d = F
                g = GPP * GATHERS.index(n)
                _, at = nc.values_load_multi_w_load_instructions(
                    blk64[0:1, bass.ds(i * (RING * GRP) + s * GRP, GRP)], engines=[mybir.EngineType.PE],
                    min_val=0, max_val=(NB - 1) * d, skip_runtime_bounds_check_because="blocks are 0..24")
                if q.get("attr"):
                    l0 = GPP * (n - (NPASS - 2))
                    pe.wait_ge(att_relu, i * RING + (l0 + s + 1))
                else:
                    pe.wait_ge(gathered[s], i * (16 * GRP) + 16 * GRP * (ITERS * GATHERS.index(n) + 1))
                pe.wait_ge(sel_ready, i * RING + (g + s + 1))
                for j in range(GRP):
                    rhs = (relu_ring if q.get("attr") else msg_ring)[:, s, j * d:(j + 1) * d]
                    last = nc.tensor.matmul(ps[:, bass.ds(at[j], d)], sel_ring[:, s, j, :], rhs,
                                            start=False, stop=False, skip_group_check=True)
                last.then_inc(summed, 1)

            def turn_attr(l, i, s, first=False):
                n = NPASS - 2 + l
                pe.wait_ge(att_loaded[s], i * 16 + 16 * (ITERS * l + 1))
                if not first:
                    pe.wait_ge(att_ready, i * RING + (GPP * l + s))
                pe.sem_inc(pe_steps, 1)
                for j in range(GRP):
                    last = nc.tensor.transpose(ps[0:F, ATT0 + j * P:ATT0 + (j + 1) * P], attr_ring[:, s, j, :], ident[:, :])
                last.then_inc(att_turned, 1)

            def project_attr(l, i, s, first=False):
                pe.wait_ge(att_ready, i * RING + (GPP * l + s + 1))
                if not first:
                    pe.wait_ge(att_added, i * RING + (GPP * l + s))
                m0 = MSG0 + BANK * (s % 2)
                for j in range(GRP):
                    last = nc.tensor.matmul(ps[:, m0 + j * F:m0 + (j + 1) * F], attrT[:, j * P:(j + 1) * P],
                                            w_msge[l][:, :], start=True, stop=True, skip_group_check=True)
                last.then_inc(att_projected, 1)

            def run_pass(n):
                q = PASSES[n]
                pe.wait_ge(acc_saved, n)
                zero_acc(n)
                if q.get("attr"):
                    l = n - (NPASS - 2)
                    turn_attr(l, 0, 0, first=(l == 0))
                    project_attr(l, 0, 0, first=(l == 0))

                    def steps(i, last=False):
                        for s in range(RING):
                            more = not (last and s == RING - 1)
                            ni, ns = (i, s + 1) if s + 1 < RING else (i + 1, 0)
                            if more:
                                turn_attr(l, ni, ns)
                            sum_group(n, i, s)
                            if more:
                                project_attr(l, ni, ns)

                    with pe.Fori(0, ITERS - 1) as i:
                        steps(i)
                    steps(ITERS - 1, last=True)
                else:
                    m = GATHERS.index(n)

                    def steps(i, last=False):
                        for s in range(RING):
                            if not (last and m == 1 and s >= RING - 2):
                                patches(1, i, RING * PST, (GPP * m + s) * PST)
                            sum_group(n, i, s)

                    with pe.Fori(0, ITERS - 1) as i:
                        steps(i)
                    steps(ITERS - 1, last=True)
                close_pass()

            def project(name, inputs, weights, bias=None):
                q = PROJ[name]
                d = q["d"]
                pitch = 256 if d == 3 * F else d
                for g in range(NG):
                    m = q["index"] * NG + g
                    for k, (of, kd) in enumerate(zip(inputs, q["k"])):
                        t = q["tr0"] + g * len(q["k"]) + k
                        if g == 0 and k == 0:
                            pe.wait_ge(proj_in, q["index"] + 1)
                        if t:
                            pe.wait_ge(turned_sb, t)
                        for b in range(GB):
                            last = nc.tensor.transpose(ps[0:kd, TR0 + b * P:TR0 + (b + 1) * P],
                                                       of[:, g * GB + b, 0:kd], ident[:, :])
                        last.then_inc(turned, 1)
                    pe.wait_ge(turned_sb, q["tr0"] + (g + 1) * len(q["k"]))
                    if m:
                        pe.wait_ge(product_out, m)
                    for b in range(GB):
                        c0 = b * pitch
                        for k, (wk, kd) in enumerate(zip(weights, q["k"])):
                            last = nc.tensor.matmul(ps[:, c0:c0 + d], xT[0:kd, k, b * P:(b + 1) * P], wk,
                                                    start=k == 0, stop=k + 1 == len(weights) and bias is None,
                                                    skip_group_check=True)
                        if bias is not None:
                            last = nc.tensor.matmul(ps[:, c0:c0 + d], ones[0:1, :], bias, start=False, stop=True,
                                                    skip_group_check=True)
                    last.then_inc(product, 1)

            def project_relational(l, of):
                q = PROJ[("rgcn1", "rgcn2")[l]]

                def turn(g):
                    t = q["tr0"] + g
                    pe.wait_ge(turned_sb, t)
                    for b in range(GB):
                        last = nc.tensor.transpose(ps[0:F, TR0 + b * P:TR0 + (b + 1) * P], of[:, g * GB + b, :],
                                                   ident[:, :])
                    last.then_inc(turned, 1)

                pe.wait_ge(proj_in, q["index"] + 1)
                turn(0)
                for g in range(NG):
                    pe.wait_ge(turned_sb, q["tr0"] + g + 1)
                    if g + 1 < NG:
                        turn(g + 1)
                    if g == 0:
                        pe.wait_ge(product_out, q["index"] * NG)
                    for b in range(GB):
                        if g:
                            pe.wait_ge(rel_out, (l * NG + g - 1) * GB + b + 1)
                        nc.tensor.matmul(ps[:, b * BANK:(b + 1) * BANK], xT[0:F, g % 2, b * P:(b + 1) * P],
                                         flat(w_rel[l]), start=True, stop=True,
                                         skip_group_check=True).then_inc(rel_made, 1)
                    if g:
                        pe.wait_ge(product_out, q["index"] * NG + g)
                    for b in range(GB):
                        last = nc.tensor.matmul(ps[:, SECOND0 + b * ROOTW:SECOND0 + (b + 1) * ROOTW],
                                                xT[0:F, g % 2, b * P:(b + 1) * P], w_root[l][:, :],
                                                start=True, stop=True, skip_group_check=True)
                    last.then_inc(product, 1)

            def flat(t):
                return t[:, :, :].rearrange("p k n -> p (k n)")

            dense_pass(0, xf)
            dense_pass(1, xf)
            project("tag1", [xf, agg], [w_tag1a[:, :], w_tag1b[:, :]], b_tag1[:, :])
            pe.wait_ge(product_out, NG * 1)
            dense_pass(2, h1)
            dense_pass(3, hop)
            project("tag2", [h1, hop, agg], [w_tag2[:, k, :] for k in range(3)], b_tag2[:, :])
            project("tag3", [xf], [flat(w_tag3)], b_tag3[:, :])
            pe.wait_ge(product_out, NG * 3)
            dense_pass(4, agg)
            dense_pass(5, agg)
            project_relational(0, x)
            pe.wait_ge(product_out, NG * 4)
            run_pass(6)
            project_relational(1, h64)
            pe.wait_ge(product_out, NG * 5)
            run_pass(7)
            project("hyper1", [x], [w_hyp[0][:, :]])
            pe.wait_ge(product_out, NG * 6)
            turned_pass(8, agg)
            dense_pass(9, agg)
            project("hyper2", [h64], [w_hyp[1][:, :]])
            pe.wait_ge(product_out, NG * 7)
            turned_pass(10, agg)
            dense_pass(11, agg)
            project("mpnn1", [x], [flat(w_node[0])])
            pe.wait_ge(product_out, NG * 8)
            run_pass(12)
            project("app1", [agg], [w_appa[0][:, :]])
            project("mpnn2", [h64], [flat(w_node[1])])
            pe.wait_ge(product_out, NG * 10)
            run_pass(13)
            project("app2", [agg], [w_appa[1][:, :]])

        @block.scalar
        def _(act):
            def make_records(i, h, waited, n=SCOL):
                c = bass.ds(i * (2 * SCOL) + h * SCOL, n)
                if waited is not None:
                    act.wait_ge(scattered[h], waited)
                for w, t in enumerate((src_i, dst_i, ew, typ_i)):
                    nc.scalar.copy(rec_ring[:, h, 0:n, w], t[:, c])
                nc.scalar.copy(slot_ring[:, h, 0:n], slot_i[0][:, c]).then_inc(slots_ready, 1)

            act.wait_ge(edges_in, 16 * N_EDGE_LOADS)
            act.wait_ge(ranked, 1)
            for h in range(2):
                make_records(0, h, None)
            with act.Fori(1, SSTEPS) as i:
                for h in range(2):
                    make_records(i, h, i * (16 * SCOL))
            make_records(SSTEPS, 0, 16 * SCOL * SSTEPS, n=1)

            act.wait_ge(patches_ready, 1)

            def select_to(k, i, w, c0, first=False):
                h = c0 // PST % 2
                if not first:
                    act.wait_ge(patch_made, i * w + (k * PATCHES + c0 - PST))
                for j in range(PST):
                    nc.scalar.activation(to_rings[k][:, h * PST + j, :], iota_f[:, :], ACT.Abs,
                                         bias=p_loc[:, bass.ds(i * w + (c0 + j), 1)]).then_inc(to_near, 1)
                act.wait_ge(to_near, i * w + (k * PATCHES + c0 + PST))
                t = to_rings[k][:, h * PST:(h + 1) * PST, :]
                nc.scalar.activation(t, t, ACT.Relu, bias=1.0, scale=-1.0).then_inc(to_ready, 1)

            for h in range(2):
                select_to(0, 0, 2 * PST, h * PST, first=True)
            with act.Fori(1, PSTEPS // 2) as i:
                for h in range(2):
                    select_to(0, i, 2 * PST, h * PST)

            def count_pass(m):
                with act.Fori(0, CSETS[m] // 2) as i:
                    for h in range(2):
                        select_to(1, i, 2 * PST, (m * CSETS[0] + h) * PST)

            def turned_out(m):
                t0 = 2 * NCH * NB * m
                with act.Fori(0, NB) as b:
                    for u in range(2 * NCH):
                        act.wait_ge(ct_turned, b * (2 * NCH) + (t0 + u + 1))
                        act.wait_ge(ct_used, b * (2 * NCH) + (t0 + u + 1))
                        n = len(SUB[u % 2]) * P
                        nc.scalar.copy(turned_ring[:, u % 2, 0:n], ps[:, (TB + u % 2) * BANK:(TB + u % 2) * BANK + n]).then_inc(ct_ready, 1)

            def turn_out(name):
                q = PROJ[name]
                for g in range(NG):
                    for k, kd in enumerate(q["k"]):
                        t = q["tr0"] + g * len(q["k"]) + k
                        m = q["index"] * NG + g
                        act.wait_ge(turned, t + 1)
                        to = k
                        if q["d2"]:
                            to = g % 2
                            act.wait_ge(product, m - min(g, 1))
                        elif m:
                            act.wait_ge(product, m)
                        nc.scalar.copy(xT[0:kd, to, :], ps[0:kd, TR0:TR0 + GB * P]).then_inc(turned_sb, 1)

            def make_std(n):
                act.wait_ge(var_made, n)
                nc.scalar.activation(std[:, :], var[:, :], ACT.Sqrt).then_inc(std_made, 1)

            def attr_out(l, i, s, first=False):
                act.wait_ge(att_turned, i * RING + (GPP * l + s + 1))
                if not first:
                    act.wait_ge(att_projected, i * RING + (GPP * l + s))
                nc.scalar.copy(attrT, ps[0:F, ATT0:ATT0 + GRP * P]).then_inc(att_ready, 1)

            def attr_pass(l):
                attr_out(l, 0, 0, first=(l == 0))

                def steps(i, last=False):
                    for s in range(RING):
                        act.wait_ge(att_added, i * RING + (GPP * l + s + 2))
                        nc.scalar.activation(relu_ring[:, s, :], relu_ring[:, s, :], ACT.Relu).then_inc(att_relu, 1)
                        if not (last and s == RING - 1):
                            ni, ns = (i, s + 1) if s + 1 < RING else (i + 1, 0)
                            attr_out(l, ni, ns)

                with act.Fori(0, ITERS - 1) as i:
                    steps(i)
                steps(ITERS - 1, last=True)

            turn_out("tag1")
            turn_out("tag2")
            turn_out("tag3")
            make_std(1)
            turn_out("rgcn1")
            act.wait_ge(ring_cleared, 1)
            count_pass(0)
            turn_out("rgcn2")
            count_pass(1)
            make_std(2)
            turn_out("hyper1")
            turned_out(0)
            turn_out("hyper2")
            turned_out(1)
            make_std(3)
            turn_out("mpnn1")
            attr_pass(0)
            turn_out("app1")
            turn_out("mpnn2")
            attr_pass(1)
            turn_out("app2")
            make_std(4)

        @block.vector
        def _(dve):
            done = [0]

            def step(ins):
                ins.then_inc(dve_step, 1)
                done[0] += 1
                dve.wait_ge(dve_step, done[0])

            v = nc.vector
            v.memset(src_i[:, COLS:EC], SENT).then_inc(fill_made, 1)
            v.memset(dst_i[:, COLS:EC], SENT).then_inc(fill_made, 1)
            v.memset(typ_i[:, COLS:EC], 0).then_inc(fill_made, 1)
            v.memset(ew[:, COLS:EC], 0.0).then_inc(fill_made, 1)
            v.memset(x[:, FULLB, :], 0.0).then_inc(fill_made, 1)
            v.memset(t64[:, :, :], 0.0)
            v.memset(rec_ring[:, :, :, :], 0.0)
            step(v.memset(filler, 0.0))
            v.memset(filler[:, :, 0:2], float(SENT)).then_inc(fill_made, 1)
            v.memset(b_tag3[:, F:3 * F], 0.0)
            for k in range(2):
                v.memset(w_hyp[k][:, F:HID], 0.0)
                v.memset(w_root[k][:, F:ROOTW], 0.0)
                v.memset(w_appa[k][:, F:HID], 0.0)
            v.memset(ones[:, :], 1.0)
            v.memset(zeros[:, :], 0.0)
            dve.wait_ge(iota_made, 3)
            step(v.tensor_copy(iota_f[:, :], iota_i[:, :]))
            step(v.tensor_copy(part_f[:, :], part_i[:, :]))
            v.tensor_copy(tile0_f[:, :], tile0_i[:, :])
            v.tensor_scalar(ident[:, :], iota_f[:, :], part_f[:, 0:1], None, ALU.is_equal)
            v.tensor_scalar(below[:, :], iota_f[:, :], part_f[:, 0:1], None, ALU.is_gt).then_inc(consts_made, 1)

            dve.wait_ge(edges_in, 16 * N_EDGE_LOADS)

            def rank(k, n):
                eq = eq_all[:, 0:(NB + 1) * n].rearrange("p (b c) -> p b c", c=n)
                cum = cum_all[:, 0:(NB + 1) * n].rearrange("p (b c) -> p b c", c=n)
                with dve.Fori(0, NB + 1) as b:
                    v.tensor_scalar(eq[:, bass.ds(b, 1), :].rearrange("p a c -> p (a c)"), blk_f[:, 0:n],
                                    iota_f[:, bass.ds(b, 1)], None, ALU.is_equal).then_inc(dve_step, 1)
                    dve.wait_ge(dve_step, b + (done[0] + 1))
                    row = eq[:, bass.ds(b, 1), :].rearrange("p a c -> p (a c)")
                    v.tensor_tensor_scan(cum[:, bass.ds(b, 1), :].rearrange("p a c -> p (a c)"), row, row, 0.0,
                                         ALU.add, ALU.bypass)
                done[0] += NB + 1
                dve.drain()
                v.tensor_copy(tot[:, :], cum[:, :, n - 1]).then_inc(totals_made, 1)
                dve.wait_ge(totals_summed, k + 1)
                step(v.tensor_scalar(padded_i[:, :], ps[:, BANK:BANK + NB + 1], float(P - 1), None, ALU.add))
                step(v.tensor_scalar(padded_i[:, :], padded_i[:, :], 7, 7, ALU.logical_shift_right,
                                     ALU.logical_shift_left))
                step(v.tensor_copy(padded_f[:, :], padded_i[:, :]))
                step(v.tensor_tensor_scan(start[:, :], padded_f[:, :], padded_f[:, :], 0.0, ALU.add, ALU.bypass))
                step(v.tensor_tensor(start[:, :], start[:, :], padded_f[:, :], ALU.subtract))
                step(v.scalar_tensor_tensor(base[:, :], ps[:, 0:NB + 1], -1.0, start[:, :], ALU.add, ALU.add))
                with dve.Fori(0, NB + 1) as b:
                    c = cum[:, bass.ds(b, 1), :].rearrange("p a c -> p (a c)")
                    v.scalar_tensor_tensor(c, c, base[:, bass.ds(b, 1)],
                                           eq[:, bass.ds(b, 1), :].rearrange("p a c -> p (a c)"),
                                           ALU.add, ALU.mult)
                dve.drain()
                step(v.tensor_reduce(blk_f[:, 0:n], cum.rearrange("p b c -> p c b"), AX.X, ALU.add))
                step(v.tensor_copy(slot_i[k][:, :], blk_f[:, 0:n]))

            def tile_blocks():
                step(v.memset(tblk[:, :], 0.0))
                for b in range(1, NB):
                    step(v.scalar_tensor_tensor(tblk[:, :], tile0_f[:, :], start[0:1, b:b + 1], tblk[:, :],
                                                ALU.is_ge, ALU.add))
                step(v.tensor_scalar(blk64[:, :], tblk[:, :], float(F), None, ALU.mult))

            def split_ids(ids, n=TILES):
                step(v.tensor_copy(low_i[:, 0:n], ids))
                step(v.tensor_scalar(blk_i[:, 0:n], low_i[:, 0:n], 7, None, ALU.logical_shift_right))
                step(v.tensor_scalar(low_i[:, 0:n], low_i[:, 0:n], P - 1, None, ALU.bitwise_and))

            def rows_of(to):
                v.scalar_tensor_tensor(to, low_i[:, :], float(NB), blk_i[:, :], ALU.mult, ALU.add)

            def place_of(to, ids):
                step(v.tensor_scalar(to, blk_i[:, :], float(NB - 1), float(-P), ALU.min, ALU.mult))
                step(v.tensor_tensor(to, ids, to, ALU.add))

            split_ids(src_i[:, :], EC)
            step(v.tensor_copy(blk_f[:, 0:EC], blk_i[:, 0:EC]))
            rank(0, EC)
            v.engine_nop().then_inc(ranked, 1)

            for c in range(MCH):
                dve.wait_ge(chunk_in[c % 2], 16 * (c // 2 + 1))
                v.tensor_copy(key_f[:, c * MT:(c + 1) * MT], chunk[c % 2][:, :, 1]).then_inc(chunk_used, 1)
            dve.wait_ge(chunk_used, MCH)
            split_ids(key_f)
            step(v.tensor_copy(blk_f, blk_i))
            rank(1, TILES)
            v.tensor_scalar(low_i, slot_i[1][:, :], P - 1, None, ALU.bitwise_and)
            step(v.tensor_scalar(blk_i, slot_i[1][:, :], 7, None, ALU.logical_shift_right))
            step(v.scalar_tensor_tensor(slot_i[1][:, :], low_i, float(TILES_D), blk_i, ALU.mult, ALU.add))
            v.engine_nop().then_inc(ranked, 1)
            with dve.Fori(0, DSTEPS) as i:
                for h in range(2):
                    dve.wait_ge(scattered[h], i * (16 * DCOL) + S_USED[h])
                    v.tensor_copy(slot_ring[:, h, :], slot_i[1][:, bass.ds(i * (2 * DCOL) + h * DCOL, DCOL)])\
                        .then_inc(slots_ready, 1)
            tile_blocks()

            for c in range(MCH):
                dve.wait_ge(chunk_in[c % 2], 16 * ((MCH + c) // 2 + 1))
                for w, t in enumerate((src_s, dst_s, w_s, typ_s)):
                    last = v.tensor_copy(t[:, c * MT:(c + 1) * MT], chunk[c % 2][:, :, w])
                last.then_inc(chunk_used, 1)
            dve.wait_ge(chunk_used, 2 * MCH)
            split_ids(dst_s)
            v.tensor_copy(blk2_f, blk_i)
            place_of(loc_dst[:, :], dst_s)
            split_ids(src_s)
            v.tensor_copy(blk_f, blk_i)
            rows_of(row_src[:, :])
            step(v.engine_nop())
            step(v.scalar_tensor_tensor(bsrc_real, blk_f, float(NB), blk_f, ALU.is_lt, ALU.mult))
            step(v.scalar_tensor_tensor(row_typed[:, :], row_src[:, :], float(TYPES), typ_s, ALU.mult, ALU.add))
            v.engine_nop().then_inc(blocks_made, 1)

            def banks(m):
                return ps[0:TQ, m * BANK:(m + 1) * BANK].rearrange("p (k c) -> p k c", k=TK)

            dve.wait_ge(tiles_turned, 1)
            v.tensor_reduce(first_b[:, :], banks(0), AX.X, ALU.min)
            v.tensor_reduce(last_b[:, :], banks(1), AX.X, ALU.max)
            v.tensor_reduce(tile_b[:, :], banks(2), AX.X, ALU.min)
            v.tensor_copy(src_t, banks(3))
            v.tensor_copy(loc_t, banks(4))
            step(v.tensor_copy(w_t, banks(5)))
            step(v.scalar_tensor_tensor(n_pat[:, :], last_b[:, :], 1.0, first_b[:, :], ALU.add, ALU.subtract))
            step(v.tensor_scalar(n_pat[:, :], n_pat[:, :], 0.0, None, ALU.max))
            v.engine_nop().then_inc(patches_counted, 1)
            dve.wait_ge(patches_summed, 1)
            step(v.tensor_copy(tot_pat[:, :], ps[0:TQ, BANK:BANK + TK]))
            step(v.tensor_tensor_scan(cum_pat[:, :], tot_pat[:, :], tot_pat[:, :], 0.0, ALU.add, ALU.bypass))
            step(v.tensor_tensor(cum_pat[:, :], cum_pat[:, :], tot_pat[:, :], ALU.subtract))
            step(v.tensor_tensor(pat0[:, :], ps[0:TQ, 0:TK], cum_pat[:, :], ALU.add))
            step(v.tensor_tensor(pat1[:, :], pat0[:, :], n_pat[:, :], ALU.add))
            step(v.tensor_tensor(shift[:, :], first_b[:, :], pat0[:, :], ALU.subtract))
            v.tensor_copy(shift_t, shift[:, :].unsqueeze(2).to_broadcast([TQ, TK, P]))
            v.tensor_copy(tile_t, tile_b[:, :].unsqueeze(2).to_broadcast([TQ, TK, P]))
            dve.wait_ge(iota_made, 4)
            step(v.tensor_copy(p_iota, p_iota_i))
            v.engine_nop().then_inc(iota_made, 1)
            for k in range(TK):
                step(v.tensor_scalar(member[:, k, :], p_iota[0:TQ, :], pat1[:, k:k + 1], None, ALU.is_lt))
                step(v.scalar_tensor_tensor(member[:, k, :], p_iota[0:TQ, :], pat0[:, k:k + 1], member[:, k, :],
                                            ALU.is_ge, ALU.mult))
            v.engine_nop().then_inc(member_made, 1)
            dve.wait_ge(iota_made, 6)
            step(v.tensor_copy(p_trash, p_iota_i))

            def two(t):
                return t.rearrange("p (h c) -> p h c", h=2)

            def chosen_at(m):
                return ps[:, 2 * m * BANK:2 * (m + 1) * BANK].rearrange("p (h c) -> p h c", h=2)[:, :, 0:PH]

            dve.wait_ge(chosen, 1)
            step(v.tensor_tensor(two(p_blk), chosen_at(1), two(p_iota), ALU.add))
            step(v.scalar_tensor_tensor(two(p_src), two(p_blk), float(-P), chosen_at(0), ALU.mult, ALU.add))
            v.tensor_scalar(two(p_loc), chosen_at(2), -1.0, None, ALU.mult)
            step(v.tensor_copy(two(p_w), chosen_at(3)))
            v.engine_nop().then_inc(chosen_read, 1)
            dve.wait_ge(chosen, 2)
            step(v.scalar_tensor_tensor(two(p_id), chosen_at(0), float(NB), two(p_blk), ALU.mult, ALU.add))
            step(v.scalar_tensor_tensor(two(p_id), two(p_id), float(-NB * NB), chosen_at(1), ALU.add, ALU.mult))
            step(v.memset(p_keep[:, 0:1], 0.0))
            step(v.tensor_tensor(p_keep[:, 1:PATCHES], p_id[:, 1:PATCHES], p_id[:, 0:PATCHES - 1], ALU.is_equal))
            r = slice(0, 1)
            step(v.scalar_tensor_tensor(two(p_tmp)[r], chosen_at(0)[r], float(P * ROWS), two(p_trash)[r],
                                        ALU.mult, ALU.subtract))
            step(v.scalar_tensor_tensor(p_tmp[r], p_blk[r], float(P), p_tmp[r], ALU.mult, ALU.add))
            step(v.tensor_scalar(p_blk[r, 0:PATCHES - 1], p_keep[r, 1:PATCHES], -1.0, 1.0, ALU.mult, ALU.add))
            step(v.memset(p_blk[r, PATCHES - 1:PATCHES], 1.0))
            step(v.scalar_tensor_tensor(p_blk[r], p_id[r], 0.0, p_blk[r], ALU.is_lt, ALU.mult))
            step(v.tensor_tensor(p_tmp[r], p_tmp[r], p_blk[r], ALU.mult))
            step(v.tensor_tensor(place_i[:, :], p_tmp[r], p_trash[r], ALU.add))
            step(v.memset(patch_rings[0][-1], 0.0))
            v.engine_nop().then_inc(patches_ready, 1)

            def select_from(k, i, w, c0, n=PST):
                slot = c0 % PSLOTS
                places = p_src[:, bass.ds(i * w + c0, n)].unsqueeze(2).to_broadcast([P, n, P])
                v.tensor_tensor(from_rings[k][:, slot:slot + n, :], iota_f[:, :].unsqueeze(1).to_broadcast([P, n, P]),
                                places, ALU.is_equal).then_inc(from_made if k == 0 else from_ready, n // (1, PST)[k])

            def join_patches(k, i, w, c0, first=False, select=False):
                if not first:
                    dve.wait_ge(patch_stored[k][c0 // PST % 2],
                                i * (16 * w // 2) + (16 * PST * (c0 // PSLOTS) + CREDIT[k]))
                for j in range(PST):
                    n = k * PATCHES + c0 + j
                    slot = (c0 + j) % PSLOTS
                    if j % 2 == 0:
                        dve.wait_ge(patch_made, i * w + (n + 2))
                    if not (first and n == 0):
                        dve.wait_ge(patch_summed, i * w + n)
                    at = (PBANK0[k] + (c0 + j) // 2 % PBANKS[k]) * BANK + j % 2 * P
                    v.scalar_tensor_tensor(patch_rings[k][slot], patch_rings[k][slot - 1],
                                           p_keep[:, bass.ds(i * w + (c0 + j), 1)], ps[:, at:at + P],
                                           ALU.mult, ALU.add).then_inc(patch_summed, 1)
                    if select and j % 2 == 0:
                        select_from(k, i, w, c0 + PSLOTS + j, 2)

            for h in range(2):
                select_from(0, 0, 2 * PST, h * PST)
            for h in range(2):
                join_patches(0, 0, 2 * PST, h * PST, first=True, select=True)
            with dve.Fori(1, PSTEPS // 2 - 1) as i:
                for h in range(2):
                    join_patches(0, i, 2 * PST, h * PST, select=True)
            for h in range(2):
                join_patches(0, PSTEPS // 2 - 1, 2 * PST, h * PST)
            dve.wait_ge(patch_summed, PATCHES)

            dve.wait_ge(x_in, 32)
            step(v.memset(xf[:, :, F:HID], 0.0))
            step(v.tensor_copy(xf[:, :, 0:F], x[:, :, :]))
            v.engine_nop().then_inc(hop_in, 1)

            def prepare(n, i, s):
                q = PASSES[n]
                g = GPP * GATHERS.index(n) + s
                c0 = i * (RING * GRP) + s * GRP
                dve.wait_ge(summed, i * RING + (g + 1))
                v.tensor_copy(idx_ring[:, s, :], index_of(q)[:, bass.ds(c0, GRP)]).then_inc(idx_ready, 1)
                places = loc_dst[:, bass.ds(c0, GRP)].unsqueeze(2).to_broadcast([P, GRP, P])
                v.tensor_tensor(sel_ring[:, s, :, :], iota_f[:, :].unsqueeze(1).to_broadcast([P, GRP, P]), places,
                                ALU.is_equal).then_inc(sel_ready, 1)

            def run_pass(n):
                if PASSES[n].get("attr"):
                    l = n - (NPASS - 2)
                    prepare(n, 0, 0)
                    prepare(n, 0, 1)

                    def steps(i, last=False):
                        for s in range(RING):
                            if not (last and s >= RING - 2):
                                ni, ns = (i, s + 2) if s + 2 < RING else (i + 1, s + 2 - RING)
                                prepare(n, ni, ns)
                            dve.wait_ge(gathered[s], i * (16 * GRP) + 16 * GRP * (ITERS * GATHERS.index(n) + 1))
                            dve.wait_ge(att_projected, i * RING + (GPP * l + s + 1))
                            m0 = MSG0 + BANK * (s % 2)
                            v.tensor_tensor(relu_ring[:, s, :], ps[:, m0:m0 + GRP * F], msg_ring[:, s, 0:GRP * F],
                                            ALU.add).then_inc(att_added, 1)

                    with dve.Fori(0, ITERS - 1) as i:
                        steps(i)
                    steps(ITERS - 1, last=True)
                else:
                    m = GATHERS.index(n)
                    if m == 0:
                        dve.wait_ge(cleared_n, 16 * 4 * DSTEPS)
                        step(v.memset(patch_rings[1][-1], 0.0))
                        for stored in patch_stored[1]:
                            v.engine_nop().then_inc(stored, CREDIT[1])
                        for h in range(2):
                            select_from(1, 0, 2 * PST, h * PST)
                    prepare(n, 0, 0)
                    prepare(n, 0, 1)

                    def steps(i, last=False):
                        for s in range(RING):
                            if not (last and s >= RING - 2):
                                ni, ns = (i, s + 2) if s + 2 < RING else (i + 1, s + 2 - RING)
                                prepare(n, ni, ns)
                            if last and m == 1 and s >= RING - 2:
                                continue
                            c0 = (GPP * m + s) * PST
                            join_patches(1, i, RING * PST, c0)
                            if not (last and m == 1):
                                select_from(1, i, RING * PST, c0 + 2 * PST)

                    with dve.Fori(0, ITERS - 1) as i:
                        steps(i)
                    steps(ITERS - 1, last=True)
                dve.wait_ge(acc_done, n + 1)

            def sums(n):
                return ps[:, 0:NB * F].rearrange("p (b d) -> p b d", d=F)

            def dense_sums(c=0, d=F):
                return ps[:, 0:NB * HID].rearrange("p (b d) -> p b d", d=HID)[:, :, c:c + d]

            def drain_products(name, post):
                q = PROJ[name]
                d = q["d"]
                pitch = 256 if d == 3 * F else d
                for g in range(NG):
                    dve.wait_ge(product, q["index"] * NG + g + 1)
                    b = slice(g * GB, (g + 1) * GB)
                    first = ps[:, 0:GB * pitch].rearrange("p (b d) -> p b d", d=pitch)[:, :, 0:d]
                    post(b, first).then_inc(product_out, 1)

            def wide_of(t, n=F):
                return t.unsqueeze(2).to_broadcast([P, NB, n])

            def layernorm(z, n):
                step(v.tensor_reduce(mean[:, :], z, AX.X, ALU.add))
                step(v.tensor_scalar(mean[:, :], mean[:, :], 1.0 / F, None, ALU.mult))
                step(v.tensor_tensor(z, z, wide_of(mean[:, :]), ALU.subtract))
                step(v.tensor_tensor(x[:, :, :], z, z, ALU.mult))
                step(v.tensor_reduce(var[:, :], x[:, :, :], AX.X, ALU.add))
                v.tensor_scalar(var[:, :], var[:, :], 1.0 / F, LN_EPS, ALU.mult, ALU.add).then_inc(var_made, 1)
                dve.wait_ge(std_made, n)
                step(v.reciprocal(rstd[:, :], std[:, :]))
                step(v.tensor_tensor(x[:, :, :], z, wide_of(rstd[:, :]), ALU.mult))

            def signal(s):
                v.engine_nop().then_inc(s, 1)

            def leaky(to):
                def post(b, first):
                    step(v.tensor_copy(to[:, b, :], first))
                    return v.scalar_tensor_tensor(to[:, b, :], to[:, b, :], SLOPE, to[:, b, :], ALU.mult, ALU.max)
                return post

            def along(t):
                return t[:, :].unsqueeze(1).to_broadcast([P, GB, F])

            def drain_relational(l):
                q = PROJ[("rgcn1", "rgcn2")[l]]
                for g in range(NG):
                    for b in range(GB):
                        dve.wait_ge(rel_made, (l * NG + g) * GB + b + 1)
                        v.tensor_copy(wide[:, g * GB + b, :], ps[:, b * BANK:(b + 1) * BANK]).then_inc(rel_out, 1)
                    dve.wait_ge(product, q["index"] * NG + g + 1)
                    root = ps[:, SECOND0:SECOND0 + GB * ROOTW].rearrange("p (b d) -> p b d", d=ROOTW)[:, :, 0:F]
                    v.tensor_tensor(r64[:, g * GB:(g + 1) * GB, :], root, along(b_root[l]), ALU.add)\
                        .then_inc(product_out, 1)
                dve.wait_ge(rel_out, (l + 1) * NB)

            def hyper(b, first):
                return v.tensor_copy(agg[:, b, 0:F], first[:, :, 0:F])

            def message(k):
                def post(b, first):
                    v.tensor_tensor(t64[:, b, :], first[:, :, 0:F], along(b_msg[k]), ALU.add)
                    return v.tensor_tensor(r64[:, b, :], first[:, :, F:HID], along(b_app[k]), ALU.add)
                return post

            def inverse_degree(k, counts):
                step(v.tensor_copy(cnt[:, :], counts))
                v.tensor_scalar(has[:, :], cnt[:, :], 1.0, None, ALU.min)
                step(v.tensor_scalar(inv[k][:, :], cnt[:, :], 1.0, None, ALU.max))
                step(v.reciprocal(inv[k][:, :], inv[k][:, :]))
                step(v.tensor_tensor(inv[k][:, :], inv[k][:, :], has[:, :], ALU.mult))

            v.engine_nop().then_inc(att_added, 1)

            def saved(n):
                dve.wait_ge(acc_saved, n)

            dve.wait_ge(acc_done, 1)
            v.tensor_copy(xf[:, :, F:HID], dense_sums()).then_inc(acc_saved, 1)
            saved(1)
            signal(hop_in)
            dve.wait_ge(acc_done, 2)
            v.tensor_copy(agg[:, :, 0:F], dense_sums(F)).then_inc(acc_saved, 1)
            saved(2)
            signal(proj_in)
            drain_products("tag1", leaky(h1))
            dve.wait_ge(product_out, NG)
            signal(hop_in)
            dve.wait_ge(acc_done, 3)
            v.tensor_copy(hop, dense_sums(0, HID)).then_inc(acc_saved, 1)
            saved(3)
            signal(hop_in)
            dve.wait_ge(acc_done, 4)
            v.tensor_copy(agg[:, :, :], dense_sums(0, HID)).then_inc(acc_saved, 1)
            saved(4)
            signal(proj_in)
            drain_products("tag2", leaky(xf))
            dve.wait_ge(product_out, 2 * NG)
            signal(proj_in)

            def split(b, first):
                v.tensor_copy(part[:, b, :], first[:, :, 0:2 * F])
                return v.tensor_copy(agg[:, b, 0:F], first[:, :, 2 * F:3 * F])

            drain_products("tag3", split)
            dve.wait_ge(product_out, 3 * NG)
            signal(hop_in)
            dve.wait_ge(acc_done, 5)
            v.tensor_tensor(agg[:, :, 0:F], dense_sums(), part[:, :, F:2 * F], ALU.add).then_inc(acc_saved, 1)
            saved(5)
            signal(hop_in)
            dve.wait_ge(acc_done, 6)
            v.tensor_tensor(h64[:, :, :], dense_sums(), part[:, :, 0:F], ALU.add).then_inc(acc_saved, 1)
            dve.wait_ge(acc_saved, 6)
            step(v.tensor_tensor(h64[:, :, :], h64[:, :, :], x[:, :, :], ALU.add))
            layernorm(h64[:, :, :], 1)
            signal(proj_in)

            signal(ring_cleared)
            drain_relational(0)
            signal(table_made)
            run_pass(6)
            v.tensor_tensor(h64[:, :, :], sums(6), r64[:, :, :], ALU.add).then_inc(acc_saved, 1)
            dve.wait_ge(acc_saved, 7)
            step(v.tensor_scalar(h64[:, :, :], h64[:, :, :], 0.0, None, ALU.max))
            signal(proj_in)
            drain_relational(1)
            signal(table_made)
            run_pass(7)
            v.tensor_tensor(h64[:, :, :], sums(7), r64[:, :, :], ALU.add).then_inc(acc_saved, 1)
            dve.wait_ge(acc_saved, 8)
            step(v.tensor_tensor(h64[:, :, :], h64[:, :, :], x[:, :, :], ALU.add))
            layernorm(h64[:, :, :], 2)
            signal(proj_in)

            for stored in patch_stored[1]:
                dve.wait_ge(stored, 16 * (PATCHES // 2) + CREDIT[1])
            v.memset(agg[:, :, F:F + 1], 1.0)
            v.memset(agg[:, :, F + 1:HID], 0.0)
            drain_products("hyper1", hyper)
            dve.wait_ge(product_out, 6 * NG)
            signal(hop_in)
            for k in range(2):
                n = 8 + 2 * k
                if k == 0:
                    v.engine_nop().then_inc(row_saved, TB)
                with dve.Fori(0, NB // TB) as i:
                    for b in range(TB):
                        dve.wait_ge(ct_used, i * (2 * NCH * TB) + (2 * NCH * (NB * k + b + 1) + 2))
                        v.tensor_copy(xf[:, bass.ds(i * TB + b, 1), :].rearrange("p a d -> p (a d)"),
                                      ps[:, b * BANK:b * BANK + P]).then_inc(row_saved, 1)
                dve.wait_ge(row_saved, TB + NB * (k + 1))
                if k == 0:
                    inverse_degree(0, xf[:, :, F])
                dve.wait_ge(acc_done, n + 1)
                v.tensor_tensor(agg[:, :, 0:F], xf[:, :, 0:F], wide_of(inv[0][:, :]), ALU.mult).then_inc(acc_saved, 1)
                saved(n + 1)
                signal(hop_in)
                dve.wait_ge(acc_done, n + 2)
                if k == 0:
                    inverse_degree(1, dense_sums(F, 1).rearrange("p b d -> p (b d)"))
                v.tensor_tensor(h64[:, :, :], dense_sums(), wide_of(inv[1][:, :]), ALU.mult).then_inc(acc_saved, 1)
                saved(n + 2)
                bias = b_hyp[k][:, :].unsqueeze(1).to_broadcast([P, NB, F])
                step(v.tensor_tensor(h64[:, :, :], h64[:, :, :], bias, ALU.add))
                if k == 0:
                    step(v.tensor_scalar(h64[:, :, :], h64[:, :, :], 0.0, None, ALU.max))
                    signal(proj_in)
                    drain_products("hyper2", hyper)
                    dve.wait_ge(product_out, 7 * NG)
                    signal(hop_in)
            step(v.tensor_tensor(h64[:, :, :], h64[:, :, :], x[:, :, :], ALU.add))
            layernorm(h64[:, :, :], 3)
            signal(proj_in)

            drain_products("mpnn1", message(0))
            signal(table_made)

            def applied(kept, to):
                def post(b, first):
                    step(v.tensor_tensor(r64[:, b, :], first[:, :, 0:F], r64[:, b, :], ALU.add))
                    return v.scalar_tensor_tensor(to[:, b, :], r64[:, b, :], 0.0, kept[:, b, :], ALU.max, ALU.add)
                return post

            run_pass(12)
            v.tensor_copy(agg[:, :, 0:F], sums(12)).then_inc(acc_saved, 1)
            signal(proj_in)
            drain_products("app1", applied(x, h64))
            signal(proj_in)
            drain_products("mpnn2", message(1))
            signal(table_made)
            run_pass(13)
            v.tensor_copy(agg[:, :, 0:F], sums(13)).then_inc(acc_saved, 1)
            signal(proj_in)
            drain_products("app2", applied(h64, h64))
            dve.wait_ge(product_out, NG * len(PROJ))
            step(v.tensor_tensor(h64[:, :, :], h64[:, :, :], x[:, :, :], ALU.add))
            layernorm(h64[:, :, :], 4)
            signal(table_made)


def kernel(**inputs):
    import numpy as np
    import concourse.bacc as bacc
    from concourse.bass_utils import run_bass_kernel_spmd

    def arr(name):
        return np.ascontiguousarray(inputs[name])

    arrays = {"x": arr("x"), "edge_attr": arr("edge_attr_64")}
    n = COLS * P
    for short, name in (("src", "src"), ("dst", "dst"), ("typ", "edge_type_8"), ("w", "edge_weight")):
        v = arr(name)
        arrays[short + "_cols"] = np.ascontiguousarray(v[:n].reshape(COLS, P).T)
        arrays[short + "_tail"] = np.ascontiguousarray(v[n:].reshape(TAIL, 1))
    for k in (1, 2, 3):
        arrays[f"L0_W{k}T"] = np.ascontiguousarray(arr(f"L0_gnn_W{k}").T)
        arrays[f"L0_b{k}"] = arr(f"L0_gnn_b{k}").reshape(1, -1)
    for k in ("1", "2"):
        arrays["L1_W" + k] = arr("L1_gnn_W" + k)
        arrays["L1_root" + k] = arr("L1_gnn_root" + k)
        arrays["L1_b" + k] = arr("L1_gnn_b" + k).reshape(1, -1)
        arrays["L2_W" + k] = arr("L2_gnn_W" + k)
        arrays["L2_b" + k] = arr("L2_gnn_b" + k).reshape(1, -1)
        for part in ("_msg", "_app"):
            arrays["L3_W" + k + part] = arr("L3_gnn_W" + k + part)
            arrays["L3_b" + k + part] = arr("L3_gnn_b" + k + part).reshape(1, -1)

    nc = bacc.Bacc("TRN2", target_bir_lowering=False, num_devices=1)
    feeds, aps = {}, {}
    for name, v in arrays.items():
        feeds["in_" + name] = v
        aps[name] = nc.dram_tensor("in_" + name, v.shape, mybir.dt.from_np(v.dtype), kind="ExternalInput").ap()
    out = nc.dram_tensor("out_0", (NODES, F), FP32, kind="ExternalOutput").ap()
    gnn_kernel(nc, aps, out)
    r = run_bass_kernel_spmd(nc, [feeds], core_ids=[0])
    return r.results[0]["out_0"]
```
